# Optimizing a Trainium2 kernel written in Bass

```python
import numpy as np
import jax
import jax.numpy as jnp

def _softmax(x, axis=-1):
    return jax.nn.softmax(x, axis=axis)

def _gelu(x):
    return jax.nn.gelu(x, approximate=True)

def _silu(x):
    return jax.nn.silu(x)

def _sigmoid(x):
    return jax.nn.sigmoid(x)

def _layernorm(x, axis=-1, eps=1e-05):
    m = jnp.mean(x, axis=axis, keepdims=True)
    v = jnp.var(x, axis=axis, keepdims=True)
    return (x - m) / jnp.sqrt(v + eps)

def _scatter_add(tgt, idx, src, axis=0):
    return tgt.at[idx].add(src)

def _segment_sum(src, seg, n):
    return jax.ops.segment_sum(src, seg, n)
kernel_name = 'mk_early_fusion_d2_tok_img1024_r4_7260df'

def setup_inputs(seed: int=0):
    np.random.seed(seed)
    _w = jnp.asarray

    def _rec_inputs():
        import jax
        import jax.numpy as jnp
        _rk = jax.random.key(seed)
        x = -0.00016672 + 0.999947 * jax.random.normal(jax.random.fold_in(_rk, 1), (4, 3, 96, 96), jnp.float32)
        txt = 0.434251 + 1.14597 * jax.random.normal(jax.random.fold_in(_rk, 2), (4, 512, 256), jnp.float32)
        return (x, txt)
    x, txt = _rec_inputs()

    def _L0_tok_setup():
        import jax, jax.numpy as jnp
        import numpy as np
        DIM = 256
        IMG = 96
        P = 16
        C = 3
        TEMP = 10000.0
        EPS = 1e-05
        PATCH_DIM = C * P * P
        HP = IMG // P

        def layernorm(x, gamma, beta):
            mu = jnp.mean(x, axis=-1, keepdims=True)
            var = jnp.var(x, axis=-1, keepdims=True)
            return (x - mu) * jax.lax.rsqrt(var + EPS) * gamma + beta

        def posemb_sincos_2d(h, w, dim, dtype):
            y, x = jnp.meshgrid(jnp.arange(h), jnp.arange(w), indexing='ij')
            omega = jnp.arange(dim // 4, dtype=jnp.float32) / (dim // 4 - 1)
            omega = 1.0 / TEMP ** omega
            y = y.reshape(-1)[:, None] * omega[None, :]
            x = x.reshape(-1)[:, None] * omega[None, :]
            pe = jnp.concatenate((jnp.sin(x), jnp.cos(x), jnp.sin(y), jnp.cos(y)), axis=1)
            return pe.astype(dtype)
        key = jax.random.key(seed)
        ks = jax.random.split(key, 8)
        B = 64
        img = jax.random.normal(ks[0], (B, C, IMG, IMG), dtype=jnp.float32)
        cls_token = jax.random.normal(ks[1], (1, 1, DIM), dtype=jnp.float32)
        cls_pos_embedding = jax.random.normal(ks[2], (1, 1, DIM), dtype=jnp.float32)
        ln1_g = jnp.ones((PATCH_DIM,), jnp.float32)
        ln1_b = jnp.zeros((PATCH_DIM,), jnp.float32)
        W = jax.random.normal(ks[3], (PATCH_DIM, DIM), dtype=jnp.float32) / np.sqrt(PATCH_DIM)
        bias = jnp.zeros((DIM,), jnp.float32)
        ln2_g = jnp.ones((DIM,), jnp.float32)
        ln2_b = jnp.zeros((DIM,), jnp.float32)
        return {'img': img, 'cls_token': cls_token, 'cls_pos_embedding': cls_pos_embedding, 'ln1_g': ln1_g, 'ln1_b': ln1_b, 'W': W, 'bias': bias, 'ln2_g': ln2_g, 'ln2_b': ln2_b}
    _L0_tok_all = _L0_tok_setup()
    _L0_tok_in = {k: v for k, v in _L0_tok_all.items() if k in ('cls_token', 'cls_pos_embedding', 'ln1_g', 'ln1_b', 'W', 'bias', 'ln2_g', 'ln2_b')}
    del _L0_tok_all

    def _L0_attn_setup():
        import jax, jax.numpy as jnp
        from jax import lax
        import numpy as np
        DIM = 256
        H = 8
        DK = 128
        DV = 64
        GATE_NORM = 16.0

        def _gla(x, Wq, Wk, Wv, Wo, Wg, bg, Wog):
            B, S, D = x.shape
            q = (x @ Wq).reshape(B, S, H, DK)
            k = (x @ Wk).reshape(B, S, H, DK) * DK ** (-0.5)
            v = (x @ Wv).reshape(B, S, H, DV)
            alpha = jax.nn.sigmoid((x @ Wg + bg) / GATE_NORM)

            def step(state, inp):
                qt, kt, vt, at = inp
                state = at[..., None, None] * state + kt[..., None] * vt[:, :, None, :]
                out_t = jnp.einsum('bhk,bhkv->bhv', qt, state)
                return (state, out_t)
            state0 = jnp.zeros((B, H, DK, DV), x.dtype)
            xs = (jnp.moveaxis(q, 1, 0), jnp.moveaxis(k, 1, 0), jnp.moveaxis(v, 1, 0), jnp.moveaxis(alpha, 1, 0))
            _, outs = lax.scan(step, state0, xs)
            out = jnp.moveaxis(outs, 0, 1).reshape(B, S, H * DV)
            og = jax.nn.sigmoid(x @ Wog)
            return out * og @ Wo
        key = jax.random.key(seed)
        ks = jax.random.split(key, 8)
        B, S = (2, 1024)

        def xavier(k, shape, gain=1.0):
            fan_in, fan_out = (shape[0], shape[1])
            lim = gain * np.sqrt(6.0 / (fan_in + fan_out))
            return jax.random.uniform(k, shape, jnp.float32, -lim, lim)
        g = 2 ** (-2.5)
        return {'x': jax.random.normal(ks[0], (B, S, DIM), jnp.float32), 'Wq': xavier(ks[1], (DIM, H * DK), g), 'Wk': xavier(ks[2], (DIM, H * DK), g), 'Wv': xavier(ks[3], (DIM, H * DV), g), 'Wo': xavier(ks[4], (H * DV, DIM)), 'Wg': xavier(ks[5], (DIM, H)), 'bg': jnp.zeros((H,), jnp.float32), 'Wog': xavier(ks[6], (DIM, H * DV))}
    _L0_attn_all = _L0_attn_setup()
    _L0_attn_in = {k: v for k, v in _L0_attn_all.items() if k in ('Wq', 'Wk', 'Wv', 'Wo', 'Wg', 'bg', 'Wog')}
    del _L0_attn_all

    def _L0_ffn_setup():
        import jax, jax.numpy as jnp
        import numpy as np
        TOP_K = 2
        N_EXPERTS = 8
        key = jax.random.key(seed)
        k_x, k_g, k_w1, k_w2 = jax.random.split(key, 4)
        B, S, d_in, d_hid, d_out, E = (8, 512, 256, 512, 256, N_EXPERTS)
        s_gate = float(np.sqrt(6.0 / (d_in + E)))
        s_w1 = float(np.sqrt(6.0 / (d_in + d_hid)))
        s_w2 = float(np.sqrt(6.0 / (d_hid + d_out)))
        x = jax.random.normal(k_x, (B, S, d_in), dtype=jnp.float32)
        gate_W = jax.random.uniform(k_g, (d_in, E), jnp.float32, -s_gate, s_gate)
        W1 = jax.random.uniform(k_w1, (E, d_in, d_hid), jnp.float32, -s_w1, s_w1)
        b1 = jnp.zeros((E, d_hid), jnp.float32)
        W2 = jax.random.uniform(k_w2, (E, d_hid, d_out), jnp.float32, -s_w2, s_w2)
        b2 = jnp.zeros((E, d_out), jnp.float32)
        return {'x': x, 'gate_W': gate_W, 'W1': W1, 'b1': b1, 'W2': W2, 'b2': b2}
    _L0_ffn_all = _L0_ffn_setup()
    _L0_ffn_in = {k: v for k, v in _L0_ffn_all.items() if k in ('gate_W', 'W1', 'b1', 'W2', 'b2')}
    del _L0_ffn_all

    def _L1_attn_setup():
        import jax, jax.numpy as jnp
        import numpy as np
        EMBED = 256
        HEADS = 16
        HDIM = EMBED // HEADS
        B, S = (4, 1024)
        key = jax.random.key(seed)
        ks = jax.random.split(key, 11)
        scale = 1.0 / np.sqrt(EMBED)

        def lin(k):
            return jax.random.uniform(k, (EMBED, EMBED), jnp.float32, -scale, scale)

        def bias(k):
            return jax.random.uniform(k, (EMBED,), jnp.float32, -scale, scale)
        return {'x': jax.random.normal(ks[0], (B, S, EMBED), jnp.float32), 'Wq': lin(ks[1]), 'bq': bias(ks[2]), 'Wk': lin(ks[3]), 'bk': bias(ks[4]), 'Wv': lin(ks[5]), 'bv': bias(ks[6]), 'Wg': lin(ks[7]), 'bg': bias(ks[8]), 'Wo': lin(ks[9]), 'bo': bias(ks[10])}
    _L1_attn_all = _L1_attn_setup()
    _L1_attn_in = {k: v for k, v in _L1_attn_all.items() if k in ('Wq', 'bq', 'Wk', 'bk', 'Wv', 'bv', 'Wg', 'bg', 'Wo', 'bo')}
    del _L1_attn_all

    def _L1_ffn_setup():
        import jax, jax.numpy as jnp
        import numpy as np
        THRESHOLD = 0.1
        key = jax.random.key(seed)
        k1, k2, k3 = jax.random.split(key, 3)
        B, S, D, E = (4, 1024, 256, 8)
        inputs = jax.random.normal(k1, (B, S, D), dtype=jnp.float32)
        gate_w = jax.random.normal(k2, (D, E), dtype=jnp.float32) * 0.02
        gate_b = jnp.zeros((E,), dtype=jnp.float32)
        expert_w = jax.random.normal(k3, (E, D, D), dtype=jnp.float32) * 0.02
        expert_b = jnp.zeros((E, D), dtype=jnp.float32)
        return {'inputs': inputs, 'gate_w': gate_w, 'gate_b': gate_b, 'expert_w': expert_w, 'expert_b': expert_b}
    _L1_ffn_all = _L1_ffn_setup()
    _L1_ffn_in = {k: v for k, v in _L1_ffn_all.items() if k in ('gate_w', 'gate_b', 'expert_w', 'expert_b')}
    del _L1_ffn_all
    return {'x': x, 'txt': txt, 'L0_tok_cls_token': _L0_tok_in['cls_token'], 'L0_tok_cls_pos_embedding': _L0_tok_in['cls_pos_embedding'], 'L0_tok_ln1_g': _L0_tok_in['ln1_g'], 'L0_tok_ln1_b': _L0_tok_in['ln1_b'], 'L0_tok_W': _L0_tok_in['W'], 'L0_tok_bias': _L0_tok_in['bias'], 'L0_tok_ln2_g': _L0_tok_in['ln2_g'], 'L0_tok_ln2_b': _L0_tok_in['ln2_b'], 'L0_attn_Wq': _L0_attn_in['Wq'], 'L0_attn_Wk': _L0_attn_in['Wk'], 'L0_attn_Wv': _L0_attn_in['Wv'], 'L0_attn_Wo': _L0_attn_in['Wo'], 'L0_attn_Wg': _L0_attn_in['Wg'], 'L0_attn_bg': _L0_attn_in['bg'], 'L0_attn_Wog': _L0_attn_in['Wog'], 'L0_ffn_gate_W': _L0_ffn_in['gate_W'], 'L0_ffn_W1': _L0_ffn_in['W1'], 'L0_ffn_b1': _L0_ffn_in['b1'], 'L0_ffn_W2': _L0_ffn_in['W2'], 'L0_ffn_b2': _L0_ffn_in['b2'], 'L1_attn_Wq': _L1_attn_in['Wq'], 'L1_attn_bq': _L1_attn_in['bq'], 'L1_attn_Wk': _L1_attn_in['Wk'], 'L1_attn_bk': _L1_attn_in['bk'], 'L1_attn_Wv': _L1_attn_in['Wv'], 'L1_attn_bv': _L1_attn_in['bv'], 'L1_attn_Wg': _L1_attn_in['Wg'], 'L1_attn_bg': _L1_attn_in['bg'], 'L1_attn_Wo': _L1_attn_in['Wo'], 'L1_attn_bo': _L1_attn_in['bo'], 'L1_ffn_gate_w': _L1_ffn_in['gate_w'], 'L1_ffn_gate_b': _L1_ffn_in['gate_b'], 'L1_ffn_expert_w': _L1_ffn_in['expert_w'], 'L1_ffn_expert_b': _L1_ffn_in['expert_b']}

def reference(x, txt, L0_tok_cls_token, L0_tok_cls_pos_embedding, L0_tok_ln1_g, L0_tok_ln1_b, L0_tok_W, L0_tok_bias, L0_tok_ln2_g, L0_tok_ln2_b, L0_attn_Wq, L0_attn_Wk, L0_attn_Wv, L0_attn_Wo, L0_attn_Wg, L0_attn_bg, L0_attn_Wog, L0_ffn_gate_W, L0_ffn_W1, L0_ffn_b1, L0_ffn_W2, L0_ffn_b2, L1_attn_Wq, L1_attn_bq, L1_attn_Wk, L1_attn_bk, L1_attn_Wv, L1_attn_bv, L1_attn_Wg, L1_attn_bg, L1_attn_Wo, L1_attn_bo, L1_ffn_gate_w, L1_ffn_gate_b, L1_ffn_expert_w, L1_ffn_expert_b):
    import jax
    import jax.numpy as jnp

    def _L0_tok_ref(img, cls_token, cls_pos_embedding, ln1_g, ln1_b, W, bias, ln2_g, ln2_b):
        import jax, jax.numpy as jnp
        import numpy as np
        DIM = 256
        IMG = 96
        P = 16
        C = 3
        TEMP = 10000.0
        EPS = 1e-05
        PATCH_DIM = C * P * P
        HP = IMG // P

        def layernorm(x, gamma, beta):
            mu = jnp.mean(x, axis=-1, keepdims=True)
            var = jnp.var(x, axis=-1, keepdims=True)
            return (x - mu) * jax.lax.rsqrt(var + EPS) * gamma + beta

        def posemb_sincos_2d(h, w, dim, dtype):
            y, x = jnp.meshgrid(jnp.arange(h), jnp.arange(w), indexing='ij')
            omega = jnp.arange(dim // 4, dtype=jnp.float32) / (dim // 4 - 1)
            omega = 1.0 / TEMP ** omega
            y = y.reshape(-1)[:, None] * omega[None, :]
            x = x.reshape(-1)[:, None] * omega[None, :]
            pe = jnp.concatenate((jnp.sin(x), jnp.cos(x), jnp.sin(y), jnp.cos(y)), axis=1)
            return pe.astype(dtype)
        b = img.shape[0]
        x = img.reshape(b, C, HP, P, HP, P)
        x = jnp.transpose(x, (0, 2, 4, 3, 5, 1))
        x = x.reshape(b, HP, HP, PATCH_DIM)
        x = layernorm(x, ln1_g, ln1_b)
        x = jnp.einsum('bhwp,pd->bhwd', x, W) + bias
        x = layernorm(x, ln2_g, ln2_b)
        pe = posemb_sincos_2d(HP, HP, DIM, x.dtype)
        x = x.reshape(b, HP * HP, DIM) + pe[None]
        cls_tokens = jnp.broadcast_to(cls_token + cls_pos_embedding, (b, 1, DIM))
        return jnp.concatenate((cls_tokens, x), axis=1)

    def _L0_attn_ref(x, Wq, Wk, Wv, Wo, Wg, bg, Wog):
        import jax, jax.numpy as jnp
        from jax import lax
        import numpy as np
        DIM = 256
        H = 8
        DK = 128
        DV = 64
        GATE_NORM = 16.0

        def _gla(x, Wq, Wk, Wv, Wo, Wg, bg, Wog):
            B, S, D = x.shape
            q = (x @ Wq).reshape(B, S, H, DK)
            k = (x @ Wk).reshape(B, S, H, DK) * DK ** (-0.5)
            v = (x @ Wv).reshape(B, S, H, DV)
            alpha = jax.nn.sigmoid((x @ Wg + bg) / GATE_NORM)

            def step(state, inp):
                qt, kt, vt, at = inp
                state = at[..., None, None] * state + kt[..., None] * vt[:, :, None, :]
                out_t = jnp.einsum('bhk,bhkv->bhv', qt, state)
                return (state, out_t)
            state0 = jnp.zeros((B, H, DK, DV), x.dtype)
            xs = (jnp.moveaxis(q, 1, 0), jnp.moveaxis(k, 1, 0), jnp.moveaxis(v, 1, 0), jnp.moveaxis(alpha, 1, 0))
            _, outs = lax.scan(step, state0, xs)
            out = jnp.moveaxis(outs, 0, 1).reshape(B, S, H * DV)
            og = jax.nn.sigmoid(x @ Wog)
            return out * og @ Wo
        return _gla(x, Wq, Wk, Wv, Wo, Wg, bg, Wog)

    def _L0_ffn_ref(x, gate_W, W1, b1, W2, b2):
        import jax, jax.numpy as jnp
        import numpy as np
        TOP_K = 2
        N_EXPERTS = 8
        E = W1.shape[0]
        d_in = x.shape[-1]
        d_out = W2.shape[-1]
        x_flat = x.reshape(-1, d_in)
        logits = x_flat @ gate_W
        gates = jax.nn.softmax(logits, axis=-1)
        tk_g, tk_i = jax.lax.top_k(gates, TOP_K)
        tk_g = tk_g / (jnp.sum(tk_g, axis=-1, keepdims=True) + 1e-08)
        cw = jnp.sum(jax.nn.one_hot(tk_i, E, dtype=x.dtype) * tk_g[..., None], axis=1)
        out = x_flat
        for e in range(E):
            h = jax.nn.relu(x_flat @ W1[e] + b1[e])
            out = out + cw[:, e:e + 1] * (h @ W2[e] + b2[e])
        return out.reshape(x.shape[:-1] + (d_out,))

    def _L1_attn_ref(x, Wq, bq, Wk, bk, Wv, bv, Wg, bg, Wo, bo):
        import jax, jax.numpy as jnp
        import numpy as np
        EMBED = 256
        HEADS = 16
        HDIM = EMBED // HEADS
        B, S = (4, 1024)
        b, s, _ = x.shape

        def split_heads(t):
            return t.reshape(b, s, HEADS, HDIM).transpose(0, 2, 1, 3)
        q = split_heads(x @ Wq + bq)
        k = split_heads(x @ Wk + bk)
        v = split_heads(x @ Wv + bv)
        q = jax.nn.elu(q) + 1.0
        k = jax.nn.elu(k) + 1.0
        kv = jnp.einsum('bhsd,bhse->bhde', k, v)
        attn = jnp.einsum('bhsd,bhde->bhse', q, kv)
        attn = attn.transpose(0, 2, 1, 3).reshape(b, s, EMBED)
        gate = jax.nn.sigmoid(x @ Wg + bg)
        out = gate * attn @ Wo + bo
        return out

    def _L1_ffn_ref(inputs, gate_w, gate_b, expert_w, expert_b):
        import jax, jax.numpy as jnp
        import numpy as np
        THRESHOLD = 0.1
        d = inputs.shape[-1]
        x = inputs.reshape(-1, d)
        gate_logits = jax.nn.softmax(x @ gate_w + gate_b, axis=-1)
        selected = (gate_logits >= THRESHOLD).astype(x.dtype)
        weights = gate_logits * selected
        wsum = jnp.sum(weights, axis=-1, keepdims=True)
        weights = weights / jnp.where(wsum == 0, jnp.ones_like(wsum), wsum)
        E = expert_w.shape[0]
        out = jnp.zeros((x.shape[0], expert_w.shape[-1]), dtype=x.dtype)
        for e in range(E):
            out = out + weights[:, e:e + 1] * (x @ expert_w[e] + expert_b[e])
        return out.reshape(*inputs.shape[:-1], out.shape[-1])
    h = _L0_tok_ref(x, L0_tok_cls_token, L0_tok_cls_pos_embedding, L0_tok_ln1_g, L0_tok_ln1_b, L0_tok_W, L0_tok_bias, L0_tok_ln2_g, L0_tok_ln2_b)
    h = jnp.concatenate([h, txt], axis=1)
    h = h + _L0_attn_ref(_layernorm(h, axis=-1), L0_attn_Wq, L0_attn_Wk, L0_attn_Wv, L0_attn_Wo, L0_attn_Wg, L0_attn_bg, L0_attn_Wog)
    h = h + _L0_ffn_ref(_layernorm(h, axis=-1), L0_ffn_gate_W, L0_ffn_W1, L0_ffn_b1, L0_ffn_W2, L0_ffn_b2)
    h = h + _L1_attn_ref(_layernorm(h, axis=-1), L1_attn_Wq, L1_attn_bq, L1_attn_Wk, L1_attn_bk, L1_attn_Wv, L1_attn_bv, L1_attn_Wg, L1_attn_bg, L1_attn_Wo, L1_attn_bo)
    h = h + _L1_ffn_ref(_layernorm(h, axis=-1), L1_ffn_gate_w, L1_ffn_gate_b, L1_ffn_expert_w, L1_ffn_expert_b)
    return h

_drawn_inputs = setup_inputs


def setup_inputs(seed=0):
    import zlib

    import numpy as np

    out = dict(_drawn_inputs(seed))
    spreads = {'L0_tok_ln1_g': (1.0, 0.6),
     'L0_tok_ln1_b': (0.0, 0.277),
     'L0_tok_bias': (0.0, 0.1),
     'L0_tok_ln2_g': (1.0, 0.545),
     'L0_tok_ln2_b': (0.0, 0.1),
     'L0_attn_bg': (0.0, 2.0),
     'L0_ffn_b1': (0.0, 0.1),
     'L0_ffn_b2': (0.0, 0.1),
     'L1_ffn_gate_b': (0.0, 2.0),
     'L1_ffn_expert_b': (0.0, 2.0)}
    factors = {'L0_tok_cls_token': 3.615,
     'L0_tok_cls_pos_embedding': 3.634,
     'L0_attn_Wq': 8.0,
     'L0_attn_Wk': 8.0,
     'L0_attn_Wv': 8.0,
     'L0_attn_Wo': 8.0,
     'L0_attn_Wg': 8.0,
     'L0_attn_Wog': 8.0,
     'L1_attn_bq': 8.0,
     'L1_attn_bk': 8.0,
     'L1_attn_bg': 3.675,
     'L1_attn_bo': 200.0,
     'L1_ffn_gate_w': 27.445,
     'L1_ffn_expert_w': 25.229}
    for name, (base, spread) in spreads.items():
        noise = np.random.default_rng([zlib.crc32(name.encode()), seed]).standard_normal(out[name].shape)
        drawn = base * np.exp(spread * noise) if base else spread * noise
        out[name] = jnp.asarray(drawn.astype(out[name].dtype))
    for name, factor in factors.items():
        out[name] = (out[name] * factor).astype(out[name].dtype)
    return out
```

```python
from contextlib import ExitStack

import concourse.bass as bass
import numpy as np
from concourse import mybir

F32 = mybir.dt.float32
F32R = mybir.dt.float32r
ALU = mybir.AluOpType
ACT = mybir.ActivationFunctionType
AX_X = mybir.AxisListType.X
ds = bass.ds

P = 128
B = 4
D = 256
KC = D // P
IMG, PATCH, COLORS = 96, 16, 3
HP = IMG // PATCH
NPATCH = HP * HP
TXT = 512
S = 1 + NPATCH + TXT
CH = 110
NCH = 5
SP = CH * NCH
NT = B * SP
G = 4 * CH
NG = NT // G
PIECES = ((0, 276), (276, SP - 276))
HEADS, DK, DV = 8, 128, 64
PAIRS = HEADS // 2
E = 8
HID = 512
EPS = 1e-5
BANK = 512
FAR = -1e30


def open_stage(nc, ctx, stage):
    def sb(name, shape, dt=F32):
        return ctx.enter_context(nc.sbuf_tensor(f"{stage}_{name}", shape, dt))

    def ps(name, shape):
        return ctx.enter_context(nc.psum_tensor(f"{stage}_{name}", shape, F32))

    sems = []

    def sem(name):
        sems.append(nc.alloc_semaphore(f"{stage}_{name}"))
        return sems[-1]

    def close():
        nc.clear_and_free_semaphores(sems)
        nc.all_engine_barrier()

    ctx.callback(close)
    return sb, ps, sem


def product(nc, out, w, x, first, last):
    (w_hi, w_lo), (x_hi, x_lo) = w, x
    nc.tensor.matmul(out, w_lo, x_hi, start=first, stop=False)
    nc.tensor.matmul(out, w_hi, x_lo, start=False, stop=False)
    return nc.tensor.matmul(out, w_hi, x_hi, start=False, stop=last)


def spread(ap, axis, n):
    wide = ap.unsqueeze(axis)
    shape = list(wide.shape)
    shape[axis] = n
    return wide.broadcast_to(shape)


def stage_tokens(nc, m, d):
    TB = 2
    TP = TB * NPATCH
    PD = COLORS * PATCH * PATCH
    PC = PD // P
    with ExitStack() as ctx:
        sb, ps, sem = open_stage(nc, ctx, "tok")
        img = sb("img", [TP, 2, PD])
        w = sb("w_patch", [P, PC, D])
        g1 = sb("g1", [P, PC])
        b1 = sb("b1", [P, PC])
        g2 = sb("g2", [P, KC])
        pos = sb("pos", [P, KC, NPATCH])
        b2 = sb("b2", [P, KC])
        posb = sb("posb", [P, KC, NPATCH])
        cls = sb("cls", [P, KC])
        cpos = sb("cpos", [P, KC])
        bias = sb("bias", [TP, D])
        txt = sb("txt", [P, B, TXT // P, D])
        stats = sb("stats", [TP, 2, 2, 6])
        mv = sb("mv", [TP, 2, 2])
        logv = sb("logv", [TP, 2])
        rstd = sb("rstd", [TP, 2])
        xg = sb("xg", [P, PC, TP])
        xt = sb("xt", [P, 2, PC, TP])
        emb = sb("emb", [TP, 2, D])
        embn = sb("embn", [TP, 2, D])
        stats2 = sb("stats2", [TP, 2, 6])
        mv2 = sb("mv2", [TP, 2, 2])
        logv2 = sb("logv2", [TP, 2])
        rstd2 = sb("rstd2", [TP, 2])
        pt = [ps(f"pt{i}", [P, BANK]) for i in range(4)]
        px = [ps(f"px{i}", [P, BANK]) for i in range(2)]
        pe_ = [ps(f"pe{i}", [P, BANK]) for i in range(2)]

        img_loaded = [sem(f"img_loaded{t}") for t in range(2)]
        txt_loaded = [sem(f"txt_loaded{b}") for b in range(B)]
        w_loaded = sem("w_loaded")
        small_loaded = sem("small_loaded")
        consts = sem("consts")
        ident_zero = sem("ident_zero")
        ident_ready = sem("ident_ready")
        txt_turned = sem("txt_turned")
        txt_kept = sem("txt_kept")
        chain = sem("dve_chain")
        stats_ready = sem("stats_ready")
        logv_ready = sem("logv_ready")
        rstd_ready = sem("rstd_ready")
        normed = sem("normed")
        patches_turned = sem("patches_turned")
        xt_ready = sem("xt_ready")
        embedded = sem("embedded")
        emb_normed = sem("emb_normed")
        emb_turned = sem("emb_turned")

        hv = m.h[:, :, :].rearrange("p k (b s) -> p k b s", b=B)

        with nc.Block() as block:
            @block.sync
            def _(sp):
                for t in range(2):
                    sp.dma_start(img[:, t], d["patches"][t * TP:(t + 1) * TP]).then_inc(img_loaded[t], 16)

            @block.gpsimd
            def _(pool):
                for b in range(B):
                    pool.dma_start(txt[:, b], d["txt"][b].rearrange("(j p) d -> p j d", p=P)).then_inc(txt_loaded[b], 16)
                nc.gpsimd.memset(m.ident[:], 0.0).then_inc(ident_zero, 1)
                pool.wait_ge(ident_zero, 1)
                nc.gpsimd.affine_select(out=m.ident[:], in_=m.ident[:], compare_op=ALU.not_equal, fill=1.0, base=0,
                                        pattern=[[-1, P]], channel_multiplier=1).then_inc(ident_ready, 1)
                nc.gpsimd.memset(m.causal[:], 0.0).then_inc(ident_zero, 1)
                pool.wait_ge(ident_zero, 2)
                nc.gpsimd.affine_select(out=m.causal[:], in_=m.causal[:], compare_op=ALU.is_ge, fill=FAR, base=0,
                                        pattern=[[1, CH]], channel_multiplier=-1).then_inc(ident_ready, 1)
                pool.wait_ge(ident_ready, 2)
                nc.gpsimd.memset(m.mean_w[:], 1.0 / D)
                nc.gpsimd.memset(m.one[:], 1.0)
                nc.gpsimd.memset(m.eps[:], EPS).then_inc(consts, 1)
                for kc in range(KC):
                    last = nc.gpsimd.memset(hv[:, kc, :, S:SP], 0.0)
                last.then_inc(consts, 1)
                pool.wait_ge(small_loaded, 16 * 8)
                for kc in range(KC):
                    last = nc.gpsimd.tensor_tensor(hv[:, kc, :, 0], cls[:, kc:kc + 1].broadcast_to([P, B]),
                                                   cpos[:, kc:kc + 1].broadcast_to([P, B]), ALU.add)
                last.then_inc(consts, 1)
                pool.wait_ge(consts, 3)

            @block.scalar
            def _(act):
                by_feature = "(k p) -> p k"
                act.dma_start(w[:], d["L0_tok_W"].rearrange("(k p) n -> p k n", p=P)).then_inc(w_loaded, 16)
                act.dma_start(g1[:], d["L0_tok_ln1_g"].rearrange(by_feature, p=P)).then_inc(small_loaded, 16)
                act.dma_start(b1[:], d["L0_tok_ln1_b"].rearrange(by_feature, p=P)).then_inc(small_loaded, 16)
                act.dma_start(bias[:], d["L0_tok_bias"].partition_broadcast(TP)).then_inc(small_loaded, 16)
                act.dma_start(g2[:], d["L0_tok_ln2_g"].rearrange(by_feature, p=P)).then_inc(small_loaded, 16)
                act.dma_start(b2[:], d["L0_tok_ln2_b"].rearrange(by_feature, p=P)).then_inc(small_loaded, 16)
                act.dma_start(pos[:], d["pos"]).then_inc(small_loaded, 16)
                act.dma_start(cls[:], d["L0_tok_cls_token"][0, 0].rearrange(by_feature, p=P)).then_inc(small_loaded, 16)
                act.dma_start(cpos[:], d["L0_tok_cls_pos_embedding"][0, 0].rearrange(by_feature, p=P)).then_inc(small_loaded, 16)
                for n in range(B * KC):
                    b, kc = divmod(n, KC)
                    act.wait_ge(txt_turned, n + 1)
                    nc.scalar.activation(m.h[:, kc, b * SP + 1 + NPATCH:b * SP + S], pt[n % 4][:], ACT.Copy).then_inc(txt_kept, 1)
                act.wait_ge(consts, 1)
                for t in range(2):
                    act.wait_ge(stats_ready, t + 1)
                    nc.scalar.activation(logv[:, t:t + 1], mv[:, t, 1:2], ACT.Ln, bias=m.eps[0:TP]).then_inc(logv_ready, 1)
                    act.wait_ge(logv_ready, t + 1)
                    nc.scalar.activation(rstd[:, t:t + 1], logv[:, t:t + 1], ACT.Exp, scale=-0.5).then_inc(rstd_ready, 1)
                for t in range(2):
                    act.wait_ge(stats_ready, t + 3)
                    nc.scalar.activation(logv2[:, t:t + 1], mv2[:, t, 1:2], ACT.Ln, bias=m.eps[0:TP]).then_inc(logv_ready, 1)
                    act.wait_ge(logv_ready, t + 3)
                    nc.scalar.activation(rstd2[:, t:t + 1], logv2[:, t:t + 1], ACT.Exp, scale=-0.5).then_inc(rstd_ready, 1)

            @block.vector
            def _(dve):
                made = [0]

                def link(ins):
                    made[0] += 1
                    ins.then_inc(chain, 1)
                    dve.wait_ge(chain, made[0])

                for t in range(2):
                    dve.wait_ge(img_loaded[t], 16)
                    for i in range(2):
                        last = nc.vector.bn_stats(stats[:, t, i], img[:, t, i * (PD // 2):(i + 1) * (PD // 2)])
                    link(last)
                    nc.vector.bn_aggr(mv[:, t], stats[:, t].rearrange("p a b -> p (a b)")).then_inc(stats_ready, 1)
                dve.wait_ge(small_loaded, 16 * 8)
                link(nc.vector.tensor_tensor(posb[:], pos[:], spread(b2[:], 2, NPATCH), ALU.add))
                for t in range(2):
                    dve.wait_ge(rstd_ready, t + 1)
                    nc.vector.tensor_scalar(img[:, t], img[:, t], mv[:, t, 0:1], rstd[:, t:t + 1],
                                            ALU.subtract, ALU.mult).then_inc(normed, 1)
                for t in range(2):
                    dve.wait_ge(patches_turned, t + 1)
                    link(nc.vector.tensor_tensor(xg[:], px[t][:, 0:PC * TP].rearrange("p (k n) -> p k n", k=PC),
                                                 spread(g1[:], 2, TP), ALU.mult))
                    nc.vector.tensor_tensor(xt[:, t], xg[:], spread(b1[:], 2, TP),
                                            ALU.add).then_inc(xt_ready, 1)
                    dve.wait_ge(xt_ready, t + 1)
                for t in range(2):
                    dve.wait_ge(embedded, t + 1)
                    link(nc.vector.tensor_tensor(emb[:, t], pe_[t][0:TP, 0:D], bias[:], ALU.add))
                    link(nc.vector.bn_stats(stats2[:, t], emb[:, t]))
                    nc.vector.bn_aggr(mv2[:, t], stats2[:, t]).then_inc(stats_ready, 1)
                for t in range(2):
                    dve.wait_ge(rstd_ready, t + 3)
                    nc.vector.tensor_scalar(embn[:, t], emb[:, t], mv2[:, t, 0:1], rstd2[:, t:t + 1],
                                            ALU.subtract, ALU.mult).then_inc(emb_normed, 1)
                for t in range(2):
                    dve.wait_ge(emb_turned, t + 1)
                    for kc in range(KC):
                        nc.vector.scalar_tensor_tensor(
                            hv[:, kc, t * TB:(t + 1) * TB, 1:1 + NPATCH],
                            px[t][:, kc * TP:(kc + 1) * TP].rearrange("p (b s) -> p b s", b=TB), g2[:, kc:kc + 1],
                            spread(posb[:, kc], 1, TB), ALU.mult, ALU.add)

            @block.tensor
            def _(pe):
                pe.wait_ge(ident_ready, 1)
                for n in range(B * KC):
                    b, kc = divmod(n, KC)
                    if kc == 0:
                        pe.wait_ge(txt_loaded[b], 16)
                    if n >= 4:
                        pe.wait_ge(txt_kept, n - 3)
                    for j in range(TXT // P):
                        last = nc.tensor.transpose(pt[n % 4][:, j * P:(j + 1) * P], txt[:, b, j, kc * P:(kc + 1) * P], m.ident[:])
                    last.then_inc(txt_turned, 1)
                for t in range(2):
                    pe.wait_ge(normed, t + 1)
                    for k in range(PC):
                        last = nc.tensor.transpose(px[t][:, k * TP:(k + 1) * TP], img[:, t, k * P:(k + 1) * P], m.ident[0:TP, 0:TP])
                    last.then_inc(patches_turned, 1)
                pe.wait_ge(w_loaded, 16)
                for t in range(2):
                    pe.wait_ge(xt_ready, t + 1)
                    for k in range(PC):
                        last = nc.tensor.matmul(pe_[t][0:TP, 0:D], xt[:, t, k], w[:, k],
                                                start=(k == 0), stop=(k == PC - 1))
                    last.then_inc(embedded, 1)
                for t in range(2):
                    pe.wait_ge(emb_normed, t + 1)
                    for kc in range(KC):
                        last = nc.tensor.transpose(px[t][:, kc * TP:(kc + 1) * TP], embn[:, t, kc * P:(kc + 1) * P], m.ident[0:TP, 0:TP])
                    last.then_inc(emb_turned, 1)


def stage_norm(nc, m, stage):
    ON_POOL = (1, 3)
    with ExitStack() as ctx:
        sb, ps, sem = open_stage(nc, ctx, stage)
        pair = sb("pair", [P, NT])
        dev = sb("dev", [P, KC, NT])
        sq = sb("sq", [P, KC, NT])
        rstd = sb("rstd_t", [P, NT])
        bank = ps("norm_bank", [P, NG, BANK])
        pair_ready = sem("pair_ready")
        mean_ready = sem("mean_ready")
        dev_ready = sem("dev_ready")
        sq_ready = sem("sq_ready")
        sum_ready = sem("sum_ready")
        var_ready = sem("var_ready")
        logv_ready = sem("logv_t_ready")
        rstd_ready = sem("rstd_t_ready")
        y_ready = sem("y_ready")
        hi_ready = sem("hi_ready")

        def group(t, i):
            return t[:, :, ds(i * G, G)]

        with nc.Block() as block:
            @block.gpsimd
            def _(pool):
                with pool.Fori(0, NG) as i:
                    nc.gpsimd.tensor_tensor(pair[:, ds(i * G, G)], m.h[:, 0, ds(i * G, G)], m.h[:, 1, ds(i * G, G)],
                                            ALU.add).then_inc(pair_ready, 1)
                with pool.Fori(0, NG) as i:
                    pool.wait_ge(sq_ready, i + 1)
                    pool.wait_ge(mean_ready, i + 1)
                    nc.gpsimd.tensor_tensor(pair[:, ds(i * G, G)], sq[:, 0, ds(i * G, G)], sq[:, 1, ds(i * G, G)],
                                            ALU.add).then_inc(sum_ready, 1)
                for i in ON_POOL:
                    at = slice(i * G, (i + 1) * G)
                    pool.wait_ge(hi_ready, i + 1)
                    nc.gpsimd.tensor_tensor(m.x_lo[:, :, at], dev[:, :, at], m.x_hi[:, :, at].bitcast(F32), ALU.subtract)

            @block.tensor
            def _(pe):
                for i in range(NG):
                    pe.wait_ge(pair_ready, i + 1)
                    nc.tensor.matmul(bank[:, i, 0:G], m.mean_w[:], pair[:, i * G:(i + 1) * G],
                                     start=True, stop=True).then_inc(mean_ready, 1)
                for i in range(NG):
                    pe.wait_ge(sum_ready, i + 1)
                    pe.wait_ge(dev_ready, i + 1)
                    nc.tensor.matmul(bank[:, i, 0:G], m.mean_w[:], pair[:, i * G:(i + 1) * G],
                                     start=True, stop=True).then_inc(var_ready, 1)

            @block.vector
            def _(dve):
                for i in range(NG):
                    at = slice(i * G, (i + 1) * G)
                    dve.wait_ge(mean_ready, i + 1)
                    nc.vector.tensor_tensor(dev[:, :, at], m.h[:, :, at], spread(bank[:, i, 0:G], 1, KC),
                                            ALU.subtract).then_inc(dev_ready, 1)
                for i in range(NG):
                    at = slice(i * G, (i + 1) * G)
                    dve.wait_ge(rstd_ready, i + 1)
                    nc.vector.tensor_tensor(dev[:, :, at], dev[:, :, at], spread(rstd[:, at], 1, KC),
                                            ALU.mult).then_inc(y_ready, 1)
                    if i not in ON_POOL:
                        dve.wait_ge(hi_ready, i + 1)
                        nc.vector.tensor_tensor(m.x_lo[:, :, at], dev[:, :, at], m.x_hi[:, :, at].bitcast(F32), ALU.subtract)

            @block.scalar
            def _(act):
                for i in range(NG):
                    at = slice(i * G, (i + 1) * G)
                    act.wait_ge(dev_ready, i + 1)
                    nc.scalar.activation(sq[:, :, at], dev[:, :, at], ACT.Square).then_inc(sq_ready, 1)
                for i in range(NG):
                    at = slice(i * G, (i + 1) * G)
                    act.wait_ge(var_ready, i + 1)
                    nc.scalar.activation(rstd[:, at], bank[:, i, 0:G], ACT.Ln, bias=m.eps[:]).then_inc(logv_ready, 1)
                act.wait_ge(logv_ready, NG)
                for i in range(NG):
                    at = slice(i * G, (i + 1) * G)
                    nc.scalar.activation(rstd[:, at], rstd[:, at], ACT.Exp, scale=-0.5).then_inc(rstd_ready, 1)
                for i in range(NG):
                    at = slice(i * G, (i + 1) * G)
                    act.wait_ge(y_ready, i + 1)
                    nc.scalar.activation(m.x_hi[:, :, at], dev[:, :, at], ACT.Copy).then_inc(hi_ready, 1)


def stage_decay(nc, m, d):
    with ExitStack() as ctx:
        sb, ps, sem = open_stage(nc, ctx, "decay")
        w = sb("wg", [P, KC, HEADS])
        w_hi = sb("wg_hi", [P, KC, P], F32R)
        w_lo = sb("wg_lo", [P, KC, P], F32R)
        bias = sb("bg", [HEADS, 1])
        z = sb("z", [HEADS, NT])
        mag = sb("mag", [HEADS, NT])
        same = sb("same_chunk", [HEADS, B * NCH, CH])
        rows = sb("decay_rows", [HEADS, NT])
        bank = ps("z_bank", [P, NG, BANK])
        turned = ps("rows_turned", [P, BANK])
        loaded = sem("wg_loaded")
        w_ready = sem("wg_ready")
        z_ready = sem("z_ready")
        logits_ready = sem("z_logits_ready")
        chain = sem("decay_chain")
        mag_ready = sem("mag_ready")
        rows_ready = sem("decay_rows_ready")
        turned_ready = sem("rows_turned_ready")
        stored = sem("decay_stored")
        mask_ready = sem("same_chunk_ready")
        with nc.Block() as block:
            @block.sync
            def _(sp):
                sp.dma_start(w[:], d["L0_attn_Wg"].rearrange("(k p) n -> p k n", p=P)).then_inc(loaded, 16)
                sp.dma_start(bias[:], d["L0_attn_bg"].rearrange("(n o) -> n o", o=1)).then_inc(loaded, 16)
                sp.wait_ge(rows_ready, 1)
                sp.dma_start(m.decay_rows_dram, rows[:]).then_inc(stored, 16)
                sp.wait_ge(stored, 16)

            @block.gpsimd
            def _(pool):
                nc.gpsimd.memset(same[:], 1.0).then_inc(mask_ready, 1)
                pool.wait_ge(mask_ready, 1)
                nc.gpsimd.memset(same[:, :, 0:1], 0.0).then_inc(mask_ready, 1)

            @block.vector
            def _(dve):
                nc.vector.memset(w_hi[:].bitcast(F32), 0.0).then_inc(chain, 1)
                nc.vector.memset(w_lo[:].bitcast(F32), 0.0).then_inc(chain, 1)
                dve.wait_ge(loaded, 32)
                dve.wait_ge(chain, 2)
                nc.vector.tensor_copy(w_hi[:, :, 0:HEADS], w[:]).then_inc(chain, 1)
                dve.wait_ge(chain, 3)
                nc.vector.tensor_tensor(w_lo[:, :, 0:HEADS], w[:], w_hi[:, :, 0:HEADS].bitcast(F32),
                                        ALU.subtract).then_inc(w_ready, 1)
                nc.vector.tensor_scalar(bias[:], bias[:], 1.0 / 16.0, None, ALU.mult).then_inc(w_ready, 1)
                dve.wait_ge(z_ready, NG)
                dve.wait_ge(mag_ready, 1)
                nc.vector.scalar_tensor_tensor(z[:], z[:], 0.0, mag[:], ALU.min, ALU.subtract).then_inc(chain, 1)
                dve.wait_ge(chain, 4)
                dve.wait_ge(mask_ready, 2)
                nc.vector.tensor_tensor_scan(rows[:], same[:].rearrange("h c t -> h (c t)"), z[:], 0.0,
                                             ALU.mult, ALU.add).then_inc(rows_ready, 1)
                dve.wait_ge(turned_ready, 1)
                nc.vector.tensor_copy(m.decay_sum[:].rearrange("t h n -> t n h"),
                                      turned[0:CH, 0:B * NCH * HEADS].rearrange("t (n h) -> t n h", h=HEADS))

            @block.scalar
            def _(act):
                act.wait_ge(w_ready, 2)
                for i in range(NG):
                    act.wait_ge(logits_ready, i + 1)
                    nc.scalar.activation(z[:, i * G:(i + 1) * G], bank[0:HEADS, i, 0:G], ACT.Identity,
                                         bias=bias[:], scale=1.0 / 16.0).then_inc(z_ready, 1)
                act.wait_ge(z_ready, NG)
                nc.scalar.activation(mag[:], z[:], ACT.Abs).then_inc(z_ready, 1)
                act.wait_ge(z_ready, NG + 1)
                nc.scalar.activation(mag[:], mag[:], ACT.Exp, scale=-1.0).then_inc(z_ready, 1)
                act.wait_ge(z_ready, NG + 2)
                nc.scalar.activation(mag[:], mag[:], ACT.Ln, bias=m.one[0:HEADS]).then_inc(mag_ready, 1)

            @block.tensor
            def _(pe):
                pe.wait_ge(w_ready, 1)
                for i in range(NG):
                    for kc in range(KC):
                        last = product(nc, bank[:, i, 0:G], (w_hi[:, kc], w_lo[:, kc]),
                                       (m.x_hi[:, kc, i * G:(i + 1) * G], m.x_lo[:, kc, i * G:(i + 1) * G]),
                                       kc == 0, kc == KC - 1)
                    last.then_inc(logits_ready, 1)
                pe.wait_ge(rows_ready, 1)
                for c in range(B * NCH):
                    last = nc.tensor.transpose(turned[0:CH, c * HEADS:(c + 1) * HEADS], rows[:, c * CH:(c + 1) * CH],
                                               m.ident[0:HEADS, 0:HEADS])
                last.then_inc(turned_ready, 1)


def stage_gla(nc, m, d):
    NPC = len(PIECES)
    KINDS = ["k0", "k0", "k1", "k1", "v", "v", "q0", "q0", "q1", "q1", "g", "g"]
    WQ, WK, WV, WO, WW = 0, 2 * DK, 4 * DK, 4 * DK + 2 * DV, 4 * DK + 4 * DV
    PJ = [("in", s, j) for s in range(2) for j in range(len(KINDS))] + [("out", s, j) for s in range(2) for j in range(2 * NPC)]
    PJ_DVE = [u for u in PJ if u[0] == "out" or KINDS[u[2]] in ("v", "q1")]
    PJ_ACT = [u for u in PJ if u not in PJ_DVE]
    TS = [(s, n) for s in range(2) for n in ("score0", "score1", "score2", "key0", "key1", "value0", "value1")] + [(0, "state"), (1, "state")]
    TS_ACT = [u for u in TS if u[1].startswith("key")]
    TS_DVE = [u for u in TS if u not in TS_ACT]
    NPJ, NTS = 4, 2
    with ExitStack() as ctx:
        sb, ps, sem = open_stage(nc, ctx, "gla")
        w_raw = sb("w_raw", [P, KC, WW])
        w_hi = sb("w_hi", [P, KC, WW], F32R)
        w_lo = sb("w_lo", [P, KC, WW], F32R)
        wo_raw = sb("wo_raw", [P, D])
        wo_hi = sb("wo_hi", [P, D], F32R)
        wo_lo = sb("wo_lo", [P, D], F32R)
        two = range(2)
        key_t = [sb(f"key_t{s}", [P, 2, SP]) for s in two]
        query_t = [sb(f"query_t{s}", [P, 2, SP]) for s in two]
        query_dec = [sb(f"query_dec{s}", [P, 2, SP]) for s in two]
        value_t = [sb(f"value_t{s}", [P, SP]) for s in two]
        sums = [sb(f"sums{s}", [P, 2, NCH, CH]) for s in two]
        since = [sb(f"since{s}", [P, 2, NCH, CH]) for s in two]
        decay = [sb(f"decay{s}", [CH, 2, NCH, CH]) for s in two]
        probs = [sb(f"probs{s}", [CH, 2, NCH, CH]) for s in two]
        key = [sb(f"key{s}", [CH, 2, NCH - 1, DK]) for s in two]
        value = [sb(f"value{s}", [CH, NCH, 2 * DV]) for s in two]
        value_dec = [sb(f"value_dec{s}", [CH, NCH - 1, 2, DV]) for s in two]
        state = [sb(f"state{s}", [P, NCH - 1, 2 * DV]) for s in two]
        gate = [sb(f"gate{s}", [P, SP]) for s in two]
        mixed = [sb(f"mixed{s}", [P, SP]) for s in two]
        mixed_hi = [sb(f"mixed_hi{s}", [P, SP], F32R) for s in two]
        mixed_lo = [sb(f"mixed_lo{s}", [P, SP], F32R) for s in two]
        pj = [ps(f"pj{i}", [P, BANK]) for i in range(NPJ)]
        ts = [ps(f"ts{i}", [P, BANK]) for i in range(NTS)]
        att = [ps(f"att{i}", [P, BANK]) for i in range(2)]

        w_loaded = sem("w_loaded")
        w_rounded = sem("w_rounded")
        w_split = sem("w_split")
        wo_loaded = sem("wo_loaded")
        wo_rounded = sem("wo_rounded")
        wo_split = sem("wo_split")
        pj_full = sem("pj_full")
        pj_act = sem("pj_taken_by_act")
        pj_dve = sem("pj_taken_by_dve")
        ts_full = sem("ts_full")
        ts_act = sem("ts_taken_by_act")
        ts_dve = sem("ts_taken_by_dve")
        state_chain = sem("state_chain")
        sums_loaded = [sem(f"sums_loaded{s}") for s in two]
        diff_ready = [sem(f"diff_ready{s}") for s in two]
        decay_ready = [sem(f"decay_ready{s}") for s in two]
        since_ready = [sem(f"since_ready{s}") for s in two]
        query_dec_ready = [sem(f"query_dec_ready{s}") for s in two]
        value_dec_ready = [sem(f"value_dec_ready{s}") for s in two]
        att_full = [sem(f"att_full{s}") for s in two]
        mixed_ready = [sem(f"mixed_ready{s}") for s in two]
        hi_ready = [sem(f"mixed_hi_ready{s}") for s in two]
        lo_ready = [sem(f"mixed_lo_ready{s}") for s in two]

        def pj_taken(eng, i, use, before=False):
            users, s_ = (PJ_DVE, pj_dve) if use in PJ_DVE else (PJ_ACT, pj_act)
            eng.wait_ge(s_, (i + (0 if before else 1)) * len(users) + users.index(use) + 1)

        def ts_taken(eng, i, use, before=False):
            users, s_ = (TS_DVE, ts_dve) if use in TS_DVE else (TS_ACT, ts_act)
            eng.wait_ge(s_, (i + (0 if before else 1)) * len(users) + users.index(use) + 1)

        def cols(t, first, n):
            return t[:, ds(first, n)]

        with nc.Block() as block:
            @block.sync
            def _(sp):
                with sp.Fori(0, 2) as j:
                    with sp.Fori(0, PAIRS) as p:
                        i = j * PAIRS + p
                        sp.wait_ge(w_split, i)
                        for src, n, at in ((d["L0_attn_Wq"], 2 * DK, WQ), (d["L0_attn_Wk"], 2 * DK, WK),
                                           (d["L0_attn_Wv"], 2 * DV, WV), (d["L0_attn_Wog"], 2 * DV, WO)):
                            sp.dma_start(w_raw[:, :, at:at + n],
                                         src.rearrange("(k p) n -> p k n", p=P)[:, :, ds(p * n, n)]).then_inc(w_loaded, 16)
                        sp.wait_ge(wo_split, i)
                        sp.dma_start(wo_raw[:], d["L0_attn_Wo"][ds(p * P, P), :]).then_inc(wo_loaded, 16)
                        for s in two:
                            sp.wait_ge(diff_ready[s], i)
                            sp.wait_ge(since_ready[s], i)
                            sp.dma_start(sums[s][:].rearrange("q h c t -> q h (c t)"),
                                         m.decay_rows_dram[ds(p * 2, 2), ds((j * 2 + s) * SP, SP)].partition_broadcast(P)
                                         ).then_inc(sums_loaded[s], 16)

            @block.gpsimd
            def _(pool):
                def low_part(i):
                    pool.wait_ge(w_rounded, i + 1)
                    nc.gpsimd.tensor_tensor(w_lo[:], w_raw[:], w_hi[:].bitcast(F32), ALU.subtract).then_inc(w_split, 1)

                def step(i, more):
                    for s in two:
                        pj_taken(pool, i, ("in", s, 7))
                        pj_taken(pool, i, ("in", s, 9))
                        pool.wait_ge(since_ready[s], i + 1)
                        pool.wait_ge(att_full[s], i * 2)
                        nc.gpsimd.tensor_tensor(query_dec[s][:], query_t[s][:], since[s][:].rearrange("q h c t -> q h (c t)"),
                                                ALU.mult).then_inc(query_dec_ready[s], 1)
                    for s in two:
                        ts_taken(pool, i, (s, "value0"))
                        pool.wait_ge(decay_ready[s], i + 1)
                        nc.gpsimd.tensor_tensor(
                            value_dec[s][:], value[s][:, 0:NCH - 1].rearrange("t c (h v) -> t c h v", h=2),
                            spread(decay[s][:, :, 0:NCH - 1, CH - 1].rearrange("t h c -> t c h"), 3, DV),
                            ALU.mult).then_inc(value_dec_ready[s], 1)
                    pool.wait_ge(wo_rounded, i * 2 + 2)
                    nc.gpsimd.tensor_tensor(wo_lo[:], wo_raw[:], wo_hi[:].bitcast(F32), ALU.subtract).then_inc(wo_split, 1)
                    if more:
                        low_part(i + 1)

                low_part(0)
                with pool.Fori(0, 2 * PAIRS - 1) as i:
                    step(i, True)
                step(2 * PAIRS - 1, False)

            @block.scalar
            def _(act):
                act.sem_inc(pj_act, len(PJ_ACT))
                act.sem_inc(ts_act, len(TS_ACT))
                def round_weights(i):
                    act.wait_ge(w_loaded, i * 64 + 64)
                    if not isinstance(i, int) or i > 0:
                        act.wait_ge(pj_full, i * len(PJ) - 4 * NPC)
                    nc.scalar.activation(w_hi[:], w_raw[:], ACT.Copy).then_inc(w_rounded, 1)

                def step(i, more):
                    for s in two:
                        act.wait_ge(sums_loaded[s], i * 16 + 16)
                        act.wait_ge(query_dec_ready[s], i)
                        ts_taken(act, i, (s, "state"), before=True)
                        nc.scalar.activation(since[s][:], sums[s][:], ACT.Exp).then_inc(since_ready[s], 1)
                    for s in two:
                        for k, kind in enumerate(KINDS):
                            if kind in ("v", "q1"):
                                continue
                            first, n = PIECES[k % NPC]
                            act.wait_ge(pj_full, i * len(PJ) + PJ.index(("in", s, k)) + 1)
                            bank = pj[PJ.index(("in", s, k)) % NPJ][:, 0:n]
                            if kind[0] == "k":
                                out = nc.scalar.activation(key_t[s][:, int(kind[1]), first:first + n], bank, ACT.Copy, scale=DK ** -0.5)
                            elif kind[0] == "q":
                                out = nc.scalar.activation(query_t[s][:, int(kind[1]), first:first + n], bank, ACT.Copy)
                            else:
                                act.wait_ge(mixed_ready[s], i * 2)
                                out = nc.scalar.activation(gate[s][:, first:first + n], bank, ACT.Tanh, scale=0.5)
                            out.then_inc(pj_act, 1)
                        act.wait_ge(diff_ready[s], i + 1)
                        nc.scalar.activation(decay[s][:], decay[s][:], ACT.Exp).then_inc(decay_ready[s], 1)
                    act.wait_ge(wo_loaded, i * 16 + 16)
                    act.wait_ge(pj_full, i * len(PJ))
                    nc.scalar.activation(wo_raw[:], wo_raw[:], ACT.Copy, scale=0.5).then_inc(wo_rounded, 1)
                    act.wait_ge(wo_rounded, i * 2 + 1)
                    nc.scalar.activation(wo_hi[:], wo_raw[:], ACT.Copy).then_inc(wo_rounded, 1)
                    for s in two:
                        for h in two:
                            act.wait_ge(ts_full, i * len(TS) + TS.index((s, f"key{h}")) + 1)
                            nc.scalar.activation(key[s][:, h].rearrange("t c k -> t (c k)"),
                                                 ts[TS.index((s, f"key{h}")) % NTS][0:CH, :], ACT.Copy).then_inc(ts_act, 1)
                    if more:
                        round_weights(i + 1)
                    for s in two:
                        act.wait_ge(mixed_ready[s], i * 2 + 2)
                        nc.scalar.activation(mixed_hi[s][:], mixed[s][:], ACT.Copy).then_inc(hi_ready[s], 1)

                round_weights(0)
                with act.Fori(0, 2 * PAIRS - 1) as i:
                    step(i, True)
                step(2 * PAIRS - 1, False)

            @block.vector
            def _(dve):
                dve.sem_inc(pj_dve, len(PJ_DVE))
                dve.sem_inc(ts_dve, len(TS_DVE))
                with dve.Fori(0, 2) as j:
                  with dve.Fori(0, PAIRS) as p:
                    i = j * PAIRS + p
                    for s in two:
                        dve.wait_ge(sums_loaded[s], i * 16 + 16)
                        dve.wait_ge(value_dec_ready[s], i)
                        for h in two:
                            for c in range(NCH):
                                own = m.decay_sum[:, ds(p * 2 + h, 1), ds((j * 2 + s) * NCH + c, 1)].rearrange("t h n -> t (h n)")
                                last = nc.vector.scalar_tensor_tensor(decay[s][:, h, c], sums[s][0:CH, h, c], own, m.causal[:],
                                                                      ALU.subtract, ALU.add)
                        last.then_inc(diff_ready[s], 1)
                    for s in two:
                        dve.wait_ge(query_dec_ready[s], i)
                        for k, out in ((4, value_t[s][:]), (5, value_t[s][:]), (8, query_t[s][:, 1]), (9, query_t[s][:, 1])):
                            first, size = PIECES[k % NPC]
                            use = PJ.index(("in", s, k))
                            dve.wait_ge(pj_full, i * len(PJ) + use + 1)
                            nc.vector.tensor_copy(out[:, first:first + size], pj[use % NPJ][:, 0:size]).then_inc(pj_dve, 1)
                    for s in two:
                        for n in range(3):
                            use = TS.index((s, f"score{n}"))
                            nchunk = 2 if n < 2 else 1
                            dve.wait_ge(ts_full, i * len(TS) + use + 1)
                            dve.wait_ge(decay_ready[s], i + 1)
                            dve.wait_ge(att_full[s], i * 2)
                            nc.vector.tensor_tensor(
                                probs[s][:, :, 2 * n:2 * n + nchunk],
                                ts[use % NTS][0:CH, 0:2 * nchunk * CH].rearrange("k (h c t) -> k h c t", h=2, c=nchunk),
                                decay[s][:, :, 2 * n:2 * n + nchunk], ALU.mult).then_inc(ts_dve, 1)
                        for n, (c0, c1) in enumerate(((0, NCH - 1), (NCH - 1, NCH))):
                            use = TS.index((s, f"value{n}"))
                            dve.wait_ge(ts_full, i * len(TS) + use + 1)
                            nc.vector.tensor_copy(value[s][:, c0:c1].rearrange("t c v -> t (c v)"),
                                                  ts[use % NTS][0:CH, 0:(c1 - c0) * 2 * DV]).then_inc(ts_dve, 1)
                    for s in two:
                        use = TS.index((s, "state"))
                        dve.wait_ge(ts_full, i * len(TS) + use + 1)
                        dve.wait_ge(since_ready[s], i + 1)
                        part = ts[use % NTS][:].rearrange("k (c v) -> k c v", c=NCH - 1)
                        nc.vector.tensor_copy(state[s][:, 0], part[:, 0]).then_inc(state_chain, 1)
                        for c in range(1, NCH - 1):
                            dve.wait_ge(state_chain, i * 6 + s * 3 + c)
                            for h in two:
                                v = slice(h * DV, (h + 1) * DV)
                                last = nc.vector.scalar_tensor_tensor(state[s][:, c, v], state[s][:, c - 1, v],
                                                                      since[s][:, h, c, CH - 1:CH], part[:, c, v], ALU.mult, ALU.add)
                            last.then_inc(state_chain if c < NCH - 2 else ts_dve, 1)
                    for s in two:
                        dve.wait_ge(lo_ready[s], i)
                        for n, (c0, c1) in enumerate(((0, NCH - 1), (NCH - 1, NCH))):
                            dve.wait_ge(att_full[s], i * 2 + n + 1)
                            pj_taken(dve, i, ("in", s, 11))
                            at = slice(c0 * CH, c1 * CH)
                            nc.vector.scalar_tensor_tensor(mixed[s][:, at], gate[s][:, at], 1.0, att[n][:, 0:(c1 - c0) * CH],
                                                           ALU.add, ALU.mult).then_inc(mixed_ready[s], 1)
                    for s in two:
                        dve.wait_ge(hi_ready[s], i + 1)
                        nc.vector.tensor_tensor(mixed_lo[s][:], mixed[s][:], mixed_hi[s][:].bitcast(F32),
                                                ALU.subtract).then_inc(lo_ready[s], 1)
                    for s in two:
                        for n in range(2 * NPC):
                            kc, (first, size) = n // NPC, PIECES[n % NPC]
                            use = PJ.index(("out", s, n))
                            dve.wait_ge(pj_full, i * len(PJ) + use + 1)
                            at = m.h[:, kc, ds((j * 2 + s) * SP + first, size)]
                            nc.vector.tensor_tensor(at, at, pj[use % NPJ][:, 0:size], ALU.add).then_inc(pj_dve, 1)

            @block.tensor
            def _(pe):
                def take_pj(i, use):
                    u = PJ.index(use)
                    pj_taken(pe, i, PJ[(u - NPJ) % len(PJ)], before=u < NPJ)
                    return pj[u % NPJ]

                def take_ts(i, use):
                    u = TS.index(use)
                    ts_taken(pe, i, TS[(u - NTS) % len(TS)], before=u < NTS)
                    return ts[u % NTS]

                with pe.Fori(0, 2) as j:
                  with pe.Fori(0, PAIRS) as p:
                    i = j * PAIRS + p
                    pe.wait_ge(w_split, i + 1)
                    for s in two:
                        for k, kind in enumerate(KINDS):
                            first, n = PIECES[k % NPC]
                            at = {"k": WK, "v": WV, "q": WQ, "g": WO}[kind[0]] + (DK if kind[-1] == "1" else 0)
                            bank = take_pj(i, ("in", s, k))
                            for kc in range(KC):
                                x = [t[:, kc, ds((j * 2 + s) * SP + first, n)] for t in (m.x_hi, m.x_lo)]
                                last = product(nc, bank[:, 0:n], (w_hi[:, kc, at:at + P], w_lo[:, kc, at:at + P]), x,
                                               kc == 0, kc == KC - 1)
                            last.then_inc(pj_full, 1)
                    for s in two:
                        pj_taken(pe, i, ("in", s, 7))
                        pj_taken(pe, i, ("in", s, 9))
                        for n in range(3):
                            nchunk = 2 if n < 2 else 1
                            bank = take_ts(i, (s, f"score{n}"))
                            for h in two:
                                for c in range(nchunk):
                                    at = slice((2 * n + c) * CH, (2 * n + c + 1) * CH)
                                    o = (h * nchunk + c) * CH
                                    last = nc.tensor.matmul(bank[0:CH, o:o + CH], key_t[s][:, h, at], query_t[s][:, h, at],
                                                            start=True, stop=True)
                            last.then_inc(ts_full, 1)
                        for h in two:
                            bank = take_ts(i, (s, f"key{h}"))
                            for c in range(NCH - 1):
                                last = nc.tensor.transpose(bank[0:CH, c * DK:(c + 1) * DK], key_t[s][:, h, c * CH:(c + 1) * CH], m.ident[:])
                            last.then_inc(ts_full, 1)
                        pj_taken(pe, i, ("in", s, 5))
                        for n, (c0, c1) in enumerate(((0, NCH - 1), (NCH - 1, NCH))):
                            bank = take_ts(i, (s, f"value{n}"))
                            for c in range(c0, c1):
                                last = nc.tensor.transpose(bank[0:CH, (c - c0) * P:(c - c0 + 1) * P], value_t[s][:, c * CH:(c + 1) * CH], m.ident[:])
                            last.then_inc(ts_full, 1)
                    for s in two:
                        ts_taken(pe, i, (s, "key1"))
                        pe.wait_ge(value_dec_ready[s], i + 1)
                        bank = take_ts(i, (s, "state"))
                        for c in range(NCH - 1):
                            for h in two:
                                o = c * 2 * DV + h * DV
                                last = nc.tensor.matmul(bank[:, o:o + DV], key[s][:, h, c], value_dec[s][:, c, h], start=True, stop=True)
                        last.then_inc(ts_full, 1)
                    for s in two:
                        pe.wait_ge(mixed_ready[1 - s], (i + s) * 2)
                        ts_taken(pe, i, (s, "state"))
                        pe.wait_ge(query_dec_ready[s], i + 1)
                        for c in range(NCH):
                            bank, o = (att[0], c * CH) if c < NCH - 1 else (att[1], 0)
                            for h in two:
                                out = bank[h * DV:(h + 1) * DV, o:o + CH]
                                last = nc.tensor.matmul(out, value[s][:, c, h * DV:(h + 1) * DV], probs[s][:, h, c], start=True, stop=c == 0)
                                if c > 0:
                                    last = nc.tensor.matmul(out, state[s][:, c - 1, h * DV:(h + 1) * DV],
                                                            query_dec[s][:, h, c * CH:(c + 1) * CH], start=False, stop=True)
                            if c >= NCH - 2:
                                last.then_inc(att_full[s], 1)
                    pe.wait_ge(wo_split, i + 1)
                    for s in two:
                        pe.wait_ge(lo_ready[s], i + 1)
                        for n in range(2 * NPC):
                            kc, (first, size) = n // NPC, PIECES[n % NPC]
                            bank = take_pj(i, ("out", s, n))
                            at = slice(kc * P, (kc + 1) * P)
                            product(nc, bank[:, 0:size], (wo_hi[:, at], wo_lo[:, at]),
                                    (mixed_hi[s][:, first:first + size], mixed_lo[s][:, first:first + size]),
                                    True, True).then_inc(pj_full, 1)


def stage_gate(nc, m, d, stage, gate_w, gate_b, top_two):
    with ExitStack() as ctx:
        sb, ps, sem = open_stage(nc, ctx, stage)
        NTILE = B * NCH
        w = sb("gate_w", [P, KC, E])
        w_hi = sb("gate_w_hi", [P, KC, P], F32R)
        w_lo = sb("gate_w_lo", [P, KC, P], F32R)
        bias = sb("gate_b", [E, 1])
        z = sb("gate_z", [E, NT])
        rank = sb("rank", [CH, NTILE, E])
        shape = [CH, NTILE, E]
        shifted, ex, g, a, b_, one1, one2, rest, cw = (sb(f"gate_{n}", shape) for n in
                                                       ("shifted", "ex", "g", "a", "b_", "one1", "one2", "rest", "cw"))
        top, total, inv, first, best, second = (sb(f"gate_{n}", [CH, NTILE]) for n in
                                                ("top", "total", "inv", "first", "best", "second"))
        rows = sb("cw_rows", [E, NT])
        bank = ps("gate_bank", [P, NG, BANK])
        turned = ps("gate_turned", [P, BANK])
        loaded = sem("gate_loaded")
        w_ready = sem("gate_w_ready")
        logits_ready = sem("gate_logits_ready")
        z_ready = sem("gate_z_ready")
        turned_ready = sem("gate_turned_ready")
        chain = sem("gate_chain")
        shifted_ready = sem("gate_shifted_ready")
        ex_ready = sem("gate_ex_ready")
        rank_ready = sem("rank_ready")
        cw_ready = sem("cw_ready")
        back_ready = sem("cw_back_ready")
        rows_ready = sem("cw_rows_ready")
        stored = sem("cw_stored")
        with nc.Block() as block:
            @block.sync
            def _(sp):
                sp.dma_start(w[:], gate_w.rearrange("(k p) n -> p k n", p=P)).then_inc(loaded, 16)
                if gate_b is not None:
                    sp.dma_start(bias[:], gate_b.rearrange("(n o) -> n o", o=1)).then_inc(loaded, 16)
                sp.wait_ge(rows_ready, NG)
                sp.dma_start(m.cw_dram, rows[:]).then_inc(stored, 16)
                sp.wait_ge(stored, 16)

            @block.gpsimd
            def _(pool):
                if gate_b is None:
                    nc.gpsimd.memset(bias[:], 0.0).then_inc(rank_ready, 1)
                for e in range(E):
                    last = nc.gpsimd.memset(rank[:, :, e:e + 1], float(E - e))
                last.then_inc(rank_ready, 1)

            @block.scalar
            def _(act):
                act.wait_ge(loaded, 16 if gate_b is None else 32)
                act.wait_ge(rank_ready, 2 if gate_b is None else 1)
                for i in range(NG):
                    act.wait_ge(logits_ready, i + 1)
                    nc.scalar.activation(z[:, i * G:(i + 1) * G], bank[0:E, i, 0:G], ACT.Identity, bias=bias[:]).then_inc(z_ready, 1)
                act.wait_ge(shifted_ready, 1)
                nc.scalar.activation(ex[:], shifted[:], ACT.Exp).then_inc(ex_ready, 1)
                for i in range(NG):
                    act.wait_ge(back_ready, i + 1)
                    nc.scalar.activation(rows[:, i * G:(i + 1) * G], bank[0:E, i, 0:G], ACT.Copy).then_inc(rows_ready, 1)

            @block.vector
            def _(dve):
                made = [0]

                def link(ins):
                    made[0] += 1
                    ins.then_inc(chain, 1)
                    dve.wait_ge(chain, made[0])

                def wide(t):
                    return spread(t[:], 2, E)

                link(nc.vector.memset(w_hi[:].bitcast(F32), 0.0))
                link(nc.vector.memset(w_lo[:].bitcast(F32), 0.0))
                dve.wait_ge(loaded, 16 if gate_b is None else 32)
                link(nc.vector.tensor_copy(w_hi[:, :, 0:E], w[:]))
                nc.vector.tensor_tensor(w_lo[:, :, 0:E], w[:], w_hi[:, :, 0:E].bitcast(F32), ALU.subtract).then_inc(w_ready, 1)
                dve.wait_ge(turned_ready, 1)
                logits = turned[0:CH, 0:NTILE * E].rearrange("t (n e) -> t n e", e=E)
                link(nc.vector.tensor_reduce(top[:], logits, AX_X, ALU.max))
                nc.vector.tensor_tensor(shifted[:], logits, wide(top), ALU.subtract).then_inc(shifted_ready, 1)
                dve.wait_ge(ex_ready, 1)
                link(nc.vector.tensor_reduce(total[:], ex[:], AX_X, ALU.add))
                link(nc.vector.reciprocal(inv[:], total[:]))
                link(nc.vector.tensor_tensor(g[:], ex[:], wide(inv), ALU.mult))
                if top_two:
                    dve.wait_ge(rank_ready, 2 if gate_b is None else 1)

                    def pick(src, value, one):
                        link(nc.vector.tensor_reduce(value[:], src[:], AX_X, ALU.max))
                        link(nc.vector.tensor_tensor(a[:], src[:], wide(value), ALU.is_ge))
                        link(nc.vector.tensor_tensor(b_[:], a[:], rank[:], ALU.mult))
                        link(nc.vector.tensor_reduce(best[:], b_[:], AX_X, ALU.max))
                        link(nc.vector.tensor_tensor(one[:], b_[:], wide(best), ALU.is_equal))

                    pick(g, first, one1)
                    link(nc.vector.scalar_tensor_tensor(rest[:], one1[:], -2.0, g[:], ALU.mult, ALU.add))
                    pick(rest, second, one2)
                    link(nc.vector.tensor_tensor(a[:], one1[:], one2[:], ALU.add))
                    link(nc.vector.tensor_tensor(b_[:], a[:], g[:], ALU.mult))
                    link(nc.vector.scalar_tensor_tensor(total[:], first[:], 1e-8, second[:], ALU.add, ALU.add))
                else:
                    link(nc.vector.scalar_tensor_tensor(b_[:], g[:], 0.1, g[:], ALU.is_ge, ALU.mult))
                    link(nc.vector.tensor_reduce(top[:], b_[:], AX_X, ALU.add))
                    link(nc.vector.scalar_tensor_tensor(total[:], top[:], 0.0, top[:], ALU.is_equal, ALU.add))
                link(nc.vector.reciprocal(inv[:], total[:]))
                nc.vector.tensor_tensor(cw[:], b_[:], wide(inv), ALU.mult).then_inc(cw_ready, 1)

            @block.tensor
            def _(pe):
                pe.wait_ge(w_ready, 1)
                for i in range(NG):
                    for kc in range(KC):
                        last = product(nc, bank[:, i, 0:G], (w_hi[:, kc], w_lo[:, kc]),
                                       (m.x_hi[:, kc, i * G:(i + 1) * G], m.x_lo[:, kc, i * G:(i + 1) * G]),
                                       kc == 0, kc == KC - 1)
                    last.then_inc(logits_ready, 1)
                pe.wait_ge(z_ready, NG)
                for c in range(NTILE):
                    last = nc.tensor.transpose(turned[0:CH, c * E:(c + 1) * E], z[:, c * CH:(c + 1) * CH], m.ident[0:E, 0:E])
                last.then_inc(turned_ready, 1)
                pe.wait_ge(cw_ready, 1)
                for c in range(NTILE):
                    i, o = divmod(c * CH, G)
                    last = nc.tensor.transpose(bank[0:E, i, o:o + CH], cw[:, c], m.ident[0:CH, 0:CH])
                    if o + CH == G:
                        last.then_inc(back_ready, 1)


def stage_hidden_experts(nc, m, d):
    HC = HID // P
    W1N, WN = KC * HID, KC * HID + HC * D
    NS = 2 * NG
    with ExitStack() as ctx:
        sb, ps, sem = open_stage(nc, ctx, "ffn0")
        two = range(2)
        raw = [sb(f"raw{s}", [P, WN]) for s in two]
        w_hi = [sb(f"e_hi{s}", [P, WN], F32R) for s in two]
        w_lo = [sb(f"e_lo{s}", [P, WN], F32R) for s in two]
        b1 = sb("b1_all", [P, E, HC])
        b1_of = [sb(f"b1_of{s}", [P, HC]) for s in two]
        b2 = sb("b2_all", [P, E, KC])
        cw = [sb(f"cw{s}", [P, NT]) for s in two]
        hid = [sb(f"hid{s}", [P, HC, G]) for s in two]
        hid_hi = [sb(f"hid_hi{s}", [P, HC, G], F32R) for s in two]
        hid_lo = [sb(f"hid_lo{s}", [P, HC, G], F32R) for s in two]
        part = [sb(f"part{s}", [P, KC, G]) for s in two]
        hb = [ps(f"hb{i}", [P, BANK]) for i in range(HC)]
        ob = [ps(f"ob{i}", [P, BANK]) for i in range(2 * KC)]
        raw_loaded = [sem(f"raw_loaded{s}") for s in two]
        cw_loaded = [sem(f"cw_loaded{s}") for s in two]
        bias_loaded = sem("bias_loaded")
        b1_ready = [sem(f"b1_ready{s}") for s in two]
        x_added = sem("x_added")
        rounded = [sem(f"w_rounded{s}") for s in two]
        split = [sem(f"w_split{s}") for s in two]
        hid_full = sem("hid_full")
        relu_done = sem("relu_done")
        hi_done = sem("hid_hi_done")
        lo_done = sem("hid_lo_done")
        out_full = sem("out_full")
        weighted = sem("weighted")
        summed = sem("summed")

        def w1(w, kc, hc):
            return w[:, kc * HID + hc * P:kc * HID + (hc + 1) * P]

        def w2(w, hc, kc):
            return w[:, W1N + hc * D + kc * P:W1N + hc * D + (kc + 1) * P]

        def reached(i, per, k, n):
            return (i + 1) * NS * per + k * per + n

        with nc.Block() as block:
            @block.sync
            def _(sp):
                sp.dma_start(b1[:], d["L0_ffn_b1"].rearrange("e (c p) -> p e c", p=P)).then_inc(bias_loaded, 16)
                sp.dma_start(b2[:], d["L0_ffn_b2"].rearrange("e (c p) -> p e c", p=P)).then_inc(bias_loaded, 16)
                with sp.Fori(0, E // 2) as i:
                    for s in two:
                        e = i * 2 + s
                        sp.wait_ge(split[s], i)
                        sp.dma_start(raw[s][:, 0:W1N].rearrange("p (k n) -> p k n", k=KC),
                                     d["L0_ffn_W1"][ds(e, 1)].rearrange("o (k p) n -> p (o k) n", p=P)).then_inc(raw_loaded[s], 16)
                        sp.dma_start(raw[s][:, W1N:WN].rearrange("p (k n) -> p k n", k=HC),
                                     d["L0_ffn_W2"][ds(e, 1)].rearrange("o (k p) n -> p (o k) n", p=P)).then_inc(raw_loaded[s], 16)
                        sp.wait_ge(weighted, reached(i, 2, s * NG + NG - 1 - NS, 2))
                        sp.dma_start(cw[s][:], m.cw_dram[ds(e, 1)].rearrange("o n -> (o n)").partition_broadcast(P)).then_inc(cw_loaded[s], 16)

            @block.gpsimd
            def _(pool):
                pool.sem_inc(summed, NS)
                def low_part(i, s):
                    pool.wait_ge(rounded[s], i + 1)
                    nc.gpsimd.tensor_tensor(w_lo[s][:], raw[s][:], w_hi[s][:].bitcast(F32), ALU.subtract).then_inc(split[s], 1)

                def step(i, more):
                    for k in range(NS):
                        at = slice(k % NG * G, (k % NG + 1) * G)
                        pool.wait_ge(weighted, reached(i, 2, k, 2))
                        pool.wait_ge(summed, reached(i, 1, k - NG, 1))
                        nc.gpsimd.tensor_tensor(m.h[:, :, at], m.h[:, :, at], part[k % 2][:], ALU.add).then_inc(summed, 1)
                        if k == 0:
                            low_part(i, 1)
                        if k == NG and more:
                            low_part(i + 1, 0)

                low_part(0, 0)
                for t in (m.x_hi, m.x_lo):
                    for i in range(NG):
                        at = slice(i * G, (i + 1) * G)
                        nc.gpsimd.tensor_tensor(m.h[:, :, at], m.h[:, :, at], t[:, :, at].bitcast(F32), ALU.add).then_inc(x_added, 1)
                    pool.wait_ge(x_added, NG if t is m.x_hi else 2 * NG)

                with pool.Fori(0, E // 2 - 1) as i:
                    step(i, True)
                step(E // 2 - 1, False)

            @block.scalar
            def _(act):
                act.sem_inc(relu_done, NS * HC)

                def round_weights(i, s):
                    act.wait_ge(raw_loaded[s], i * 32 + 32)
                    act.wait_ge(out_full, reached(i, 1, s * NG + NG - 1 - NS, 1))
                    nc.scalar.activation(w_hi[s][:], raw[s][:], ACT.Copy).then_inc(rounded[s], 1)

                def step(i, more):
                    for k in range(NS):
                        if k % NG == 0:
                            act.wait_ge(b1_ready[k // NG], i + 1)
                        act.wait_ge(lo_done, reached(i, 1, k - 2, 1))
                        for hc in range(HC):
                            act.wait_ge(hid_full, i * NS * HC + k * HC + hc + 1)
                            nc.scalar.activation(hid[k % 2][:, hc], hb[hc][:, 0:G], ACT.Relu,
                                                 bias=b1_of[k // NG][:, hc:hc + 1]).then_inc(relu_done, 1)
                        if k == 0:
                            round_weights(i, 1)
                        if k == NG and more:
                            round_weights(i + 1, 0)

                round_weights(0, 0)
                with act.Fori(0, E // 2 - 1) as i:
                    step(i, True)
                step(E // 2 - 1, False)

            @block.vector
            def _(dve):
                dve.sem_inc(lo_done, NS)
                dve.sem_inc(weighted, NS * 2)
                dve.wait_ge(bias_loaded, 32)
                with dve.Fori(0, E // 2) as i:
                    def weigh(k):
                        s, g = divmod(k, NG)
                        dve.wait_ge(out_full, reached(i, 1, k, 1))
                        dve.wait_ge(summed, reached(i, 1, k - 2, 1))
                        for kc in range(KC):
                            nc.vector.scalar_tensor_tensor(part[k % 2][:, kc], ob[k % 2 * KC + kc][:, 0:G],
                                                           b2[:, ds(i * 2 + s, 1), kc],
                                                           cw[s][:, g * G:(g + 1) * G], ALU.add, ALU.mult).then_inc(weighted, 1)

                    for k in range(NS):
                        if k < 2:
                            nc.vector.tensor_copy(b1_of[k][:], b1[:, ds(i * 2 + k, 1)].rearrange("p o c -> p (o c)")).then_inc(b1_ready[k], 1)
                        if k % NG == 0:
                            dve.wait_ge(cw_loaded[k // NG], i * 16 + 16)
                        dve.wait_ge(relu_done, reached(i, HC, k, HC))
                        dve.wait_ge(out_full, reached(i, 1, k - 2, 1))
                        nc.vector.tensor_copy(hid_hi[k % 2][:], hid[k % 2][:]).then_inc(hi_done, 1)
                        dve.wait_ge(hi_done, i * NS + k + 1)
                        nc.vector.tensor_tensor(hid_lo[k % 2][:], hid[k % 2][:], hid_hi[k % 2][:].bitcast(F32),
                                                ALU.subtract).then_inc(lo_done, 1)
                        if k > 0:
                            weigh(k - 1)
                    weigh(NS - 1)

            @block.tensor
            def _(pe):
                pe.sem_inc(out_full, NS)
                with pe.Fori(0, E // 2) as i:
                    def up(k):
                        s, g = divmod(k, NG)
                        if g == 0:
                            pe.wait_ge(split[s], i + 1)
                        for hc in range(HC):
                            pe.wait_ge(relu_done, reached(i, HC, k - 1, hc + 1))
                            for kc in range(KC):
                                x = [t[:, kc, g * G:(g + 1) * G] for t in (m.x_hi, m.x_lo)]
                                last = product(nc, hb[hc][:, 0:G], (w1(w_hi[s], kc, hc), w1(w_lo[s], kc, hc)), x, kc == 0, kc == KC - 1)
                            last.then_inc(hid_full, 1)

                    def down(k):
                        s = k // NG
                        pe.wait_ge(lo_done, reached(i, 1, k, 1))
                        pe.wait_ge(weighted, reached(i, 2, k - 2, 2))
                        for kc in range(KC):
                            for hc in range(HC):
                                last = product(nc, ob[k % 2 * KC + kc][:, 0:G], (w2(w_hi[s], hc, kc), w2(w_lo[s], hc, kc)),
                                               (hid_hi[k % 2][:, hc], hid_lo[k % 2][:, hc]), hc == 0, hc == HC - 1)
                        last.then_inc(out_full, 1)

                    up(0)
                    for k in range(1, NS):
                        up(k)
                        down(k - 1)
                    down(NS - 1)


def stage_linear_attention(nc, m, d):
    HDIM = 16
    NPC = len(PIECES)
    MATS = "kvqgo"
    KINDS = [(kind, mc, n) for kind in "kvqg" for mc in range(KC) for n in range(NPC)]
    PJ = ([("in", s) + u for s in range(2) for u in KINDS] + [("att", s, mc, n) for s in range(2) for mc in range(KC) for n in range(NPC)]
          + [("out", s, mc, n) for s in range(2) for mc in range(KC) for n in range(NPC)])
    PJ_ACT = [u for u in PJ if u[0] == "in"]
    PJ_DVE = [u for u in PJ if u not in PJ_ACT]
    ELU = [u for u in PJ if u[0] == "in" and u[2] in "kq"]
    NPJ, NTS = 4, 2
    with ExitStack() as ctx:
        sb, ps, sem = open_stage(nc, ctx, "attn1")
        two = range(2)
        raw = sb("raw", [P, 5, KC, D])
        w_hi = sb("hi", [P, 5, KC, D], F32R)
        w_lo = sb("lo", [P, 5, KC, D], F32R)
        bias = sb("bias", [P, 5, KC])
        half_bias = sb("half_bias", [P, KC])
        block_mask = sb("block_mask", [P, P])
        key_t = [sb(f"key_t{s}", [P, KC, SP]) for s in two]
        value_t = [sb(f"value_t{s}", [P, KC, SP]) for s in two]
        query_t = [sb(f"query_t{s}", [P, KC, SP]) for s in two]
        gate = [sb(f"gate{s}", [P, KC, SP]) for s in two]
        ex = [sb(f"ex{i}", [P, PIECES[0][1]]) for i in range(4)]
        pos = [sb(f"pos{i}", [P, PIECES[0][1]]) for i in range(4)]
        rows = [sb(f"rows{s}", [CH, NCH, 2 * D]) for s in two]
        kv = [sb(f"kv{s}", [P, KC, P]) for s in two]
        mixed = [sb(f"mixed{s}", [P, KC, SP]) for s in two]
        mixed_hi = [sb(f"mixed_hi{s}", [P, KC, SP], F32R) for s in two]
        mixed_lo = [sb(f"mixed_lo{s}", [P, KC, SP], F32R) for s in two]
        pj = [ps(f"pj{i}", [P, BANK]) for i in range(NPJ)]
        ts = [ps(f"ts{i}", [P, BANK]) for i in range(NTS)]
        kvb = [ps(f"kvb{s}", [P, BANK]) for s in two]
        loaded = sem("loaded")
        rounded = sem("rounded")
        split = sem("split")
        mask_ready = sem("mask_ready")
        bias_ready = sem("bias_ready")
        pj_full = sem("pj_full")
        pj_act = sem("pj_taken_by_act")
        pj_dve = sem("pj_taken_by_dve")
        elu_ready = sem("elu_ready")
        ts_full = sem("ts_full")
        rows_ready = sem("rows_ready")
        kv_full = sem("kv_full")
        kv_ready = sem("kv_ready")
        hi_ready = sem("hi_ready")
        lo_ready = sem("lo_ready")

        def pj_taken(eng, i, use, before=False):
            users, s_ = (PJ_DVE, pj_dve) if use in PJ_DVE else (PJ_ACT, pj_act)
            eng.wait_ge(s_, (i + (0 if before else 1)) * len(users) + users.index(use) + 1)

        with nc.Block() as block:
            @block.sync
            def _(sp):
                for n, w in enumerate((d["L1_attn_Wk"], d["L1_attn_Wv"], d["L1_attn_Wq"], d["L1_attn_Wg"], d["L1_attn_Wo"])):
                    sp.dma_start(raw[:, n], w.rearrange("(k p) n -> p k n", p=P)).then_inc(loaded, 16)
                for n, b in enumerate((d["L1_attn_bk"], d["L1_attn_bv"], d["L1_attn_bq"], d["L1_attn_bg"], d["L1_attn_bo"])):
                    sp.dma_start(bias[:, n], b.rearrange("(k p) -> p k", p=P)).then_inc(loaded, 16)

            @block.gpsimd
            def _(pool):
                nc.gpsimd.memset(block_mask[:], 1.0).then_inc(mask_ready, 1)
                blocks = block_mask[:].rearrange("p (n c) -> p n c", c=HDIM)
                pool.wait_ge(mask_ready, 1)
                nc.gpsimd.affine_select(out=blocks, in_=blocks, compare_op=ALU.is_ge, fill=0.0, base=0,
                                        pattern=[[-HDIM, P // HDIM], [0, HDIM]], channel_multiplier=1).then_inc(mask_ready, 1)
                pool.wait_ge(mask_ready, 2)
                nc.gpsimd.affine_select(out=blocks, in_=blocks, compare_op=ALU.is_ge, fill=0.0, base=HDIM - 1,
                                        pattern=[[HDIM, P // HDIM], [0, HDIM]], channel_multiplier=-1).then_inc(mask_ready, 1)
                pool.wait_ge(loaded, 160)
                nc.gpsimd.tensor_scalar(half_bias[:], bias[:, MATS.index("g")], 0.5, None, ALU.mult).then_inc(bias_ready, 1)
                nc.gpsimd.tensor_scalar(raw[:, MATS.index("o")], raw[:, MATS.index("o")], 0.5, None, ALU.mult).then_inc(bias_ready, 1)
                for n in range(5):
                    pool.wait_ge(rounded, n + 1)
                    nc.gpsimd.tensor_tensor(w_lo[:, n], raw[:, n], w_hi[:, n].bitcast(F32), ALU.subtract).then_inc(split, 1)
                with pool.Fori(0, B // 2) as i:
                    for s in two:
                        pool.wait_ge(hi_ready, i * 2 + s + 1)
                        nc.gpsimd.tensor_tensor(mixed_lo[s][:], mixed[s][:], mixed_hi[s][:].bitcast(F32),
                                                ALU.subtract).then_inc(lo_ready, 1)

            @block.scalar
            def _(act):
                act.sem_inc(pj_act, len(PJ_ACT))
                act.wait_ge(loaded, 160)
                for n in range(5):
                    if n == MATS.index("o"):
                        act.wait_ge(bias_ready, 2)
                    nc.scalar.activation(w_hi[:, n], raw[:, n], ACT.Copy).then_inc(rounded, 1)
                with act.Fori(0, B // 2) as i:
                    for s in two:
                        for kind, mc, n in KINDS:
                            first, size = PIECES[n]
                            use = ("in", s, kind, mc, n)
                            u = PJ.index(use)
                            bank = pj[u % NPJ][:, 0:size]
                            act.wait_ge(pj_full, i * len(PJ) + u + 1)
                            if kind in "kq":
                                v = ELU.index(use)
                                act.wait_ge(elu_ready, (i + 1) * len(ELU) + v - 3)
                                nc.scalar.activation(ex[v % 4][:, 0:size], bank, ACT.Exp, bias=bias[:, MATS.index(kind), mc:mc + 1])
                                nc.scalar.activation(pos[v % 4][:, 0:size], bank, ACT.Relu,
                                                     bias=bias[:, MATS.index(kind), mc:mc + 1]).then_inc(pj_act, 1)
                            elif kind == "v":
                                nc.scalar.activation(value_t[s][:, mc, first:first + size], bank, ACT.Identity,
                                                     bias=bias[:, MATS.index("v"), mc:mc + 1]).then_inc(pj_act, 1)
                            else:
                                pj_taken(act, i, ("att", s, KC - 1, NPC - 1), before=True)
                                nc.scalar.activation(gate[s][:, mc, first:first + size], bank, ACT.Tanh, scale=0.5,
                                                     bias=half_bias[:, mc:mc + 1]).then_inc(pj_act, 1)
                    for s in two:
                        pj_taken(act, i, ("att", s, KC - 1, NPC - 1))
                        nc.scalar.activation(mixed_hi[s][:], mixed[s][:], ACT.Copy).then_inc(hi_ready, 1)

            @block.vector
            def _(dve):
                dve.sem_inc(pj_dve, len(PJ_DVE))
                dve.sem_inc(elu_ready, len(ELU))
                dve.wait_ge(loaded, 160)
                dve.wait_ge(mask_ready, 3)
                with dve.Fori(0, B // 2) as i:
                    for s in two:
                        for kind, mc, n in KINDS:
                            if kind not in "kq":
                                continue
                            first, size = PIECES[n]
                            use = ("in", s, kind, mc, n)
                            v = ELU.index(use)
                            pj_taken(dve, i, use)
                            out = (key_t if kind == "k" else query_t)[s]
                            nc.vector.scalar_tensor_tensor(out[:, mc, first:first + size], ex[v % 4][:, 0:size], 1.0,
                                                           pos[v % 4][:, 0:size], ALU.min, ALU.add).then_inc(elu_ready, 1)
                    for s in two:
                        for c in range(NCH):
                            dve.wait_ge(ts_full, i * 2 * NCH + s * NCH + c + 1)
                            nc.vector.tensor_copy(rows[s][:, c], ts[(s * NCH + c) % NTS][0:CH, :]).then_inc(rows_ready, 1)
                    for s in two:
                        dve.wait_ge(kv_full, i * 2 + s + 1)
                        nc.vector.tensor_tensor(kv[s][:], kvb[s][:, 0:KC * P].rearrange("p (k n) -> p k n", k=KC),
                                                spread(block_mask[:], 1, KC), ALU.mult).then_inc(kv_ready, 1)
                    for s in two:
                        dve.wait_ge(lo_ready, i * 2)
                        pj_taken(dve, i, ("in", s, "g", KC - 1, NPC - 1))
                        for mc in range(KC):
                            for n, (first, size) in enumerate(PIECES):
                                use = ("att", s, mc, n)
                                u = PJ.index(use)
                                dve.wait_ge(pj_full, i * len(PJ) + u + 1)
                                at = slice(first, first + size)
                                nc.vector.scalar_tensor_tensor(mixed[s][:, mc, at], gate[s][:, mc, at], 1.0,
                                                               pj[u % NPJ][:, 0:size], ALU.add, ALU.mult).then_inc(pj_dve, 1)
                    for s in two:
                        for mc in range(KC):
                            for n, (first, size) in enumerate(PIECES):
                                use = ("out", s, mc, n)
                                u = PJ.index(use)
                                dve.wait_ge(pj_full, i * len(PJ) + u + 1)
                                at = m.h[:, mc, ds((i * 2 + s) * SP + first, size)]
                                nc.vector.scalar_tensor_tensor(at, pj[u % NPJ][:, 0:size], bias[:, MATS.index("o"), mc:mc + 1], at,
                                                               ALU.add, ALU.add).then_inc(pj_dve, 1)

            @block.tensor
            def _(pe):
                def take_pj(i, use):
                    u = PJ.index(use)
                    pj_taken(pe, i, PJ[(u - NPJ) % len(PJ)], before=u < NPJ)
                    return pj[u % NPJ]

                with pe.Fori(0, B // 2) as i:
                    for s in two:
                        for kind, mc, n in KINDS:
                            if s == 0 and mc == 0 and n == 0:
                                pe.wait_ge(split, MATS.index(kind) + 1)
                            first, size = PIECES[n]
                            bank = take_pj(i, ("in", s, kind, mc, n))
                            wn, at = MATS.index(kind), slice(mc * P, (mc + 1) * P)
                            for kc in range(KC):
                                x = [t[:, kc, ds((i * 2 + s) * SP + first, size)] for t in (m.x_hi, m.x_lo)]
                                last = product(nc, bank[:, 0:size], (w_hi[:, wn, kc, at], w_lo[:, wn, kc, at]), x, kc == 0, kc == KC - 1)
                            last.then_inc(pj_full, 1)
                    for s in two:
                        pe.wait_ge(elu_ready, (i + 1) * len(ELU) + ELU.index(("in", s, "k", KC - 1, NPC - 1)) + 1)
                        pj_taken(pe, i, ("in", s, "v", KC - 1, NPC - 1))
                        for c in range(NCH):
                            pe.wait_ge(rows_ready, i * 2 * NCH + s * NCH + c - 1 if s * NCH + c >= NTS else i * 2 * NCH)
                            for t, src in enumerate((key_t[s], value_t[s])):
                                for mc in range(KC):
                                    last = nc.tensor.transpose(ts[(s * NCH + c) % NTS][0:CH, t * D + mc * P:t * D + (mc + 1) * P],
                                                               src[:, mc, c * CH:(c + 1) * CH], m.ident[:])
                            last.then_inc(ts_full, 1)
                    for s in two:
                        pe.wait_ge(rows_ready, i * 2 * NCH + (s + 1) * NCH)
                        pe.wait_ge(kv_ready, i * 2)
                        for mc in range(KC):
                            for c in range(NCH):
                                n = min(CH, S - c * CH)
                                last = nc.tensor.matmul(kvb[s][:, mc * P:(mc + 1) * P], rows[s][0:n, c, mc * P:(mc + 1) * P],
                                                        rows[s][0:n, c, D + mc * P:D + (mc + 1) * P], start=c == 0, stop=c == NCH - 1)
                        last.then_inc(kv_full, 1)
                    for s in two:
                        pe.wait_ge(kv_ready, i * 2 + s + 1)
                        pe.wait_ge(elu_ready, (i + 1) * len(ELU) + ELU.index(("in", s, "q", KC - 1, NPC - 1)) + 1)
                        for mc in range(KC):
                            for n, (first, size) in enumerate(PIECES):
                                bank = take_pj(i, ("att", s, mc, n))
                                nc.tensor.matmul(bank[:, 0:size], kv[s][:, mc], query_t[s][:, mc, first:first + size],
                                                 start=True, stop=True).then_inc(pj_full, 1)
                    pe.wait_ge(split, 5)
                    for s in two:
                        pe.wait_ge(lo_ready, i * 2 + s + 1)
                        for mc in range(KC):
                            for n, (first, size) in enumerate(PIECES):
                                bank = take_pj(i, ("out", s, mc, n))
                                wn, at = MATS.index("o"), slice(mc * P, (mc + 1) * P)
                                for kc in range(KC):
                                    last = product(nc, bank[:, 0:size], (w_hi[:, wn, kc, at], w_lo[:, wn, kc, at]),
                                                   (mixed_hi[s][:, kc, first:first + size], mixed_lo[s][:, kc, first:first + size]),
                                                   kc == 0, kc == KC - 1)
                                last.then_inc(pj_full, 1)


def stage_flat_experts(nc, m, d):
    WN = KC * D
    NS = 2 * NG
    DEPTH = 2
    with ExitStack() as ctx:
        sb, ps, sem = open_stage(nc, ctx, "ffn1")
        two = range(2)
        raw = [sb(f"f_raw{s}", [P, KC, D]) for s in two]
        w_hi = [sb(f"f_hi{s}", [P, KC, D], F32R) for s in two]
        w_lo = [sb(f"f_lo{s}", [P, KC, D], F32R) for s in two]
        bias = sb("f_bias", [P, E, KC])
        cw = [sb(f"f_cw{s}", [P, NT]) for s in two]
        part = [sb(f"f_part{i}", [P, KC, G]) for i in range(2)]
        ob = [ps(f"f_ob{i}", [P, BANK]) for i in range(DEPTH * KC)]
        raw_loaded = [sem(f"f_raw_loaded{s}") for s in two]
        cw_loaded = [sem(f"f_cw_loaded{s}") for s in two]
        bias_loaded = sem("f_bias_loaded")
        rounded = [sem(f"f_rounded{s}") for s in two]
        split = [sem(f"f_split{s}") for s in two]
        out_full = sem("f_out_full")
        weighted = sem("f_weighted")
        summed = sem("f_summed")

        def reached(i, per, k):
            return (i + 1) * NS * per + (k + 1) * per

        with nc.Block() as block:
            @block.sync
            def _(sp):
                sp.dma_start(bias[:], d["L1_ffn_expert_b"].rearrange("e (c p) -> p e c", p=P)).then_inc(bias_loaded, 16)
                with sp.Fori(0, E // 2) as i:
                    for s in two:
                        e = i * 2 + s
                        sp.wait_ge(split[s], i)
                        sp.dma_start(raw[s][:], d["L1_ffn_expert_w"][ds(e, 1)].rearrange("o (k p) n -> p (o k) n", p=P)).then_inc(raw_loaded[s], 16)
                        sp.wait_ge(weighted, reached(i, 2, s * NG + NG - 1 - NS))
                        sp.dma_start(cw[s][:], m.cw_dram[ds(e, 1)].rearrange("o n -> (o n)").partition_broadcast(P)).then_inc(cw_loaded[s], 16)

            @block.scalar
            def _(act):
                def round_weights(i, s):
                    act.wait_ge(raw_loaded[s], i * 16 + 16)
                    act.wait_ge(out_full, reached(i, 1, s * NG + NG - 1 - NS))
                    nc.scalar.activation(w_hi[s][:], raw[s][:], ACT.Copy).then_inc(rounded[s], 1)

                with act.Fori(0, E // 2) as i:
                    for s in two:
                        round_weights(i, s)

            @block.gpsimd
            def _(pool):
                pool.sem_inc(summed, NS)

                def low_part(i, s):
                    pool.wait_ge(rounded[s], i + 1)
                    nc.gpsimd.tensor_tensor(w_lo[s][:], raw[s][:], w_hi[s][:].bitcast(F32), ALU.subtract).then_inc(split[s], 1)

                def step(i, more):
                    for k in range(NS):
                        at = slice(k % NG * G, (k % NG + 1) * G)
                        pool.wait_ge(weighted, reached(i, 2, k))
                        pool.wait_ge(summed, reached(i, 1, k - NG))
                        nc.gpsimd.tensor_tensor(m.h[:, :, at], m.h[:, :, at], part[k % 2][:], ALU.add).then_inc(summed, 1)
                        if k == 0:
                            low_part(i, 1)
                        if k == NG and more:
                            low_part(i + 1, 0)

                low_part(0, 0)
                with pool.Fori(0, E // 2 - 1) as i:
                    step(i, True)
                step(E // 2 - 1, False)

            @block.vector
            def _(dve):
                dve.sem_inc(weighted, NS * 2)
                dve.wait_ge(bias_loaded, 16)
                with dve.Fori(0, E // 2) as i:
                    for k in range(NS):
                        s, g = divmod(k, NG)
                        if g == 0:
                            dve.wait_ge(cw_loaded[s], i * 16 + 16)
                        dve.wait_ge(out_full, reached(i, 1, k))
                        dve.wait_ge(summed, reached(i, 1, k - 2))
                        for kc in range(KC):
                            nc.vector.scalar_tensor_tensor(part[k % 2][:, kc], ob[k % DEPTH * KC + kc][:, 0:G],
                                                           bias[:, ds(i * 2 + s, 1), kc],
                                                           cw[s][:, g * G:(g + 1) * G], ALU.add, ALU.mult).then_inc(weighted, 1)

            @block.tensor
            def _(pe):
                pe.sem_inc(out_full, NS)
                with pe.Fori(0, E // 2) as i:
                    for k in range(NS):
                        s, g = divmod(k, NG)
                        if g == 0:
                            pe.wait_ge(split[s], i + 1)
                        pe.wait_ge(weighted, reached(i, 2, k - DEPTH))
                        for kc in range(KC):
                            for c in range(KC):
                                x = [t[:, c, g * G:(g + 1) * G] for t in (m.x_hi, m.x_lo)]
                                at = slice(kc * P, (kc + 1) * P)
                                last = product(nc, ob[k % DEPTH * KC + kc][:, 0:G], (w_hi[s][:, c, at], w_lo[s][:, c, at]), x, c == 0, c == KC - 1)
                        last.then_inc(out_full, 1)


def stage_out(nc, m, d):
    with ExitStack() as ctx:
        sb, ps, sem = open_stage(nc, ctx, "out")
        held = sb("held", [P, 2, KC, SP])
        rows = sb("rows", [CH, 2, NCH, D])
        turned = [ps(f"turned{i}", [P, BANK]) for i in range(NCH)]
        held_ready = [sem(f"held_ready{s}") for s in range(2)]
        turned_ready = sem("turned_ready")
        rows_ready = [sem(f"rows_ready{s}") for s in range(2)]
        stored = [sem(f"stored{s}") for s in range(2)]
        with nc.Block() as block:
            @block.scalar
            def _(act):
                act.sem_inc(rows_ready[0], 5)
                act.sem_inc(rows_ready[1], 5)
                with act.Fori(0, 2) as i:
                    for s in range(2):
                        act.wait_ge(rows_ready[s], i * 5 + 5)
                        nc.scalar.activation(held[:, s], m.h[:, :, ds((i * 2 + s) * SP, SP)], ACT.Copy).then_inc(held_ready[s], 1)
                    for s in range(2):
                        for c in range(NCH):
                            act.wait_ge(turned_ready, i * 10 + s * 5 + c + 1)
                            if c == 0:
                                act.wait_ge(stored[s], i * 32)
                            nc.scalar.activation(rows[:, s, c], turned[c][0:CH, 0:D], ACT.Copy).then_inc(rows_ready[s], 1)

            @block.tensor
            def _(pe):
                with pe.Fori(0, 2) as i:
                    for s in range(2):
                        pe.wait_ge(held_ready[s], i + 1)
                        for c in range(NCH):
                            pe.wait_ge(rows_ready[1 - s], i * 5 + (5 * s) + c + 1)
                            for kc in range(KC):
                                last = nc.tensor.transpose(turned[c][0:CH, kc * P:(kc + 1) * P],
                                                           held[:, s, kc, c * CH:(c + 1) * CH], m.ident[:])
                            last.then_inc(turned_ready, 1)

            @block.sync
            def _(sp):
                with sp.Fori(0, 2) as i:
                    for s in range(2):
                        sp.wait_ge(rows_ready[s], i * 5 + 10)
                        b = i * 2 + s
                        full = NCH - 1
                        sp.dma_start(d["out"][ds(b, 1), 0:full * CH].rearrange("o (c p) n -> p (o c) n", p=CH),
                                     rows[:, s, 0:full]).then_inc(stored[s], 16)
                        sp.dma_start(d["out"][ds(b, 1), full * CH:S].rearrange("o p n -> p (o n)"),
                                     rows[0:S - full * CH, s, full]).then_inc(stored[s], 16)
                for s in range(2):
                    sp.wait_ge(stored[s], 2 * 32)


class Held:

    def __init__(self, nc, ctx):
        def sb(name, shape, dt=F32):
            return ctx.enter_context(nc.sbuf_tensor(name, shape, dt))

        self.h = sb("h", [P, KC, NT])
        self.x_hi = sb("x_hi", [P, KC, NT], F32R)
        self.x_lo = sb("x_lo", [P, KC, NT], F32R)
        self.ident = sb("ident", [P, P])
        self.mean_w = sb("mean_w", [P, P])
        self.eps = sb("eps", [P, 1])
        self.one = sb("one", [P, 1])
        self.causal = sb("causal", [CH, CH])
        self.decay_sum = sb("decay_sum", [CH, HEADS, B * NCH])
        self.decay_rows_dram = nc.dram_tensor("decay_rows_dram", (HEADS, NT), F32, kind="Internal").ap()
        self.cw_dram = nc.dram_tensor("cw_dram", (E, NT), F32, kind="Internal").ap()


def build(nc, d, upto=99):
    with ExitStack() as ctx:
        m = Held(nc, ctx)
        ctx.enter_context(nc.allow_non_contiguous_dma(reason="vectors of a few hundred elements"))
        stage_tokens(nc, m, d)
        if upto >= 1:
            stage_norm(nc, m, "norm0")
            stage_decay(nc, m, d)
            stage_gla(nc, m, d)
        if upto >= 2:
            stage_norm(nc, m, "norm1")
            stage_gate(nc, m, d, "gate0", d["L0_ffn_gate_W"], None, True)
            stage_hidden_experts(nc, m, d)
        if upto >= 3:
            stage_norm(nc, m, "norm2")
            stage_linear_attention(nc, m, d)
        if upto >= 4:
            stage_norm(nc, m, "norm3")
            stage_gate(nc, m, d, "gate1", d["L1_ffn_gate_w"], d["L1_ffn_gate_b"], False)
            stage_flat_experts(nc, m, d)
        stage_out(nc, m, d)


_ARGS = ['txt', 'L0_tok_cls_token', 'L0_tok_cls_pos_embedding', 'L0_tok_ln1_g', 'L0_tok_ln1_b', 'L0_tok_W',
         'L0_tok_bias', 'L0_tok_ln2_g', 'L0_tok_ln2_b', 'L0_attn_Wq', 'L0_attn_Wk', 'L0_attn_Wv', 'L0_attn_Wo',
         'L0_attn_Wg', 'L0_attn_bg', 'L0_attn_Wog', 'L0_ffn_gate_W', 'L0_ffn_W1', 'L0_ffn_b1', 'L0_ffn_W2', 'L0_ffn_b2',
         'L1_attn_Wq', 'L1_attn_bq', 'L1_attn_Wk', 'L1_attn_bk', 'L1_attn_Wv', 'L1_attn_bv', 'L1_attn_Wg', 'L1_attn_bg',
         'L1_attn_Wo', 'L1_attn_bo', 'L1_ffn_gate_w', 'L1_ffn_gate_b', 'L1_ffn_expert_w', 'L1_ffn_expert_b']


def position_table():
    omega = 1.0 / 10000.0 ** (np.arange(D // 4, dtype=np.float32) / np.float32(D // 4 - 1))
    omega = omega.astype(np.float32)
    y, x = np.meshgrid(np.arange(HP), np.arange(HP), indexing="ij")
    y = y.reshape(-1)[:, None].astype(np.float32) * omega[None]
    x = x.reshape(-1)[:, None].astype(np.float32) * omega[None]
    table = np.concatenate((np.sin(x), np.cos(x), np.sin(y), np.cos(y)), axis=1).astype(np.float32)
    return np.ascontiguousarray(table.T.reshape(KC, P, NPATCH).transpose(1, 0, 2))


def patch_rows(x):
    x = x.reshape(B, COLORS, HP, PATCH, HP, PATCH).transpose(0, 2, 4, 3, 5, 1)
    return np.ascontiguousarray(x.reshape(B * NPATCH, PATCH * PATCH * COLORS))


def make(nc, shapes, upto=99):
    d = {name: nc.dram_tensor(f"in_{name}", shape, F32, kind="ExternalInput").ap() for name, shape in shapes.items()}
    d["out"] = nc.dram_tensor("out_0", (B, S, D), F32, kind="ExternalOutput").ap()
    build(nc, d, upto)


def kernel(**inputs):
    import concourse.bacc as bacc
    from concourse.bass_utils import run_bass_kernel_spmd

    nc = bacc.Bacc("TRN2", target_bir_lowering=False, num_devices=1)
    arrays = {name: np.ascontiguousarray(inputs[name]) for name in _ARGS}
    arrays["pos"] = position_table()
    arrays["patches"] = patch_rows(np.asarray(inputs["x"]))
    make(nc, {n: a.shape for n, a in arrays.items()})
    r = run_bass_kernel_spmd(nc, [{f"in_{n}": a for n, a in arrays.items()}], core_ids=[0])
    return r.results[0]["out_0"]
```

```python
from contextlib import ExitStack

import concourse.bass as bass
import numpy as np
from concourse import mybir

F32 = mybir.dt.float32
F32R = mybir.dt.float32r
ALU = mybir.AluOpType
ACT = mybir.ActivationFunctionType
AX_X = mybir.AxisListType.X
ds = bass.ds

P = 128
B = 4
D = 256
KC = D // P
IMG, PATCH, COLORS = 96, 16, 3
HP = IMG // PATCH
NPATCH = HP * HP
TXT = 512
S = 1 + NPATCH + TXT
CH = 110
NCH = 5
SP = CH * NCH
NT = B * SP
G = 4 * CH
NG = NT // G
PIECES = ((0, 276), (276, SP - 276))
HEADS, DK, DV = 8, 128, 64
PAIRS = HEADS // 2
E = 8
HID = 512
EPS = 1e-5
BANK = 512
FAR = -1e30


def open_stage(nc, ctx, stage):
    def sb(name, shape, dt=F32):
        return ctx.enter_context(nc.sbuf_tensor(f"{stage}_{name}", shape, dt))

    def ps(name, shape):
        return ctx.enter_context(nc.psum_tensor(f"{stage}_{name}", shape, F32))

    sems = []

    def sem(name):
        sems.append(nc.alloc_semaphore(f"{stage}_{name}"))
        return sems[-1]

    def close():
        nc.clear_and_free_semaphores(sems)
        nc.all_engine_barrier()

    ctx.callback(close)
    return sb, ps, sem


def product(nc, out, w, x, first, last):
    (w_hi, w_lo), (x_hi, x_lo) = w, x
    nc.tensor.matmul(out, w_lo, x_hi, start=first, stop=False)
    nc.tensor.matmul(out, w_hi, x_lo, start=False, stop=False)
    return nc.tensor.matmul(out, w_hi, x_hi, start=False, stop=last)


def spread(ap, axis, n):
    wide = ap.unsqueeze(axis)
    shape = list(wide.shape)
    shape[axis] = n
    return wide.broadcast_to(shape)


def stage_tokens(nc, m, d):
    TB = 2
    TP = TB * NPATCH
    PD = COLORS * PATCH * PATCH
    PC = PD // P
    with ExitStack() as ctx:
        sb, ps, sem = open_stage(nc, ctx, "tok")
        img = sb("img", [TP, 2, PD])
        w = sb("w_patch", [P, PC, D])
        g1 = sb("g1", [P, PC])
        b1 = sb("b1", [P, PC])
        g2 = sb("g2", [P, KC])
        pos = sb("pos", [P, KC, NPATCH])
        b2 = sb("b2", [P, KC])
        posb = sb("posb", [P, KC, NPATCH])
        cls = sb("cls", [P, KC])
        cpos = sb("cpos", [P, KC])
        bias = sb("bias", [TP, D])
        txt = sb("txt", [P, B, TXT // P, D])
        stats = sb("stats", [TP, 2, 2, 6])
        mv = sb("mv", [TP, 2, 2])
        root = sb("root", [TP, 2])
        rstd = sb("rstd", [TP, 2])
        xg = sb("xg", [P, PC, TP])
        xt = sb("xt", [P, 2, PC, TP])
        emb = sb("emb", [TP, 2, D])
        embn = sb("embn", [TP, 2, D])
        stats2 = sb("stats2", [TP, 2, 6])
        mv2 = sb("mv2", [TP, 2, 2])
        root2 = sb("root2", [TP, 2])
        rstd2 = sb("rstd2", [TP, 2])
        pt = [ps(f"pt{i}", [P, BANK]) for i in range(4)]
        px = [ps(f"px{i}", [P, BANK]) for i in range(2)]
        pe_ = [ps(f"pe{i}", [P, BANK]) for i in range(2)]

        img_loaded = [sem(f"img_loaded{t}") for t in range(2)]
        txt_loaded = [sem(f"txt_loaded{b}") for b in range(B)]
        w_loaded = sem("w_loaded")
        patch_params_loaded = sem("patch_params_loaded")
        small_loaded = sem("small_loaded")
        consts = sem("consts")
        ident_zero = sem("ident_zero")
        ident_ready = sem("ident_ready")
        txt_turned = sem("txt_turned")
        txt_kept = sem("txt_kept")
        chain = sem("dve_chain")
        stats_ready = sem("stats_ready")
        eps_ready = sem("eps_ready")
        root_ready = sem("root_ready")
        normed = sem("normed")
        patches_turned = sem("patches_turned")
        xt_ready = sem("xt_ready")
        embedded = sem("embedded")
        emb_normed = sem("emb_normed")
        emb_turned = sem("emb_turned")

        hv = m.h[:, :, :].rearrange("p k (b s) -> p k b s", b=B)

        with nc.Block() as block:
            @block.sync
            def _(sp):
                by_feature = "(k p) -> p k"
                for t in range(2):
                    sp.dma_start(img[:, t], d["patches"][t * TP:(t + 1) * TP]).then_inc(img_loaded[t], 16)
                sp.dma_start(g1[:], d["L0_tok_ln1_g"].rearrange(by_feature, p=P)).then_inc(patch_params_loaded, 16)
                sp.dma_start(b1[:], d["L0_tok_ln1_b"].rearrange(by_feature, p=P)).then_inc(patch_params_loaded, 16)

            @block.gpsimd
            def _(pool):
                nc.gpsimd.memset(m.eps[:], EPS).then_inc(eps_ready, 1)
                for b in range(B):
                    pool.dma_start(txt[:, b], d["txt"][b].rearrange("(j p) d -> p j d", p=P)).then_inc(txt_loaded[b], 16)
                nc.gpsimd.memset(m.ident[:], 0.0).then_inc(ident_zero, 1)
                pool.wait_ge(ident_zero, 1)
                nc.gpsimd.affine_select(out=m.ident[:], in_=m.ident[:], compare_op=ALU.not_equal, fill=1.0, base=0,
                                        pattern=[[-1, P]], channel_multiplier=1).then_inc(ident_ready, 1)
                nc.gpsimd.memset(m.causal[:], 0.0).then_inc(ident_zero, 1)
                pool.wait_ge(ident_zero, 2)
                nc.gpsimd.affine_select(out=m.causal[:], in_=m.causal[:], compare_op=ALU.is_ge, fill=FAR, base=0,
                                        pattern=[[1, CH]], channel_multiplier=-1).then_inc(ident_ready, 1)
                pool.wait_ge(ident_ready, 2)
                nc.gpsimd.memset(m.mean_w[:], 1.0 / D)
                nc.gpsimd.memset(m.one[:], 1.0).then_inc(consts, 1)
                for kc in range(KC):
                    last = nc.gpsimd.memset(hv[:, kc, :, S:SP], 0.0)
                last.then_inc(consts, 1)
                pool.wait_ge(small_loaded, 16 * 6)
                for kc in range(KC):
                    last = nc.gpsimd.tensor_tensor(hv[:, kc, :, 0], cls[:, kc:kc + 1].broadcast_to([P, B]),
                                                   cpos[:, kc:kc + 1].broadcast_to([P, B]), ALU.add)
                last.then_inc(consts, 1)
                pool.wait_ge(consts, 3)

            @block.scalar
            def _(act):
                by_feature = "(k p) -> p k"
                act.dma_start(w[:], d["L0_tok_W"].rearrange("(k p) n -> p k n", p=P)).then_inc(w_loaded, 16)
                act.dma_start(bias[:], d["L0_tok_bias"].partition_broadcast(TP)).then_inc(small_loaded, 16)
                act.dma_start(g2[:], d["L0_tok_ln2_g"].rearrange(by_feature, p=P)).then_inc(small_loaded, 16)
                act.dma_start(b2[:], d["L0_tok_ln2_b"].rearrange(by_feature, p=P)).then_inc(small_loaded, 16)
                act.dma_start(pos[:], d["pos"]).then_inc(small_loaded, 16)
                act.dma_start(cls[:], d["L0_tok_cls_token"][0, 0].rearrange(by_feature, p=P)).then_inc(small_loaded, 16)
                act.dma_start(cpos[:], d["L0_tok_cls_pos_embedding"][0, 0].rearrange(by_feature, p=P)).then_inc(small_loaded, 16)
                def root_of(t, out, source, count):
                    act.wait_ge(stats_ready, count)
                    nc.scalar.activation(out[:, t:t + 1], source[:, t, 1:2], ACT.Sqrt, bias=m.eps[0:TP]).then_inc(root_ready, 1)

                act.wait_ge(eps_ready, 1)
                root_of(0, root, mv, 1)
                for n in range(B * KC):
                    if n == 1:
                        root_of(1, root, mv, 2)
                    b, kc = divmod(n, KC)
                    act.wait_ge(txt_turned, n + 1)
                    nc.scalar.activation(m.h[:, kc, b * SP + 1 + NPATCH:b * SP + S], pt[n % 4][:], ACT.Copy).then_inc(txt_kept, 1)
                for t in range(2):
                    root_of(t, root2, mv2, t + 3)

            @block.vector
            def _(dve):
                made = [0]

                def link(ins):
                    made[0] += 1
                    ins.then_inc(chain, 1)
                    dve.wait_ge(chain, made[0])

                for t in range(2):
                    dve.wait_ge(img_loaded[t], 16)
                    for i in range(2):
                        last = nc.vector.bn_stats(stats[:, t, i], img[:, t, i * (PD // 2):(i + 1) * (PD // 2)])
                    link(last)
                    nc.vector.bn_aggr(mv[:, t], stats[:, t].rearrange("p a b -> p (a b)")).then_inc(stats_ready, 1)
                for t in range(2):
                    dve.wait_ge(root_ready, t + 1)
                    link(nc.vector.reciprocal(rstd[:, t:t + 1], root[:, t:t + 1]))
                    nc.vector.tensor_scalar(img[:, t], img[:, t], mv[:, t, 0:1], rstd[:, t:t + 1],
                                            ALU.subtract, ALU.mult).then_inc(normed, 1)
                dve.wait_ge(patch_params_loaded, 32)
                for t in range(2):
                    dve.wait_ge(patches_turned, t + 1)
                    link(nc.vector.tensor_tensor(xg[:], px[t][:, 0:PC * TP].rearrange("p (k n) -> p k n", k=PC),
                                                 spread(g1[:], 2, TP), ALU.mult))
                    nc.vector.tensor_tensor(xt[:, t], xg[:], spread(b1[:], 2, TP),
                                            ALU.add).then_inc(xt_ready, 1)
                    dve.wait_ge(xt_ready, t + 1)
                dve.wait_ge(small_loaded, 16 * 6)
                link(nc.vector.tensor_tensor(posb[:], pos[:], spread(b2[:], 2, NPATCH), ALU.add))
                for t in range(2):
                    dve.wait_ge(embedded, t + 1)
                    link(nc.vector.tensor_tensor(emb[:, t], pe_[t][0:TP, 0:D], bias[:], ALU.add))
                    link(nc.vector.bn_stats(stats2[:, t], emb[:, t]))
                    nc.vector.bn_aggr(mv2[:, t], stats2[:, t]).then_inc(stats_ready, 1)
                for t in range(2):
                    dve.wait_ge(root_ready, t + 3)
                    link(nc.vector.reciprocal(rstd2[:, t:t + 1], root2[:, t:t + 1]))
                    nc.vector.tensor_scalar(embn[:, t], emb[:, t], mv2[:, t, 0:1], rstd2[:, t:t + 1],
                                            ALU.subtract, ALU.mult).then_inc(emb_normed, 1)
                for t in range(2):
                    dve.wait_ge(emb_turned, t + 1)
                    for kc in range(KC):
                        nc.vector.scalar_tensor_tensor(
                            hv[:, kc, t * TB:(t + 1) * TB, 1:1 + NPATCH],
                            px[t][:, kc * TP:(kc + 1) * TP].rearrange("p (b s) -> p b s", b=TB), g2[:, kc:kc + 1],
                            spread(posb[:, kc], 1, TB), ALU.mult, ALU.add)

            @block.tensor
            def _(pe):
                pe.wait_ge(ident_ready, 1)

                def turn_text(n):
                    b, kc = divmod(n, KC)
                    if kc == 0:
                        pe.wait_ge(txt_loaded[b], 16)
                    if n >= 4:
                        pe.wait_ge(txt_kept, n - 3)
                    for j in range(TXT // P):
                        last = nc.tensor.transpose(pt[n % 4][:, j * P:(j + 1) * P], txt[:, b, j, kc * P:(kc + 1) * P], m.ident[:])
                    last.then_inc(txt_turned, 1)

                def turn_patches(t):
                    pe.wait_ge(normed, t + 1)
                    for k in range(PC):
                        last = nc.tensor.transpose(px[t][:, k * TP:(k + 1) * TP], img[:, t, k * P:(k + 1) * P], m.ident[0:TP, 0:TP])
                    last.then_inc(patches_turned, 1)

                def embed(t):
                    pe.wait_ge(xt_ready, t + 1)
                    for k in range(PC):
                        last = nc.tensor.matmul(pe_[t][0:TP, 0:D], xt[:, t, k], w[:, k],
                                                start=(k == 0), stop=(k == PC - 1))
                    last.then_inc(embedded, 1)

                turn_text(0)
                turn_text(1)
                turn_patches(0)
                turn_text(2)
                turn_patches(1)
                turn_text(3)
                turn_text(4)
                pe.wait_ge(w_loaded, 16)
                embed(0)
                turn_text(5)
                embed(1)
                turn_text(6)
                turn_text(7)
                for t in range(2):
                    pe.wait_ge(emb_normed, t + 1)
                    for kc in range(KC):
                        last = nc.tensor.transpose(px[t][:, kc * TP:(kc + 1) * TP], embn[:, t, kc * P:(kc + 1) * P], m.ident[0:TP, 0:TP])
                    last.then_inc(emb_turned, 1)


def after(eng, sem, value):
    if not isinstance(value, int) or value > 0:
        eng.wait_ge(sem, value)


class Norm:
    PAIR_BY_VECTOR = (0, 1)
    HIGH_BY_VECTOR = (0, 1)
    LOW_BY_VECTOR = (0, 1, 2, 3)

    def __init__(self, nc, m, sem, y, pair, sq, banks):
        self.nc, self.m, self.y, self.pair, self.rstd, self.banks = nc, m, y, pair, pair, banks
        self.sq = [t.rearrange("p (k g) -> p k g", k=KC) for t in sq]
        self.pair_by_vector = sem("norm_pair_by_vector")
        self.pair_by_pool = sem("norm_pair_by_pool")
        self.mean_ready = sem("norm_mean_ready")
        self.dev_ready = sem("norm_dev_ready")
        self.sq_ready = sem("norm_sq_ready")
        self.sum_ready = sem("norm_sum_ready")
        self.var_ready = sem("norm_var_ready")
        self.logv_ready = sem("norm_logv_ready")
        self.rstd_ready = sem("norm_rstd_ready")
        self.y_ready = sem("norm_y_ready")
        self.hi_by_vector = sem("norm_hi_by_vector")
        self.hi_by_scalar = sem("norm_hi_by_scalar")
        self.lo_by_vector = sem("norm_lo_by_vector")
        self.lo_by_pool = sem("norm_lo_by_pool")

    def bank(self, i):
        return self.banks[i % len(self.banks)]

    def add_pair_by_vector(self, i):
        at = slice(i * G, (i + 1) * G)
        self.nc.vector.tensor_tensor(self.pair[:, at], self.m.h[:, 0, at], self.m.h[:, 1, at], ALU.add).then_inc(self.pair_by_vector, 1)

    def add_pair_by_pool(self, i):
        at = slice(i * G, (i + 1) * G)
        self.nc.gpsimd.tensor_tensor(self.pair[:, at], self.m.h[:, 0, at], self.m.h[:, 1, at], ALU.add).then_inc(self.pair_by_pool, 1)

    def mean(self, pe, i):
        if i in self.PAIR_BY_VECTOR:
            pe.wait_ge(self.pair_by_vector, i + 1)
        else:
            pe.wait_ge(self.pair_by_pool, i + 1 - len(self.PAIR_BY_VECTOR))
        if i >= len(self.banks):
            pe.wait_ge(self.logv_ready, i - len(self.banks) + 1)
        self.nc.tensor.matmul(self.bank(i)[:, 0:G], self.m.mean_w[:], self.pair[:, i * G:(i + 1) * G],
                              start=True, stop=True).then_inc(self.mean_ready, 1)

    def deviation(self, dve, i):
        at = slice(i * G, (i + 1) * G)
        dve.wait_ge(self.mean_ready, i + 1)
        self.nc.vector.tensor_tensor(self.y[:, :, at], self.m.h[:, :, at], spread(self.bank(i)[:, 0:G], 1, KC),
                                     ALU.subtract).then_inc(self.dev_ready, 1)

    def square(self, act, i):
        at = slice(i * G, (i + 1) * G)
        act.wait_ge(self.dev_ready, i + 1)
        if i >= len(self.sq):
            act.wait_ge(self.sum_ready, i - len(self.sq) + 1)
        self.nc.scalar.activation(self.sq[i % len(self.sq)], self.y[:, :, at], ACT.Square).then_inc(self.sq_ready, 1)

    def add_squares(self, pool, i):
        at = slice(i * G, (i + 1) * G)
        pool.wait_ge(self.sq_ready, i + 1)
        pool.wait_ge(self.mean_ready, i + 1)
        sq = self.sq[i % len(self.sq)]
        self.nc.gpsimd.tensor_tensor(self.pair[:, at], sq[:, 0], sq[:, 1], ALU.add).then_inc(self.sum_ready, 1)

    def variance(self, pe, i):
        pe.wait_ge(self.sum_ready, i + 1)
        pe.wait_ge(self.dev_ready, i + 1)
        self.nc.tensor.matmul(self.bank(i)[:, 0:G], self.m.mean_w[:], self.pair[:, i * G:(i + 1) * G],
                              start=True, stop=True).then_inc(self.var_ready, 1)

    def reciprocal_deviation(self, act, groups):
        for i in groups:
            act.wait_ge(self.var_ready, i + 1)
            self.nc.scalar.activation(self.rstd[:, i * G:(i + 1) * G], self.bank(i)[:, 0:G], ACT.Ln,
                                      bias=self.m.eps[:]).then_inc(self.logv_ready, 1)
        for i in groups:
            at = slice(i * G, (i + 1) * G)
            act.wait_ge(self.logv_ready, i + 1)
            self.nc.scalar.activation(self.rstd[:, at], self.rstd[:, at], ACT.Exp, scale=-0.5).then_inc(self.rstd_ready, 1)

    def scale(self, dve, i):
        at = slice(i * G, (i + 1) * G)
        dve.wait_ge(self.rstd_ready, i + 1)
        self.nc.vector.tensor_tensor(self.y[:, :, at], self.y[:, :, at], spread(self.rstd[:, at], 1, KC),
                                     ALU.mult).then_inc(self.y_ready, 1)

    def high_part_by_scalar(self, act, i):
        at = slice(i * G, (i + 1) * G)
        act.wait_ge(self.y_ready, i + 1)
        self.nc.scalar.activation(self.m.x_hi[:, :, at], self.y[:, :, at], ACT.Copy).then_inc(self.hi_by_scalar, 1)

    def high_part_by_vector(self, dve, i):
        at = slice(i * G, (i + 1) * G)
        dve.wait_ge(self.y_ready, i + 1)
        self.nc.vector.tensor_copy(self.m.x_hi[:, :, at], self.y[:, :, at]).then_inc(self.hi_by_vector, 1)

    def high_part_ready(self, eng, i):
        if i in self.HIGH_BY_VECTOR:
            eng.wait_ge(self.hi_by_vector, i + 1)
        else:
            eng.wait_ge(self.hi_by_scalar, i + 1 - len(self.HIGH_BY_VECTOR))

    def low_part_by_vector(self, dve, i):
        at = slice(i * G, (i + 1) * G)
        self.high_part_ready(dve, i)
        self.nc.vector.tensor_tensor(self.m.x_lo[:, :, at], self.y[:, :, at], self.m.x_hi[:, :, at].bitcast(F32),
                                     ALU.subtract).then_inc(self.lo_by_vector, 1)

    def low_part_by_pool(self, pool, i):
        at = slice(i * G, (i + 1) * G)
        self.high_part_ready(pool, i)
        self.nc.gpsimd.tensor_tensor(self.m.x_lo[:, :, at], self.y[:, :, at], self.m.x_hi[:, :, at].bitcast(F32),
                                     ALU.subtract).then_inc(self.lo_by_pool, 1)

    def x_ready(self, eng, i):
        if i in self.LOW_BY_VECTOR:
            eng.wait_ge(self.lo_by_vector, i + 1)
        else:
            eng.wait_ge(self.lo_by_pool, i + 1 - len(self.LOW_BY_VECTOR))


    def on_tensor(self, pe):
        for i in range(3):
            self.mean(pe, i)
        self.variance(pe, 0)
        self.mean(pe, 3)
        self.variance(pe, 1)
        self.mean(pe, 4)
        for i in range(2, NG):
            self.variance(pe, i)

    def on_vector(self, dve, prepare_weights=None):
        for i in self.PAIR_BY_VECTOR:
            self.add_pair_by_vector(i)
        for i in range(NG):
            self.deviation(dve, i)
        if prepare_weights is not None:
            prepare_weights(dve)
        for i in self.HIGH_BY_VECTOR:
            self.scale(dve, i)
            self.high_part_by_vector(dve, i)
            self.low_part_by_vector(dve, i)
        for i in range(2, NG):
            self.scale(dve, i)
        for i in self.LOW_BY_VECTOR[2:]:
            self.low_part_by_vector(dve, i)

    def on_scalar(self, act, round_weights):
        for i in range(3):
            self.square(act, i)
        self.reciprocal_deviation(act, (0, 1))
        for i in range(3, NG):
            self.square(act, i)
        round_weights()
        self.reciprocal_deviation(act, (2, 3, 4))
        for i in range(2, NG):
            self.high_part_by_scalar(act, i)

    def on_pool(self, pool, low_part_of_weights):
        for i in range(2, NG):
            self.add_pair_by_pool(i)
        for i in range(NG):
            self.add_squares(pool, i)
        low_part_of_weights()
        for i in range(len(self.LOW_BY_VECTOR), NG):
            self.low_part_by_pool(pool, i)


class Decay:

    def __init__(self, nc, m, sb, sem, z, mag, rows, same):
        self.nc, self.m = nc, m
        self.w = sb("wg", [P, KC, HEADS])
        self.w_hi = sb("wg_hi", [P, KC, P], F32R)
        self.w_lo = sb("wg_lo", [P, KC, P], F32R)
        self.bias = sb("bg", [HEADS, 1])
        self.z, self.mag, self.rows, self.same = z, mag, rows, same
        self.loaded = sem("wg_loaded")
        self.w_ready = sem("wg_ready")
        self.z_ready = sem("z_ready")
        self.logits_ready = sem("z_logits_ready")
        self.chain = sem("decay_chain")
        self.neg_ready = sem("neg_ready")
        self.mag_ready = sem("mag_ready")
        self.rows_ready = sem("decay_rows_ready")
        self.turned_ready = sem("rows_turned_ready")
        self.sum_ready = sem("decay_sum_ready")
        self.stored = sem("decay_stored")
        self.mask_ready = sem("same_chunk_ready")

    def load(self, sp, weights, bias):
        sp.dma_start(self.w[:], weights.rearrange("(k p) n -> p k n", p=P)).then_inc(self.loaded, 16)
        sp.dma_start(self.bias[:], bias.rearrange("(n o) -> n o", o=1)).then_inc(self.loaded, 16)

    def store(self, sp):
        sp.wait_ge(self.rows_ready, 1)
        sp.dma_start(self.m.decay_rows_dram, self.rows).then_inc(self.stored, 16)
        sp.wait_ge(self.stored, 16)

    def mask(self, pool):
        self.nc.gpsimd.memset(self.same, 1.0).then_inc(self.mask_ready, 1)
        pool.wait_ge(self.mask_ready, 1)
        self.nc.gpsimd.memset(self.same.rearrange("h (c t) -> h c t", t=CH)[:, :, 0:1], 0.0).then_inc(self.mask_ready, 1)

    def prepare_weights(self, dve):
        nc = self.nc
        nc.vector.memset(self.w_hi[:].bitcast(F32), 0.0).then_inc(self.chain, 1)
        nc.vector.memset(self.w_lo[:].bitcast(F32), 0.0).then_inc(self.chain, 1)
        dve.wait_ge(self.loaded, 32)
        dve.wait_ge(self.chain, 2)
        nc.vector.tensor_copy(self.w_hi[:, :, 0:HEADS], self.w[:]).then_inc(self.chain, 1)
        dve.wait_ge(self.chain, 3)
        nc.vector.tensor_tensor(self.w_lo[:, :, 0:HEADS], self.w[:], self.w_hi[:, :, 0:HEADS].bitcast(F32),
                                ALU.subtract).then_inc(self.w_ready, 1)
        nc.vector.tensor_scalar(self.bias[:], self.bias[:], 1.0 / 16.0, None, ALU.mult).then_inc(self.w_ready, 1)

    def logits(self, pe, i, bank):
        if i == 0:
            pe.wait_ge(self.w_ready, 1)
        at = slice(i * G, (i + 1) * G)
        for kc in range(KC):
            last = product(self.nc, bank[:, 0:G], (self.w_hi[:, kc], self.w_lo[:, kc]),
                           (self.m.x_hi[:, kc, at], self.m.x_lo[:, kc, at]), kc == 0, kc == KC - 1)
        last.then_inc(self.logits_ready, 1)

    def keep(self, act, i, bank):
        if i == 0:
            act.wait_ge(self.w_ready, 2)
        act.wait_ge(self.logits_ready, i + 1)
        self.nc.scalar.activation(self.z[:, i * G:(i + 1) * G], bank[0:HEADS, 0:G], ACT.Identity,
                                  bias=self.bias[:], scale=1.0 / 16.0).then_inc(self.z_ready, 1)

    def log_part(self, act, meanwhile):
        act.wait_ge(self.neg_ready, 1)
        self.nc.scalar.activation(self.mag, self.mag, ACT.Exp).then_inc(self.neg_ready, 1)
        meanwhile()
        act.wait_ge(self.neg_ready, 2)
        self.nc.scalar.activation(self.mag, self.mag, ACT.Ln, bias=self.m.one[0:HEADS]).then_inc(self.mag_ready, 1)

    def sum_up(self, dve, meanwhile):
        dve.wait_ge(self.z_ready, NG)
        self.nc.vector.scalar_tensor_tensor(self.mag, self.z, -1.0, self.z, ALU.mult, ALU.min).then_inc(self.neg_ready, 1)
        meanwhile()
        dve.wait_ge(self.mag_ready, 1)
        self.nc.vector.scalar_tensor_tensor(self.z, self.z, 0.0, self.mag, ALU.min, ALU.subtract).then_inc(self.chain, 1)
        dve.wait_ge(self.chain, 4)
        dve.wait_ge(self.mask_ready, 2)
        self.nc.vector.tensor_tensor_scan(self.rows, self.same, self.z, 0.0, ALU.mult, ALU.add).then_inc(self.rows_ready, 1)

    def turn(self, pe, bank):
        pe.wait_ge(self.rows_ready, 1)
        for c in range(B * NCH):
            last = self.nc.tensor.transpose(bank[0:CH, c * HEADS:(c + 1) * HEADS], self.rows[:, c * CH:(c + 1) * CH],
                                            self.m.ident[0:HEADS, 0:HEADS])
        last.then_inc(self.turned_ready, 1)

    def keep_sums(self, dve, bank):
        dve.wait_ge(self.turned_ready, 1)
        self.nc.vector.tensor_copy(self.m.decay_sum[:].rearrange("t h n -> t n h"),
                                   bank[0:CH, 0:B * NCH * HEADS].rearrange("t (n h) -> t n h", h=HEADS)).then_inc(self.sum_ready, 1)
        dve.wait_ge(self.sum_ready, 1)


def stage_gla(nc, m, d):
    NPC = len(PIECES)
    KINDS = ["k0", "k0", "k1", "k1", "v", "v", "q0", "q0", "q1", "q1", "g", "g"]
    WQ, WK, WV, WO, WW = 0, 2 * DK, 4 * DK, 4 * DK + 2 * DV, 4 * DK + 4 * DV
    GATES = (10, 11)
    PJ = [("in", s, j) for s in range(2) for j in range(GATES[0])] + [("in", s, j) for s in range(2) for j in GATES] + [("out", s, j) for s in range(2) for j in range(2 * NPC)]
    PJ_DVE = [u for u in PJ if u[0] == "out" or KINDS[u[2]] in ("v", "q1")]
    PJ_ACT = [u for u in PJ if u not in PJ_DVE]
    TS = [(s, n) for s in range(2) for n in ("score0", "score1", "score2", "key0", "key1", "value0", "value1")] + [(0, "state"), (1, "state")]
    TS_ACT = [u for u in TS if u[1].startswith("key")]
    TS_DVE = [u for u in TS if u not in TS_ACT]
    NPJ, NTS = 4, 2
    with ExitStack() as ctx:
        sb, ps, sem = open_stage(nc, ctx, "gla")
        w_raw = sb("w_raw", [P, KC, WW])
        w_hi = sb("w_hi", [P, KC, WW], F32R)
        w_lo = sb("w_lo", [P, KC, WW], F32R)
        wo_raw = sb("wo_raw", [P, D])
        wo_hi = sb("wo_hi", [P, D], F32R)
        wo_lo = sb("wo_lo", [P, D], F32R)
        two = range(2)
        key_t = [sb(f"key_t{s}", [P, 2, SP]) for s in two]
        query_t = [sb(f"query_t{s}", [P, 2, SP]) for s in two]
        query_dec_all = sb("query_dec", [P, 2, 2, SP])
        query_dec = [query_dec_all[:, s] for s in two]
        value_t = [sb(f"value_t{s}", [P, SP]) for s in two]
        sums_all = sb("sums", [P, 2, 2, NCH, CH])
        sums = [sums_all[:, s] for s in two]
        since_all = sb("since", [P, 2, 2, NCH, CH])
        since = [since_all[:, s] for s in two]
        decay_all = sb("decay", [CH, 2, 2, NCH, CH])
        decay = [decay_all[:, s] for s in two]
        probs_all = sb("probs", [CH, 2, 2, NCH, CH])
        probs = [probs_all[:, s] for s in two]
        key = [sb(f"key{s}", [CH, 2, NCH - 1, DK]) for s in two]
        value = [sb(f"value{s}", [CH, NCH, 2 * DV]) for s in two]
        value_dec = [sb(f"value_dec{s}", [CH, NCH - 1, 2, DV]) for s in two]
        state = [sb(f"state{s}", [P, NCH - 1, 2 * DV]) for s in two]
        gate_all = sb("gate", [P, 2, SP])
        gate = [gate_all[:, s] for s in two]
        mixed_all = sb("mixed", [P, 2, SP])
        mixed = [mixed_all[:, s] for s in two]
        mixed_hi = [sb(f"mixed_hi{s}", [P, SP], F32R) for s in two]
        mixed_lo = [sb(f"mixed_lo{s}", [P, SP], F32R) for s in two]
        pj = [ps(f"pj{i}", [P, BANK]) for i in range(NPJ)]
        ts = [ps(f"ts{i}", [P, BANK]) for i in range(NTS)]
        att = [ps(f"att{i}", [P, BANK]) for i in range(2)]

        y = sb("y", [P, KC, NT])
        norm = Norm(nc, m, sem, y, query_dec_all[:].rearrange("p s h c -> p (s h c)"),
                    [t[:].rearrange("p s c -> p (s c)")[:, 0:KC * G] for t in (gate_all, mixed_all)], ts + att)

        def decay_rows(t):
            return t[0:HEADS].rearrange("p s h c t -> p (s h c t)")

        decays = Decay(nc, m, sb, sem, decay_rows(probs_all), decay_rows(decay_all), decay_rows(since_all), decay_rows(sums_all))
        w_loaded = sem("w_loaded")
        w_rounded = sem("w_rounded")
        w_split = sem("w_split")
        wo_loaded = sem("wo_loaded")
        wo_rounded = sem("wo_rounded")
        wo_split = sem("wo_split")
        pj_full = sem("pj_full")
        pj_act = sem("pj_taken_by_act")
        pj_dve = sem("pj_taken_by_dve")
        ts_full = sem("ts_full")
        ts_act = sem("ts_taken_by_act")
        ts_dve = sem("ts_taken_by_dve")
        state_chain = sem("state_chain")
        sums_loaded = [sem(f"sums_loaded{s}") for s in two]
        diff_ready = [sem(f"diff_ready{s}") for s in two]
        decay_ready = [sem(f"decay_ready{s}") for s in two]
        since_ready = [sem(f"since_ready{s}") for s in two]
        query_dec_ready = [sem(f"query_dec_ready{s}") for s in two]
        value_dec_ready = [sem(f"value_dec_ready{s}") for s in two]
        att_full = [sem(f"att_full{s}") for s in two]
        mixed_ready = [sem(f"mixed_ready{s}") for s in two]
        hi_ready = [sem(f"mixed_hi_ready{s}") for s in two]
        lo_ready = [sem(f"mixed_lo_ready{s}") for s in two]

        def pj_taken(eng, i, use, before=False):
            users, s_ = (PJ_DVE, pj_dve) if use in PJ_DVE else (PJ_ACT, pj_act)
            eng.wait_ge(s_, (i + (0 if before else 1)) * len(users) + users.index(use) + 1)

        def ts_taken(eng, i, use, before=False):
            users, s_ = (TS_DVE, ts_dve) if use in TS_DVE else (TS_ACT, ts_act)
            eng.wait_ge(s_, (i + (0 if before else 1)) * len(users) + users.index(use) + 1)

        def cols(t, first, n):
            return t[:, ds(first, n)]

        with nc.Block() as block:
            @block.sync
            def _(sp):
                def load_weights(i, p):
                    after(sp, w_split, i)
                    for src, n, at in ((d["L0_attn_Wq"], 2 * DK, WQ), (d["L0_attn_Wk"], 2 * DK, WK),
                                       (d["L0_attn_Wv"], 2 * DV, WV), (d["L0_attn_Wog"], 2 * DV, WO)):
                        sp.dma_start(w_raw[:, :, at:at + n],
                                     src.rearrange("(k p) n -> p k n", p=P)[:, :, ds(p * n, n)]).then_inc(w_loaded, 16)
                    after(sp, wo_split, i)
                    sp.dma_start(wo_raw[:], d["L0_attn_Wo"][ds(p * P, P), :]).then_inc(wo_loaded, 16)

                def load_sums(i, j, p):
                    for s in two:
                        after(sp, diff_ready[s], i)
                        after(sp, since_ready[s], i)
                        sp.dma_start(sums[s].rearrange("q h c t -> q h (c t)"),
                                     m.decay_rows_dram[ds(p * 2, 2), ds((j * 2 + s) * SP, SP)].partition_broadcast(P)
                                     ).then_inc(sums_loaded[s], 16)

                load_weights(0, 0)
                decays.load(sp, d["L0_attn_Wg"], d["L0_attn_bg"])
                decays.store(sp)
                load_sums(0, 0, 0)
                with sp.Fori(1, PAIRS) as p:
                    load_weights(p, p)
                    load_sums(p, 0, p)
                with sp.Fori(0, PAIRS) as p:
                    load_weights(PAIRS + p, p)
                    load_sums(PAIRS + p, 1, p)

            @block.gpsimd
            def _(pool):
                def low_part(i):
                    pool.wait_ge(w_rounded, i + 1)
                    nc.gpsimd.tensor_tensor(w_lo[:], w_raw[:], w_hi[:].bitcast(F32), ALU.subtract).then_inc(w_split, 1)

                def step(i, more):
                    for s in two:
                        pj_taken(pool, i, ("in", s, 7))
                        pj_taken(pool, i, ("in", s, 9))
                        pool.wait_ge(since_ready[s], i + 1)
                        after(pool, att_full[s], i * 2)
                        nc.gpsimd.tensor_tensor(query_dec[s], query_t[s][:], since[s].rearrange("q h c t -> q h (c t)"),
                                                ALU.mult).then_inc(query_dec_ready[s], 1)
                    for s in two:
                        ts_taken(pool, i, (s, "value0"))
                        pool.wait_ge(decay_ready[s], i + 1)
                        nc.gpsimd.tensor_tensor(
                            value_dec[s][:], value[s][:, 0:NCH - 1].rearrange("t c (h v) -> t c h v", h=2),
                            spread(decay[s][:, :, 0:NCH - 1, CH - 1].rearrange("t h c -> t c h"), 3, DV),
                            ALU.mult).then_inc(value_dec_ready[s], 1)
                    pool.wait_ge(wo_rounded, i * 2 + 2)
                    nc.gpsimd.tensor_tensor(wo_lo[:], wo_raw[:], wo_hi[:].bitcast(F32), ALU.subtract).then_inc(wo_split, 1)
                    if more:
                        low_part(i + 1)

                norm.on_pool(pool, lambda: low_part(0))
                decays.mask(pool)
                step(0, True)
                with pool.Fori(1, 2 * PAIRS - 1) as i:
                    step(i, True)
                step(2 * PAIRS - 1, False)

            @block.scalar
            def _(act):
                act.sem_inc(pj_act, len(PJ_ACT))
                act.sem_inc(ts_act, len(TS_ACT))
                def round_weights(i):
                    act.wait_ge(w_loaded, i * 64 + 64)
                    after(act, pj_full, i * len(PJ) - 4 * NPC)
                    nc.scalar.activation(w_hi[:], w_raw[:], ACT.Copy).then_inc(w_rounded, 1)

                def since_start(i, s):
                    act.wait_ge(sums_loaded[s], i * 16 + 16)
                    after(act, query_dec_ready[s], i)
                    ts_taken(act, i, (s, "state"), before=True)
                    nc.scalar.activation(since[s], sums[s], ACT.Exp).then_inc(since_ready[s], 1)

                def keep_projections(i, s, pieces=range(GATES[0])):
                    for k in pieces:
                        kind = KINDS[k]
                        if kind in ("v", "q1"):
                            continue
                        first, n = PIECES[k % NPC]
                        act.wait_ge(pj_full, i * len(PJ) + PJ.index(("in", s, k)) + 1)
                        bank = pj[PJ.index(("in", s, k)) % NPJ][:, 0:n]
                        if kind[0] == "k":
                            out = nc.scalar.activation(key_t[s][:, int(kind[1]), first:first + n], bank, ACT.Copy, scale=DK ** -0.5)
                        elif kind[0] == "q":
                            out = nc.scalar.activation(query_t[s][:, int(kind[1]), first:first + n], bank, ACT.Copy)
                        else:
                            after(act, mixed_ready[s], i * 2)
                            out = nc.scalar.activation(gate[s][:, first:first + n], bank, ACT.Tanh, scale=0.5)
                        out.then_inc(pj_act, 1)

                def exponential(i, s):
                    act.wait_ge(diff_ready[s], i + 1)
                    nc.scalar.activation(decay[s], decay[s], ACT.Exp).then_inc(decay_ready[s], 1)

                def step(i, more):
                    if isinstance(i, int) and i == 0:
                        keep_projections(i, 0, range(4, GATES[0]))
                        keep_projections(i, 1)
                        act.wait_ge(decays.turned_ready, 1)
                        for s in two:
                            since_start(i, s)
                        for s in two:
                            exponential(i, s)
                    else:
                        for s in two:
                            since_start(i, s)
                        for s in two:
                            keep_projections(i, s)
                            exponential(i, s)
                    act.wait_ge(wo_loaded, i * 16 + 16)
                    after(act, pj_full, i * len(PJ))
                    nc.scalar.activation(wo_raw[:], wo_raw[:], ACT.Copy, scale=0.5).then_inc(wo_rounded, 1)
                    act.wait_ge(wo_rounded, i * 2 + 1)
                    nc.scalar.activation(wo_hi[:], wo_raw[:], ACT.Copy).then_inc(wo_rounded, 1)
                    for s in two:
                        for h in two:
                            act.wait_ge(ts_full, i * len(TS) + TS.index((s, f"key{h}")) + 1)
                            nc.scalar.activation(key[s][:, h].rearrange("t c k -> t (c k)"),
                                                 ts[TS.index((s, f"key{h}")) % NTS][0:CH, :], ACT.Copy).then_inc(ts_act, 1)
                        keep_projections(i, 0, GATES[s:s + 1])
                    keep_projections(i, 1, GATES)
                    for s in two:
                        act.wait_ge(mixed_ready[s], i * 2 + 2)
                        nc.scalar.activation(mixed_hi[s][:], mixed[s], ACT.Copy).then_inc(hi_ready[s], 1)
                        if more and s == 0:
                            round_weights(i + 1)

                norm.on_scalar(act, lambda: round_weights(0))
                for g in range(NG):
                    decays.keep(act, g, att[g % 2])
                decays.log_part(act, lambda: keep_projections(0, 0, range(4)))
                step(0, True)
                with act.Fori(1, 2 * PAIRS - 1) as i:
                    step(i, True)
                step(2 * PAIRS - 1, False)

            @block.vector
            def _(dve):
                dve.sem_inc(pj_dve, len(PJ_DVE))
                dve.sem_inc(ts_dve, len(TS_DVE))
                def differences(i, j, p):
                    for s in two:
                        dve.wait_ge(sums_loaded[s], i * 16 + 16)
                        after(dve, value_dec_ready[s], i)
                        for h in two:
                            for c in range(NCH):
                                own = m.decay_sum[:, ds(p * 2 + h, 1), ds((j * 2 + s) * NCH + c, 1)].rearrange("t h n -> t (h n)")
                                last = nc.vector.scalar_tensor_tensor(decay[s][:, h, c], sums[s][0:CH, h, c], own, m.causal[:],
                                                                      ALU.subtract, ALU.add)
                        last.then_inc(diff_ready[s], 1)

                PLACES = {4: (value_t, None), 5: (value_t, None), 8: (query_t, 1), 9: (query_t, 1)}

                def keep_projections(i, s, pieces=(4, 5, 8, 9)):
                    for k in pieces:
                        out, h = PLACES[k]
                        out = out[s][:] if h is None else out[s][:, h]
                        first, size = PIECES[k % NPC]
                        use = PJ.index(("in", s, k))
                        dve.wait_ge(pj_full, i * len(PJ) + use + 1)
                        nc.vector.tensor_copy(out[:, first:first + size], pj[use % NPJ][:, 0:size]).then_inc(pj_dve, 1)

                def step(j, p):
                    i = j * PAIRS + p
                    if isinstance(i, int):
                        keep_projections(i, 0, (8, 9))
                        keep_projections(i, 1)
                        decays.keep_sums(dve, ts[0])
                        differences(i, j, p)
                    else:
                        differences(i, j, p)
                        for s in two:
                            after(dve, query_dec_ready[s], i)
                            keep_projections(i, s)
                    for s in two:
                        for n in range(3):
                            use = TS.index((s, f"score{n}"))
                            nchunk = 2 if n < 2 else 1
                            dve.wait_ge(ts_full, i * len(TS) + use + 1)
                            dve.wait_ge(decay_ready[s], i + 1)
                            after(dve, att_full[s], i * 2)
                            nc.vector.tensor_tensor(
                                probs[s][:, :, 2 * n:2 * n + nchunk],
                                ts[use % NTS][0:CH, 0:2 * nchunk * CH].rearrange("k (h c t) -> k h c t", h=2, c=nchunk),
                                decay[s][:, :, 2 * n:2 * n + nchunk], ALU.mult).then_inc(ts_dve, 1)
                        for n, (c0, c1) in enumerate(((0, NCH - 1), (NCH - 1, NCH))):
                            use = TS.index((s, f"value{n}"))
                            dve.wait_ge(ts_full, i * len(TS) + use + 1)
                            nc.vector.tensor_copy(value[s][:, c0:c1].rearrange("t c v -> t (c v)"),
                                                  ts[use % NTS][0:CH, 0:(c1 - c0) * 2 * DV]).then_inc(ts_dve, 1)
                    for s in two:
                        use = TS.index((s, "state"))
                        dve.wait_ge(ts_full, i * len(TS) + use + 1)
                        dve.wait_ge(since_ready[s], i + 1)
                        part = ts[use % NTS][:].rearrange("k (c v) -> k c v", c=NCH - 1)
                        nc.vector.tensor_copy(state[s][:, 0], part[:, 0]).then_inc(state_chain, 1)
                        for c in range(1, NCH - 1):
                            dve.wait_ge(state_chain, i * 6 + s * 3 + c)
                            for h in two:
                                v = slice(h * DV, (h + 1) * DV)
                                last = nc.vector.scalar_tensor_tensor(state[s][:, c, v], state[s][:, c - 1, v],
                                                                      since[s][:, h, c, CH - 1:CH], part[:, c, v], ALU.mult, ALU.add)
                            last.then_inc(state_chain if c < NCH - 2 else ts_dve, 1)
                    for s in two:
                        after(dve, lo_ready[s], i)
                        for n, (c0, c1) in enumerate(((0, NCH - 1), (NCH - 1, NCH))):
                            dve.wait_ge(att_full[s], i * 2 + n + 1)
                            pj_taken(dve, i, ("in", s, 11))
                            at = slice(c0 * CH, c1 * CH)
                            nc.vector.scalar_tensor_tensor(mixed[s][:, at], gate[s][:, at], 1.0, att[n][:, 0:(c1 - c0) * CH],
                                                           ALU.add, ALU.mult).then_inc(mixed_ready[s], 1)
                        dve.wait_ge(hi_ready[s], i + 1)
                        nc.vector.tensor_tensor(mixed_lo[s][:], mixed[s], mixed_hi[s][:].bitcast(F32),
                                                ALU.subtract).then_inc(lo_ready[s], 1)
                    for s in two:
                        for n in range(2 * NPC):
                            kc, (first, size) = n // NPC, PIECES[n % NPC]
                            use = PJ.index(("out", s, n))
                            dve.wait_ge(pj_full, i * len(PJ) + use + 1)
                            at = m.h[:, kc, ds((j * 2 + s) * SP + first, size)]
                            nc.vector.tensor_tensor(at, at, pj[use % NPJ][:, 0:size], ALU.add).then_inc(pj_dve, 1)

                norm.on_vector(dve, decays.prepare_weights)
                decays.sum_up(dve, lambda: keep_projections(0, 0, (4, 5)))
                step(0, 0)
                with dve.Fori(1, PAIRS) as p:
                    step(0, p)
                with dve.Fori(0, PAIRS) as p:
                    step(1, p)

            @block.tensor
            def _(pe):
                def take_pj(i, use):
                    u = PJ.index(use)
                    pj_taken(pe, i, PJ[(u - NPJ) % len(PJ)], before=u < NPJ)
                    return pj[u % NPJ]

                def take_ts(i, use):
                    u = TS.index(use)
                    ts_taken(pe, i, TS[(u - NTS) % len(TS)], before=u < NTS)
                    return ts[u % NTS]

                def step(j, p):
                    i = j * PAIRS + p
                    pe.wait_ge(w_split, i + 1)

                    def project(s, k):
                        kind, (first, n) = KINDS[k], PIECES[k % NPC]
                        at = {"k": WK, "v": WV, "q": WQ, "g": WO}[kind[0]] + (DK if kind[-1] == "1" else 0)
                        bank = take_pj(i, ("in", s, k))
                        for kc in range(KC):
                            x = [t[:, kc, ds((j * 2 + s) * SP + first, n)] for t in (m.x_hi, m.x_lo)]
                            last = product(nc, bank[:, 0:n], (w_hi[:, kc, at:at + P], w_lo[:, kc, at:at + P]), x,
                                           kc == 0, kc == KC - 1)
                        last.then_inc(pj_full, 1)

                    for s in two:
                        for k in range(GATES[0]):
                            if isinstance(i, int) and (s, k) == (1, 4):
                                decays.turn(pe, ts[0])
                            project(s, k)
                    for s in two:
                        if isinstance(i, int):
                            pe.wait_ge(decays.sum_ready, 1)
                        pj_taken(pe, i, ("in", s, 7))
                        pj_taken(pe, i, ("in", s, 9))
                        for n in range(3):
                            nchunk = 2 if n < 2 else 1
                            bank = take_ts(i, (s, f"score{n}"))
                            for h in two:
                                for c in range(nchunk):
                                    at = slice((2 * n + c) * CH, (2 * n + c + 1) * CH)
                                    o = (h * nchunk + c) * CH
                                    last = nc.tensor.matmul(bank[0:CH, o:o + CH], key_t[s][:, h, at], query_t[s][:, h, at],
                                                            start=True, stop=True)
                            last.then_inc(ts_full, 1)
                        for h in two:
                            bank = take_ts(i, (s, f"key{h}"))
                            for c in range(NCH - 1):
                                last = nc.tensor.transpose(bank[0:CH, c * DK:(c + 1) * DK], key_t[s][:, h, c * CH:(c + 1) * CH], m.ident[:])
                            last.then_inc(ts_full, 1)
                        pj_taken(pe, i, ("in", s, 5))
                        for n, (c0, c1) in enumerate(((0, NCH - 1), (NCH - 1, NCH))):
                            bank = take_ts(i, (s, f"value{n}"))
                            for c in range(c0, c1):
                                last = nc.tensor.transpose(bank[0:CH, (c - c0) * P:(c - c0 + 1) * P], value_t[s][:, c * CH:(c + 1) * CH], m.ident[:])
                            last.then_inc(ts_full, 1)
                            if n == 0:
                                project(0, GATES[s])
                    project(1, GATES[0])
                    for s in two:
                        ts_taken(pe, i, (s, "key1"))
                        pe.wait_ge(value_dec_ready[s], i + 1)
                        bank = take_ts(i, (s, "state"))
                        for c in range(NCH - 1):
                            for h in two:
                                o = c * 2 * DV + h * DV
                                last = nc.tensor.matmul(bank[:, o:o + DV], key[s][:, h, c], value_dec[s][:, c, h], start=True, stop=True)
                        last.then_inc(ts_full, 1)
                    for s in two:
                        if s == 1:
                            project(1, GATES[1])
                        after(pe, mixed_ready[1 - s], (i + s) * 2)
                        ts_taken(pe, i, (s, "state"))
                        pe.wait_ge(query_dec_ready[s], i + 1)
                        for c in range(NCH):
                            bank, o = (att[0], c * CH) if c < NCH - 1 else (att[1], 0)
                            for h in two:
                                out = bank[h * DV:(h + 1) * DV, o:o + CH]
                                last = nc.tensor.matmul(out, value[s][:, c, h * DV:(h + 1) * DV], probs[s][:, h, c], start=True, stop=c == 0)
                                if c > 0:
                                    last = nc.tensor.matmul(out, state[s][:, c - 1, h * DV:(h + 1) * DV],
                                                            query_dec[s][:, h, c * CH:(c + 1) * CH], start=False, stop=True)
                            if c >= NCH - 2:
                                last.then_inc(att_full[s], 1)
                    pe.wait_ge(wo_split, i + 1)
                    for s in two:
                        pe.wait_ge(lo_ready[s], i + 1)
                        for n in range(2 * NPC):
                            kc, (first, size) = n // NPC, PIECES[n % NPC]
                            bank = take_pj(i, ("out", s, n))
                            at = slice(kc * P, (kc + 1) * P)
                            product(nc, bank[:, 0:size], (wo_hi[:, at], wo_lo[:, at]),
                                    (mixed_hi[s][:, first:first + size], mixed_lo[s][:, first:first + size]),
                                    True, True).then_inc(pj_full, 1)

                norm.on_tensor(pe)
                for g in range(NG):
                    norm.x_ready(pe, g)
                    if g >= 2:
                        pe.wait_ge(decays.z_ready, g - 1)
                    else:
                        pe.wait_ge(norm.logv_ready, g + 3)
                    decays.logits(pe, g, att[g % 2])
                step(0, 0)
                with pe.Fori(1, PAIRS) as p:
                    step(0, p)
                with pe.Fori(0, PAIRS) as p:
                    step(1, p)


class Gate:
    NTILE = B * NCH
    FIRST = P // E

    def __init__(self, nc, m, sb, sem, gate_w, gate_b, top_two):
        self.nc, self.m, self.gate_w, self.gate_b, self.top_two = nc, m, gate_w, gate_b, top_two
        self.w = sb("gate_w", [P, KC, E])
        self.w_hi = sb("gate_w_hi", [P, KC, P], F32R)
        self.w_lo = sb("gate_w_lo", [P, KC, P], F32R)
        self.bias = sb("gate_b", [E, 1])
        self.z = sb("gate_z", [E, NT])
        self.rank = sb("gate_rank", [CH, self.NTILE, E])
        (self.shifted, self.ex, self.g, self.a, self.b, self.one1, self.one2, self.rest, self.cw) = (
            sb(f"gate_{n}", [CH, self.NTILE, E]) for n in ("shifted", "exp", "g", "a", "b_", "one1", "one2", "rest", "cw"))
        (self.top, self.total, self.inv, self.first, self.best, self.second) = (
            sb(f"gate_{n}", [CH, self.NTILE]) for n in ("top", "total", "inv", "first", "best", "second"))
        self.rows = sb("cw_rows", [P, 2, CH])
        self.loaded = sem("gate_loaded")
        self.bias_ready = sem("gate_bias_ready")
        self.rank_ready = sem("gate_rank_ready")
        self.w_ready = sem("gate_w_ready")
        self.logits_ready = sem("gate_logits_ready")
        self.z_ready = sem("gate_z_ready")
        self.turned_ready = sem("gate_turned_ready")
        self.chain = sem("gate_chain")
        self.shifted_ready = sem("gate_shifted_ready")
        self.ex_ready = sem("gate_ex_ready")
        self.cw_ready = sem("gate_cw_ready")
        self.back_ready = sem("gate_back_ready")
        self.rows_ready = sem("gate_rows_ready")
        self.stored = sem("gate_stored")

    def load(self, sp):
        sp.dma_start(self.w[:], self.gate_w.rearrange("(k p) n -> p k n", p=P)).then_inc(self.loaded, 16)
        if self.gate_b is not None:
            sp.dma_start(self.bias[:], self.gate_b.rearrange("(n o) -> n o", o=1)).then_inc(self.bias_ready, 16)

    def fill(self):
        for e in range(E):
            last = self.nc.gpsimd.memset(self.rank[:, :, e:e + 1], float(E - e))
        last.then_inc(self.rank_ready, 1)

    def link(self, dve, n, ins):
        ins.then_inc(self.chain, 1)
        dve.wait_ge(self.chain, n)

    def prepare_weights(self, dve):
        nc = self.nc
        if self.gate_b is None:
            nc.vector.memset(self.bias[:], 0.0).then_inc(self.bias_ready, 16)
        self.link(dve, 1, nc.vector.memset(self.w_hi[:].bitcast(F32), 0.0))
        self.link(dve, 2, nc.vector.memset(self.w_lo[:].bitcast(F32), 0.0))
        dve.wait_ge(self.loaded, 16)
        self.link(dve, 3, nc.vector.tensor_copy(self.w_hi[:, :, 0:E], self.w[:]))
        nc.vector.tensor_tensor(self.w_lo[:, :, 0:E], self.w[:], self.w_hi[:, :, 0:E].bitcast(F32), ALU.subtract).then_inc(self.w_ready, 1)

    def logits(self, pe, i, bank):
        if i == 0:
            pe.wait_ge(self.w_ready, 1)
        x = (self.m.x_hi, self.m.x_lo)
        for kc in range(KC):
            last = product(self.nc, bank[:, 0:G], (self.w_hi[:, kc], self.w_lo[:, kc]),
                           [t[:, kc, i * G:(i + 1) * G] for t in x], kc == 0, kc == KC - 1)
        last.then_inc(self.logits_ready, 1)

    def keep(self, act, i, bank):
        if i == 0:
            act.wait_ge(self.bias_ready, 16)
        act.wait_ge(self.logits_ready, i + 1)
        self.nc.scalar.activation(self.z[:, i * G:(i + 1) * G], bank[0:E, 0:G], ACT.Identity, bias=self.bias[:]).then_inc(self.z_ready, 1)

    def turn(self, pe, bank):
        pe.wait_ge(self.z_ready, NG)
        for c in range(self.NTILE):
            last = self.nc.tensor.transpose(bank[0:CH, c * E:(c + 1) * E], self.z[:, c * CH:(c + 1) * CH], self.m.ident[0:E, 0:E])
        last.then_inc(self.turned_ready, 1)

    def exponentials(self, act):
        act.wait_ge(self.shifted_ready, 1)
        self.nc.scalar.activation(self.ex[:], self.shifted[:], ACT.Exp).then_inc(self.ex_ready, 1)

    def choose(self, dve, bank):
        nc, made = self.nc, [3]

        def link(ins):
            made[0] += 1
            self.link(dve, made[0], ins)

        def wide(t):
            return spread(t[:], 2, E)

        dve.wait_ge(self.turned_ready, 1)
        logits = bank[0:CH, 0:self.NTILE * E].rearrange("t (n e) -> t n e", e=E)
        link(nc.vector.tensor_reduce(self.top[:], logits, AX_X, ALU.max))
        nc.vector.tensor_tensor(self.shifted[:], logits, wide(self.top), ALU.subtract).then_inc(self.shifted_ready, 1)
        dve.wait_ge(self.ex_ready, 1)
        link(nc.vector.tensor_reduce(self.total[:], self.ex[:], AX_X, ALU.add))
        link(nc.vector.reciprocal(self.inv[:], self.total[:]))
        link(nc.vector.tensor_tensor(self.g[:], self.ex[:], wide(self.inv), ALU.mult))
        if self.top_two:
            dve.wait_ge(self.rank_ready, 1)

            def pick(src, value, one):
                link(nc.vector.tensor_reduce(value[:], src[:], AX_X, ALU.max))
                link(nc.vector.tensor_tensor(self.a[:], src[:], wide(value), ALU.is_ge))
                link(nc.vector.tensor_tensor(self.b[:], self.a[:], self.rank[:], ALU.mult))
                link(nc.vector.tensor_reduce(self.best[:], self.b[:], AX_X, ALU.max))
                link(nc.vector.tensor_tensor(one[:], self.b[:], wide(self.best), ALU.is_equal))

            pick(self.g, self.first, self.one1)
            link(nc.vector.scalar_tensor_tensor(self.rest[:], self.one1[:], -2.0, self.g[:], ALU.mult, ALU.add))
            pick(self.rest, self.second, self.one2)
            link(nc.vector.tensor_tensor(self.a[:], self.one1[:], self.one2[:], ALU.add))
            link(nc.vector.tensor_tensor(self.b[:], self.a[:], self.g[:], ALU.mult))
            link(nc.vector.scalar_tensor_tensor(self.total[:], self.first[:], 1e-8, self.second[:], ALU.add, ALU.add))
        else:
            link(nc.vector.scalar_tensor_tensor(self.b[:], self.g[:], 0.1, self.g[:], ALU.is_ge, ALU.mult))
            link(nc.vector.tensor_reduce(self.top[:], self.b[:], AX_X, ALU.add))
            link(nc.vector.scalar_tensor_tensor(self.total[:], self.top[:], 0.0, self.top[:], ALU.is_equal, ALU.add))
        link(nc.vector.reciprocal(self.inv[:], self.total[:]))
        nc.vector.tensor_tensor(self.cw[:], self.b[:], wide(self.inv), ALU.mult).then_inc(self.cw_ready, 1)

    def turn_back(self, pe, bank):
        pe.wait_ge(self.cw_ready, 1)
        cw = self.cw[:].rearrange("t n e -> t (n e)")
        self.nc.tensor.transpose(bank[:, 0:CH], cw[:, 0:P], self.m.ident[0:CH, 0:CH])
        rest = (self.NTILE - self.FIRST) * E
        self.nc.tensor.transpose(bank[0:rest, CH:2 * CH], cw[:, P:P + rest], self.m.ident[0:CH, 0:CH]).then_inc(self.back_ready, 1)

    def keep_rows(self, act, bank):
        act.wait_ge(self.back_ready, 1)
        rest = (self.NTILE - self.FIRST) * E
        self.nc.scalar.activation(self.rows[:, 0], bank[:, 0:CH], ACT.Copy).then_inc(self.rows_ready, 1)
        self.nc.scalar.activation(self.rows[0:rest, 1], bank[0:rest, CH:2 * CH], ACT.Copy).then_inc(self.rows_ready, 1)

    def store(self, sp):
        sp.wait_ge(self.rows_ready, 2)
        rest = (self.NTILE - self.FIRST) * E
        chunks = self.m.cw_dram.rearrange("e (c t) -> c e t", t=CH)
        sp.dma_start(chunks[0:self.FIRST], self.rows[:, 0]).then_inc(self.stored, 16)
        sp.dma_start(chunks[self.FIRST:self.NTILE], self.rows[0:rest, 1]).then_inc(self.stored, 16)
        sp.wait_ge(self.stored, 32)


def stage_hidden_experts(nc, m, d):
    HC = HID // P
    W1N, WN = KC * HID, KC * HID + HC * D
    NS = 2 * NG
    with ExitStack() as ctx:
        sb, ps, sem = open_stage(nc, ctx, "ffn0")
        two = range(2)
        raw = [sb(f"raw{s}", [P, WN]) for s in two]
        w_hi = [sb(f"e_hi{s}", [P, WN], F32R) for s in two]
        w_lo = [sb(f"e_lo{s}", [P, WN], F32R) for s in two]
        b1 = sb("b1_all", [P, E, HC])
        b1_of = [sb(f"b1_of{s}", [P, HC]) for s in two]
        b2 = sb("b2_all", [P, E, KC])
        cw_or_y = sb("cw_or_y", [P, 2, NT])
        cw = [cw_or_y[:, s] for s in two]
        hid = [sb(f"hid{s}", [P, HC, G]) for s in two]
        hid_hi = [sb(f"hid_hi{s}", [P, HC, G], F32R) for s in two]
        hid_lo = [sb(f"hid_lo{s}", [P, HC, G], F32R) for s in two]
        part = [sb(f"part{s}", [P, KC, G]) for s in two]
        hb = [ps(f"hb{i}", [P, BANK]) for i in range(HC)]
        ob = [ps(f"ob{i}", [P, BANK]) for i in range(2 * KC)]
        pair = sb("pair", [P, NT])
        norm = Norm(nc, m, sem, cw_or_y, pair, [t[:].rearrange("p k g -> p (k g)") for t in part], ob + hb[HC - 1:])
        gate = Gate(nc, m, sb, sem, d["L0_ffn_gate_W"], None, True)
        raw_loaded = [sem(f"raw_loaded{s}") for s in two]
        cw_loaded = [sem(f"cw_loaded{s}") for s in two]
        bias_loaded = sem("bias_loaded")
        b1_ready = [sem(f"b1_ready{s}") for s in two]
        x_added = sem("x_added")
        rounded = [sem(f"w_rounded{s}") for s in two]
        split = [sem(f"w_split{s}") for s in two]
        hid_full = sem("hid_full")
        relu_done = sem("relu_done")
        hi_done = sem("hid_hi_done")
        lo_done = sem("hid_lo_done")
        out_full = sem("out_full")
        weighted = sem("weighted")
        summed = sem("summed")

        def w1(w, kc, hc):
            return w[:, kc * HID + hc * P:kc * HID + (hc + 1) * P]

        def w2(w, hc, kc):
            return w[:, W1N + hc * D + kc * P:W1N + hc * D + (kc + 1) * P]

        def reached(i, per, k, n):
            return (i + 1) * NS * per + k * per + n

        with nc.Block() as block:
            @block.sync
            def _(sp):
                sp.dma_start(b1[:], d["L0_ffn_b1"].rearrange("e (c p) -> p e c", p=P)).then_inc(bias_loaded, 16)
                sp.dma_start(b2[:], d["L0_ffn_b2"].rearrange("e (c p) -> p e c", p=P)).then_inc(bias_loaded, 16)

                def load_weights(i, s):
                        e = i * 2 + s
                        sp.dma_start(raw[s][:, 0:W1N].rearrange("p (k n) -> p k n", k=KC),
                                     d["L0_ffn_W1"][ds(e, 1)].rearrange("o (k p) n -> p (o k) n", p=P)).then_inc(raw_loaded[s], 16)
                        sp.dma_start(raw[s][:, W1N:WN].rearrange("p (k n) -> p k n", k=HC),
                                     d["L0_ffn_W2"][ds(e, 1)].rearrange("o (k p) n -> p (o k) n", p=P)).then_inc(raw_loaded[s], 16)

                def load_expert_weights(i, s):
                        e = i * 2 + s
                        sp.dma_start(cw[s], m.cw_dram[ds(e, 1)].rearrange("o n -> (o n)").partition_broadcast(P)).then_inc(cw_loaded[s], 16)

                load_weights(0, 0)
                gate.load(sp)
                load_weights(0, 1)
                gate.store(sp)
                sp.wait_ge(x_added, NG)
                for s in two:
                    load_expert_weights(0, s)
                with sp.Fori(1, E // 2) as i:
                    for s in two:
                        sp.wait_ge(split[s], i)
                        load_weights(i, s)
                        sp.wait_ge(weighted, reached(i, 2, s * NG + NG - 1 - NS, 2))
                        load_expert_weights(i, s)

            @block.gpsimd
            def _(pool):
                pool.sem_inc(summed, NS)

                def low_part(i, s):
                    pool.wait_ge(rounded[s], i + 1)
                    nc.gpsimd.tensor_tensor(w_lo[s][:], raw[s][:], w_hi[s][:].bitcast(F32), ALU.subtract).then_inc(split[s], 1)

                def step(i, more):
                    for k in range(NS):
                        at = slice(k % NG * G, (k % NG + 1) * G)
                        pool.wait_ge(weighted, reached(i, 2, k, 2))
                        pool.wait_ge(summed, reached(i, 1, k - NG, 1))
                        nc.gpsimd.tensor_tensor(m.h[:, :, at], m.h[:, :, at], part[k % 2][:], ALU.add).then_inc(summed, 1)
                        if k == 0:
                            low_part(i, 1)
                        if k == NG and more:
                            low_part(i + 1, 0)

                norm.on_pool(pool, lambda: low_part(0, 0))
                gate.fill()
                for i in range(NG):
                    at = slice(i * G, (i + 1) * G)
                    pool.wait_ge(norm.y_ready, i + 1)
                    nc.gpsimd.tensor_tensor(m.h[:, :, at], m.h[:, :, at], cw_or_y[:, :, at], ALU.add).then_inc(x_added, 1)
                pool.wait_ge(x_added, NG)
                with pool.Fori(0, E // 2 - 1) as i:
                    step(i, True)
                step(E // 2 - 1, False)

            @block.scalar
            def _(act):
                act.sem_inc(relu_done, NS * HC)

                def round_weights(i, s):
                    act.wait_ge(raw_loaded[s], i * 32 + 32)
                    act.wait_ge(out_full, reached(i, 1, s * NG + NG - 1 - NS, 1))
                    nc.scalar.activation(w_hi[s][:], raw[s][:], ACT.Copy).then_inc(rounded[s], 1)

                def relu(i, k):
                        if k % NG == 0:
                            act.wait_ge(b1_ready[k // NG], i + 1)
                        act.wait_ge(lo_done, reached(i, 1, k - 2, 1))
                        for hc in range(HC):
                            act.wait_ge(hid_full, i * NS * HC + k * HC + hc + 1)
                            nc.scalar.activation(hid[k % 2][:, hc], hb[hc][:, 0:G], ACT.Relu,
                                                 bias=b1_of[k // NG][:, hc:hc + 1]).then_inc(relu_done, 1)

                def step(i, more, first=0):
                    for k in range(first, NS):
                        relu(i, k)
                        if k == 0:
                            round_weights(i, 1)
                        if k == NG and more:
                            round_weights(i + 1, 0)

                norm.on_scalar(act, lambda: round_weights(0, 0))
                gate.keep(act, 0, ob[0])
                relu(0, 0)
                for g in range(1, NG):
                    gate.keep(act, g, ob[g % 4])
                gate.exponentials(act)
                relu(0, 1)
                round_weights(0, 1)
                relu(0, 2)
                gate.keep_rows(act, ob[3])
                step(0, True, 3)
                with act.Fori(1, E // 2 - 1) as i:
                    step(i, True)
                step(E // 2 - 1, False)

            @block.vector
            def _(dve):
                dve.sem_inc(lo_done, NS)
                dve.sem_inc(weighted, NS * 2)

                def place_bias(i, s):
                    nc.vector.tensor_copy(b1_of[s][:], b1[:, ds(i * 2 + s, 1)].rearrange("p o c -> p (o c)")).then_inc(b1_ready[s], 1)

                def split_hidden(i, k):
                    dve.wait_ge(relu_done, reached(i, HC, k, HC))
                    dve.wait_ge(out_full, reached(i, 1, k - 2, 1))
                    nc.vector.tensor_copy(hid_hi[k % 2][:], hid[k % 2][:]).then_inc(hi_done, 1)
                    dve.wait_ge(hi_done, i * NS + k + 1)
                    nc.vector.tensor_tensor(hid_lo[k % 2][:], hid[k % 2][:], hid_hi[k % 2][:].bitcast(F32),
                                            ALU.subtract).then_inc(lo_done, 1)

                def weigh(i, k):
                    s, g = divmod(k, NG)
                    if g == 0:
                        dve.wait_ge(cw_loaded[s], i * 16 + 16)
                    dve.wait_ge(out_full, reached(i, 1, k, 1))
                    dve.wait_ge(summed, reached(i, 1, k - 2, 1))
                    for kc in range(KC):
                        nc.vector.scalar_tensor_tensor(part[k % 2][:, kc], ob[k % 2 * KC + kc][:, 0:G],
                                                       b2[:, ds(i * 2 + s, 1), kc],
                                                       cw[s][:, g * G:(g + 1) * G], ALU.add, ALU.mult).then_inc(weighted, 1)

                norm.on_vector(dve, gate.prepare_weights)
                dve.wait_ge(bias_loaded, 32)
                for s in two:
                    place_bias(0, s)
                split_hidden(0, 0)
                gate.choose(dve, ob[2])
                split_hidden(0, 1)
                split_hidden(0, 2)
                weigh(0, 0)
                weigh(0, 1)
                for k in range(3, NS):
                    split_hidden(0, k)
                    weigh(0, k - 1)
                weigh(0, NS - 1)
                with dve.Fori(1, E // 2) as i:
                    for k in range(NS):
                        if k < 2:
                            place_bias(i, k)
                        split_hidden(i, k)
                        if k > 0:
                            weigh(i, k - 1)
                    weigh(i, NS - 1)

            @block.tensor
            def _(pe):
                pe.sem_inc(out_full, NS)

                def up(i, k):
                    s, g = divmod(k, NG)
                    if g == 0:
                        pe.wait_ge(split[s], i + 1)
                    for hc in range(HC):
                        pe.wait_ge(relu_done, reached(i, HC, k - 1, hc + 1))
                        for kc in range(KC):
                            x = [t[:, kc, g * G:(g + 1) * G] for t in (m.x_hi, m.x_lo)]
                            last = product(nc, hb[hc][:, 0:G], (w1(w_hi[s], kc, hc), w1(w_lo[s], kc, hc)), x, kc == 0, kc == KC - 1)
                        last.then_inc(hid_full, 1)

                def down(i, k):
                    s = k // NG
                    pe.wait_ge(lo_done, reached(i, 1, k, 1))
                    pe.wait_ge(weighted, reached(i, 2, k - 2, 2))
                    for kc in range(KC):
                        for hc in range(HC):
                            last = product(nc, ob[k % 2 * KC + kc][:, 0:G], (w2(w_hi[s], hc, kc), w2(w_lo[s], hc, kc)),
                                           (hid_hi[k % 2][:, hc], hid_lo[k % 2][:, hc]), hc == 0, hc == HC - 1)
                    last.then_inc(out_full, 1)

                norm.on_tensor(pe)
                for g in range(NG):
                    norm.x_ready(pe, g)
                    if g == NG - 1:
                        pe.wait_ge(gate.z_ready, g % 4 + 1)
                    else:
                        pe.wait_ge(norm.logv_ready, NG if g % 4 == NG - 1 else g + 1)
                    gate.logits(pe, g, ob[g % 4])
                    if g == 0:
                        pe.wait_ge(norm.logv_ready, NG)
                        up(0, 0)
                gate.turn(pe, ob[2])
                up(0, 1)
                down(0, 0)
                up(0, 2)
                gate.turn_back(pe, ob[3])
                pe.wait_ge(gate.shifted_ready, 1)
                pe.wait_ge(gate.rows_ready, 2)
                down(0, 1)
                for k in range(3, NS):
                    up(0, k)
                    down(0, k - 1)
                down(0, NS - 1)
                with pe.Fori(1, E // 2) as i:
                    up(i, 0)
                    for k in range(1, NS):
                        up(i, k)
                        down(i, k - 1)
                    down(i, NS - 1)


def stage_linear_attention(nc, m, d):
    HDIM = 16
    NPC = len(PIECES)
    MATS = "kvqgo"
    KINDS = [(kind, mc, n) for kind in "kvqg" for mc in range(KC) for n in range(NPC)]
    PJ = ([("in", s) + u for s in range(2) for u in KINDS] + [("att", s, mc, n) for s in range(2) for mc in range(KC) for n in range(NPC)]
          + [("out", s, mc, n) for s in range(2) for mc in range(KC) for n in range(NPC)])
    PJ_ACT = [u for u in PJ if u[0] == "in"]
    PJ_DVE = [u for u in PJ if u not in PJ_ACT]
    ELU = [u for u in PJ if u[0] == "in" and u[2] in "kq"]
    NPJ, NTS = 4, 2
    with ExitStack() as ctx:
        sb, ps, sem = open_stage(nc, ctx, "attn1")
        two = range(2)
        raw = sb("raw", [P, 5, KC, D])
        w_hi = sb("hi", [P, 5, KC, D], F32R)
        w_lo = sb("lo", [P, 5, KC, D], F32R)
        bias = sb("bias", [P, 5, KC])
        half_bias = sb("half_bias", [P, KC])
        block_mask = sb("block_mask", [P, P])
        key_t = [sb(f"key_t{s}", [P, KC, SP]) for s in two]
        value_t = [sb(f"value_t{s}", [P, KC, SP]) for s in two]
        query_t = [sb(f"query_t{s}", [P, KC, SP]) for s in two]
        gate = [sb(f"gate{s}", [P, KC, SP]) for s in two]
        ex_pos = sb("ex_pos", [P, 8 * PIECES[0][1]])
        ex = [ex_pos[:, i * PIECES[0][1]:(i + 1) * PIECES[0][1]] for i in range(4)]
        pos = [ex_pos[:, i * PIECES[0][1]:(i + 1) * PIECES[0][1]] for i in range(4, 8)]
        rows = [sb(f"rows{s}", [CH, NCH, 2 * D]) for s in two]
        kv = [sb(f"kv{s}", [P, KC, P]) for s in two]
        mixed = [sb(f"mixed{s}", [P, KC, SP]) for s in two]
        mixed_hi = [sb(f"mixed_hi{s}", [P, KC, SP], F32R) for s in two]
        mixed_lo = [sb(f"mixed_lo{s}", [P, KC, SP], F32R) for s in two]
        pj = [ps(f"pj{i}", [P, BANK]) for i in range(NPJ)]
        ts = [ps(f"ts{i}", [P, BANK]) for i in range(NTS)]
        kvb = [ps(f"kvb{s}", [P, BANK]) for s in two]
        y = sb("y", [P, KC, NT])
        norm = Norm(nc, m, sem, y, ex_pos[:, 0:NT],
                    [t[:].rearrange("p k c -> p (k c)")[:, 0:KC * G] for t in gate], ts + kvb)
        loaded = sem("loaded")
        rounded = sem("rounded")
        split = sem("split")
        mask_ready = sem("mask_ready")
        bias_ready = sem("bias_ready")
        halved = sem("output_weights_halved")
        pj_full = sem("pj_full")
        pj_act = sem("pj_taken_by_act")
        pj_dve = sem("pj_taken_by_dve")
        elu_ready = sem("elu_ready")
        ts_full = sem("ts_full")
        rows_ready = sem("rows_ready")
        kv_full = sem("kv_full")
        kv_ready = sem("kv_ready")
        hi_ready = sem("hi_ready")
        lo_ready = sem("lo_ready")

        def pj_taken(eng, i, use, before=False):
            users, s_ = (PJ_DVE, pj_dve) if use in PJ_DVE else (PJ_ACT, pj_act)
            eng.wait_ge(s_, (i + (0 if before else 1)) * len(users) + users.index(use) + 1)

        with nc.Block() as block:
            @block.sync
            def _(sp):
                for n, w in enumerate((d["L1_attn_Wk"], d["L1_attn_Wv"], d["L1_attn_Wq"], d["L1_attn_Wg"], d["L1_attn_Wo"])):
                    sp.dma_start(raw[:, n], w.rearrange("(k p) n -> p k n", p=P)).then_inc(loaded, 16)
                for n, b in enumerate((d["L1_attn_bk"], d["L1_attn_bv"], d["L1_attn_bq"], d["L1_attn_bg"], d["L1_attn_bo"])):
                    sp.dma_start(bias[:, n], b.rearrange("(k p) -> p k", p=P)).then_inc(loaded, 16)

            @block.gpsimd
            def _(pool):
                def low_part(n):
                    pool.wait_ge(rounded, n + 1)
                    nc.gpsimd.tensor_tensor(w_lo[:, n], raw[:, n], w_hi[:, n].bitcast(F32), ALU.subtract).then_inc(split, 1)

                def low_parts():
                    for n in range(MATS.index("o")):
                        low_part(n)
                    pool.wait_ge(loaded, 160)
                    nc.gpsimd.tensor_scalar(half_bias[:], bias[:, MATS.index("g")], 0.5, None, ALU.mult).then_inc(bias_ready, 1)

                norm.on_pool(pool, low_parts)
                nc.gpsimd.memset(block_mask[:], 1.0).then_inc(mask_ready, 1)
                blocks = block_mask[:].rearrange("p (n c) -> p n c", c=HDIM)
                pool.wait_ge(mask_ready, 1)
                nc.gpsimd.affine_select(out=blocks, in_=blocks, compare_op=ALU.is_ge, fill=0.0, base=0,
                                        pattern=[[-HDIM, P // HDIM], [0, HDIM]], channel_multiplier=1).then_inc(mask_ready, 1)
                pool.wait_ge(mask_ready, 2)
                nc.gpsimd.affine_select(out=blocks, in_=blocks, compare_op=ALU.is_ge, fill=0.0, base=HDIM - 1,
                                        pattern=[[HDIM, P // HDIM], [0, HDIM]], channel_multiplier=-1).then_inc(mask_ready, 1)
                low_part(MATS.index("o"))

            @block.scalar
            def _(act):
                act.sem_inc(pj_act, len(PJ_ACT))

                def round_matrices():
                    act.wait_ge(loaded, 160)
                    for n in range(MATS.index("o")):
                        nc.scalar.activation(w_hi[:, n], raw[:, n], ACT.Copy).then_inc(rounded, 1)

                norm.on_scalar(act, round_matrices)
                act.wait_ge(bias_ready, 1)
                n = MATS.index("o")
                nc.scalar.activation(raw[:, n], raw[:, n], ACT.Copy, scale=0.5).then_inc(halved, 1)
                act.wait_ge(halved, 1)
                nc.scalar.activation(w_hi[:, n], raw[:, n], ACT.Copy).then_inc(rounded, 1)
                with act.Fori(0, B // 2) as i:
                    for s in two:
                        for kind, mc, n in KINDS:
                            first, size = PIECES[n]
                            use = ("in", s, kind, mc, n)
                            u = PJ.index(use)
                            bank = pj[u % NPJ][:, 0:size]
                            act.wait_ge(pj_full, i * len(PJ) + u + 1)
                            if kind in "kq":
                                v = ELU.index(use)
                                act.wait_ge(elu_ready, (i + 1) * len(ELU) + v - 3)
                                nc.scalar.activation(ex[v % 4][:, 0:size], bank, ACT.Exp, bias=bias[:, MATS.index(kind), mc:mc + 1])
                                nc.scalar.activation(pos[v % 4][:, 0:size], bank, ACT.Relu,
                                                     bias=bias[:, MATS.index(kind), mc:mc + 1]).then_inc(pj_act, 1)
                            elif kind == "v":
                                nc.scalar.activation(value_t[s][:, mc, first:first + size], bank, ACT.Identity,
                                                     bias=bias[:, MATS.index("v"), mc:mc + 1]).then_inc(pj_act, 1)
                            else:
                                pj_taken(act, i, ("att", s, KC - 1, NPC - 1), before=True)
                                nc.scalar.activation(gate[s][:, mc, first:first + size], bank, ACT.Tanh, scale=0.5,
                                                     bias=half_bias[:, mc:mc + 1]).then_inc(pj_act, 1)
                    for s in two:
                        pj_taken(act, i, ("att", s, KC - 1, NPC - 1))
                        nc.scalar.activation(mixed_hi[s][:], mixed[s][:], ACT.Copy).then_inc(hi_ready, 1)

            @block.vector
            def _(dve):
                dve.sem_inc(pj_dve, len(PJ_DVE))
                dve.sem_inc(elu_ready, len(ELU))
                norm.on_vector(dve)
                dve.wait_ge(loaded, 160)
                dve.wait_ge(mask_ready, 3)
                for i in range(B // 2):
                    for s in two:
                        for kind, mc, n in KINDS:
                            if kind not in "kq":
                                continue
                            first, size = PIECES[n]
                            use = ("in", s, kind, mc, n)
                            v = ELU.index(use)
                            pj_taken(dve, i, use)
                            out = (key_t if kind == "k" else query_t)[s]
                            nc.vector.scalar_tensor_tensor(out[:, mc, first:first + size], ex[v % 4][:, 0:size], 1.0,
                                                           pos[v % 4][:, 0:size], ALU.min, ALU.add).then_inc(elu_ready, 1)
                    for s in two:
                        for c in range(NCH):
                            dve.wait_ge(ts_full, i * 2 * NCH + s * NCH + c + 1)
                            nc.vector.tensor_copy(rows[s][:, c], ts[(s * NCH + c) % NTS][0:CH, :]).then_inc(rows_ready, 1)
                    for s in two:
                        dve.wait_ge(kv_full, i * 2 + s + 1)
                        nc.vector.tensor_tensor(kv[s][:], kvb[s][:, 0:KC * P].rearrange("p (k n) -> p k n", k=KC),
                                                spread(block_mask[:], 1, KC), ALU.mult).then_inc(kv_ready, 1)
                    for s in two:
                        after(dve, lo_ready, i * 2)
                        pj_taken(dve, i, ("in", s, "g", KC - 1, NPC - 1))
                        for mc in range(KC):
                            for n, (first, size) in enumerate(PIECES):
                                use = ("att", s, mc, n)
                                u = PJ.index(use)
                                dve.wait_ge(pj_full, i * len(PJ) + u + 1)
                                at = slice(first, first + size)
                                nc.vector.scalar_tensor_tensor(mixed[s][:, mc, at], gate[s][:, mc, at], 1.0,
                                                               pj[u % NPJ][:, 0:size], ALU.add, ALU.mult).then_inc(pj_dve, 1)
                    for s in two:
                        dve.wait_ge(hi_ready, i * 2 + s + 1)
                        nc.vector.tensor_tensor(mixed_lo[s][:], mixed[s][:], mixed_hi[s][:].bitcast(F32),
                                                ALU.subtract).then_inc(lo_ready, 1)
                    for s in two:
                        for mc in range(KC):
                            for n, (first, size) in enumerate(PIECES):
                                use = ("out", s, mc, n)
                                u = PJ.index(use)
                                dve.wait_ge(pj_full, i * len(PJ) + u + 1)
                                at = m.h[:, mc, ds((i * 2 + s) * SP + first, size)]
                                nc.vector.scalar_tensor_tensor(at, pj[u % NPJ][:, 0:size], bias[:, MATS.index("o"), mc:mc + 1], at,
                                                               ALU.add, ALU.add).then_inc(pj_dve, 1)

            @block.tensor
            def _(pe):
                def take_pj(i, use):
                    u = PJ.index(use)
                    pj_taken(pe, i, PJ[(u - NPJ) % len(PJ)], before=u < NPJ)
                    return pj[u % NPJ]

                norm.on_tensor(pe)
                for i in range(B // 2):
                    for s in two:
                        for g in range((i * 2 + s) * SP // G, ((i * 2 + s + 1) * SP - 1) // G + 1):
                            norm.x_ready(pe, g)
                        for kind, mc, n in KINDS:
                            if s == 0 and mc == 0 and n == 0:
                                pe.wait_ge(split, MATS.index(kind) + 1)
                            first, size = PIECES[n]
                            bank = take_pj(i, ("in", s, kind, mc, n))
                            wn, at = MATS.index(kind), slice(mc * P, (mc + 1) * P)
                            for kc in range(KC):
                                x = [t[:, kc, ds((i * 2 + s) * SP + first, size)] for t in (m.x_hi, m.x_lo)]
                                last = product(nc, bank[:, 0:size], (w_hi[:, wn, kc, at], w_lo[:, wn, kc, at]), x, kc == 0, kc == KC - 1)
                            last.then_inc(pj_full, 1)
                    pe.wait_ge(norm.logv_ready, NG)
                    for s in two:
                        pe.wait_ge(elu_ready, (i + 1) * len(ELU) + ELU.index(("in", s, "k", KC - 1, NPC - 1)) + 1)
                        pj_taken(pe, i, ("in", s, "v", KC - 1, NPC - 1))
                        for c in range(NCH):
                            after(pe, rows_ready, i * 2 * NCH + s * NCH + c - 1 if s * NCH + c >= NTS else i * 2 * NCH)
                            for t, src in enumerate((key_t[s], value_t[s])):
                                for mc in range(KC):
                                    last = nc.tensor.transpose(ts[(s * NCH + c) % NTS][0:CH, t * D + mc * P:t * D + (mc + 1) * P],
                                                               src[:, mc, c * CH:(c + 1) * CH], m.ident[:])
                            last.then_inc(ts_full, 1)
                    for s in two:
                        pe.wait_ge(rows_ready, i * 2 * NCH + (s + 1) * NCH)
                        after(pe, kv_ready, i * 2)
                        for mc in range(KC):
                            for c in range(NCH):
                                n = min(CH, S - c * CH)
                                last = nc.tensor.matmul(kvb[s][:, mc * P:(mc + 1) * P], rows[s][0:n, c, mc * P:(mc + 1) * P],
                                                        rows[s][0:n, c, D + mc * P:D + (mc + 1) * P], start=c == 0, stop=c == NCH - 1)
                        last.then_inc(kv_full, 1)
                    for s in two:
                        pe.wait_ge(kv_ready, i * 2 + s + 1)
                        pe.wait_ge(elu_ready, (i + 1) * len(ELU) + ELU.index(("in", s, "q", KC - 1, NPC - 1)) + 1)
                        for mc in range(KC):
                            for n, (first, size) in enumerate(PIECES):
                                bank = take_pj(i, ("att", s, mc, n))
                                nc.tensor.matmul(bank[:, 0:size], kv[s][:, mc], query_t[s][:, mc, first:first + size],
                                                 start=True, stop=True).then_inc(pj_full, 1)
                    pe.wait_ge(split, 5)
                    for s in two:
                        pe.wait_ge(lo_ready, i * 2 + s + 1)
                        for mc in range(KC):
                            for n, (first, size) in enumerate(PIECES):
                                bank = take_pj(i, ("out", s, mc, n))
                                wn, at = MATS.index("o"), slice(mc * P, (mc + 1) * P)
                                for kc in range(KC):
                                    last = product(nc, bank[:, 0:size], (w_hi[:, wn, kc, at], w_lo[:, wn, kc, at]),
                                                   (mixed_hi[s][:, kc, first:first + size], mixed_lo[s][:, kc, first:first + size]),
                                                   kc == 0, kc == KC - 1)
                                last.then_inc(pj_full, 1)


def stage_flat_experts(nc, m, d):
    WN = KC * D
    NS = 2 * NG
    DEPTH = 2
    with ExitStack() as ctx:
        sb, ps, sem = open_stage(nc, ctx, "ffn1")
        two = range(2)
        raw = [sb(f"f_raw{s}", [P, KC, D]) for s in two]
        w_hi = [sb(f"f_hi{s}", [P, KC, D], F32R) for s in two]
        w_lo = [sb(f"f_lo{s}", [P, KC, D], F32R) for s in two]
        bias = sb("f_bias", [P, E, KC])
        cw_or_y = sb("cw_or_y", [P, 2, NT])
        cw = [cw_or_y[:, s] for s in two]
        part = [sb(f"f_part{i}", [P, KC, G]) for i in range(2)]
        ob = [ps(f"f_ob{i}", [P, BANK]) for i in range(DEPTH * KC)]
        gb = [ps(f"f_gb{i}", [P, BANK]) for i in range(4)]
        pair = sb("pair", [P, NT])
        norm = Norm(nc, m, sem, cw_or_y, pair, [t[:].rearrange("p k g -> p (k g)") for t in part], gb + ob[DEPTH * KC - 1:])
        gate = Gate(nc, m, sb, sem, d["L1_ffn_gate_w"], d["L1_ffn_gate_b"], False)
        out_rows = sb("out_rows", [CH, B * NCH, D])
        out_turned = sem("f_out_turned")
        out_kept = sem("f_out_kept")
        stored = sem("f_stored")
        PAIRS_OF_CHUNKS = B * NCH // 2
        FIRST = 2 * G
        first_loaded = sem("f_first_cw_loaded")
        raw_loaded = [sem(f"f_raw_loaded{s}") for s in two]
        cw_loaded = [sem(f"f_cw_loaded{s}") for s in two]
        bias_loaded = sem("f_bias_loaded")
        rounded = [sem(f"f_rounded{s}") for s in two]
        split = [sem(f"f_split{s}") for s in two]
        out_full = sem("f_out_full")
        weighted = sem("f_weighted")
        summed = sem("f_summed")

        def reached(i, per, k):
            return (i + 1) * NS * per + (k + 1) * per

        with nc.Block() as block:
            @block.sync
            def _(sp):
                sp.dma_start(bias[:], d["L1_ffn_expert_b"].rearrange("e (c p) -> p e c", p=P)).then_inc(bias_loaded, 16)

                def load_weights(i, s):
                    sp.dma_start(raw[s][:], d["L1_ffn_expert_w"][ds(i * 2 + s, 1)].rearrange("o (k p) n -> p (o k) n", p=P)).then_inc(raw_loaded[s], 16)

                def load_expert_weights(i, s):
                    sp.dma_start(cw[s], m.cw_dram[ds(i * 2 + s, 1)].rearrange("o n -> (o n)").partition_broadcast(P)).then_inc(cw_loaded[s], 16)

                gate.load(sp)
                for s in two:
                    load_weights(0, s)
                gate.store(sp)
                row = m.cw_dram[0]
                sp.dma_start(cw[0][:, 0:FIRST], row[0:FIRST].partition_broadcast(P)).then_inc(first_loaded, 16)
                sp.dma_start(cw[0][:, FIRST:NT], row[FIRST:NT].partition_broadcast(P)).then_inc(cw_loaded[0], 16)
                load_expert_weights(0, 1)
                with sp.Fori(1, E // 2) as i:
                    for s in two:
                        sp.wait_ge(split[s], i)
                        load_weights(i, s)
                        sp.wait_ge(weighted, reached(i, 2, s * NG + NG - 1 - NS))
                        load_expert_weights(i, s)
                for c in range(B * NCH):
                    b, at = c // NCH, c % NCH * CH
                    n = min(CH, S - at)
                    sp.wait_ge(out_kept, c // 2 + 1)
                    sp.dma_start(d["out"][b, at:at + n], out_rows[0:n, c]).then_inc(stored, 16)
                sp.wait_ge(stored, 16 * B * NCH)

            @block.scalar
            def _(act):
                def round_weights(i, s):
                    act.wait_ge(raw_loaded[s], i * 16 + 16)
                    act.wait_ge(out_full, reached(i, 1, s * NG + NG - 1 - NS))
                    nc.scalar.activation(w_hi[s][:], raw[s][:], ACT.Copy).then_inc(rounded[s], 1)

                norm.on_scalar(act, lambda: round_weights(0, 0))
                for g in range(NG):
                    gate.keep(act, g, gb[g % 4])
                round_weights(0, 1)
                gate.exponentials(act)
                gate.keep_rows(act, gb[3])
                with act.Fori(1, E // 2) as i:
                    for s in two:
                        round_weights(i, s)
                for n in range(PAIRS_OF_CHUNKS):
                    act.wait_ge(out_turned, n + 1)
                    nc.scalar.activation(out_rows[:, 2 * n:2 * n + 2].rearrange("p c d -> p (c d)"), gb[n % 4][0:CH, :], ACT.Copy).then_inc(out_kept, 1)

            @block.gpsimd
            def _(pool):
                pool.sem_inc(summed, NS)

                def low_part(i, s):
                    pool.wait_ge(rounded[s], i + 1)
                    nc.gpsimd.tensor_tensor(w_lo[s][:], raw[s][:], w_hi[s][:].bitcast(F32), ALU.subtract).then_inc(split[s], 1)

                def step(i, more):
                    for k in range(NS):
                        at = slice(k % NG * G, (k % NG + 1) * G)
                        pool.wait_ge(weighted, reached(i, 2, k))
                        pool.wait_ge(summed, reached(i, 1, k - NG))
                        nc.gpsimd.tensor_tensor(m.h[:, :, at], m.h[:, :, at], part[k % 2][:], ALU.add).then_inc(summed, 1)
                        if k == 0:
                            low_part(i, 1)
                        if k == NG and more:
                            low_part(i + 1, 0)

                norm.on_pool(pool, lambda: low_part(0, 0))
                gate.fill()
                with pool.Fori(0, E // 2 - 1) as i:
                    step(i, True)
                step(E // 2 - 1, False)

            @block.vector
            def _(dve):
                dve.sem_inc(weighted, NS * 2)
                norm.on_vector(dve, gate.prepare_weights)
                gate.choose(dve, gb[2])
                dve.wait_ge(bias_loaded, 16)

                def weigh(i, k):
                    s, g = divmod(k, NG)
                    if g == 0 and not (isinstance(i, int) and s == 0):
                        dve.wait_ge(cw_loaded[s], i * 16 + 16)
                    dve.wait_ge(out_full, reached(i, 1, k))
                    dve.wait_ge(summed, reached(i, 1, k - 2))
                    for kc in range(KC):
                        nc.vector.scalar_tensor_tensor(part[k % 2][:, kc], ob[k % DEPTH * KC + kc][:, 0:G],
                                                       bias[:, ds(i * 2 + s, 1), kc],
                                                       cw[s][:, g * G:(g + 1) * G], ALU.add, ALU.mult).then_inc(weighted, 1)

                for k in range(NS):
                    if k == 0:
                        dve.wait_ge(first_loaded, 16)
                    if k == FIRST // G:
                        dve.wait_ge(cw_loaded[0], 16)
                    weigh(0, k)
                with dve.Fori(1, E // 2) as i:
                    for k in range(NS):
                        weigh(i, k)

            @block.tensor
            def _(pe):
                pe.sem_inc(out_full, NS)

                def turn(i, k):
                    s, g = divmod(k, NG)
                    if g == 0:
                        pe.wait_ge(split[s], i + 1)
                    pe.wait_ge(weighted, reached(i, 2, k - DEPTH))
                    for kc in range(KC):
                        for c in range(KC):
                            x = [t[:, c, g * G:(g + 1) * G] for t in (m.x_hi, m.x_lo)]
                            at = slice(kc * P, (kc + 1) * P)
                            last = product(nc, ob[k % DEPTH * KC + kc][:, 0:G], (w_hi[s][:, c, at], w_lo[s][:, c, at]), x, c == 0, c == KC - 1)
                    last.then_inc(out_full, 1)

                norm.on_tensor(pe)
                for g in range(NG):
                    norm.x_ready(pe, g)
                    if g == NG - 1:
                        pe.wait_ge(gate.z_ready, 1)
                    else:
                        pe.wait_ge(norm.logv_ready, g + 1)
                    gate.logits(pe, g, gb[g % 4])
                gate.turn(pe, gb[2])
                pe.wait_ge(norm.logv_ready, NG)
                for k in range(2):
                    turn(0, k)
                gate.turn_back(pe, gb[3])
                for k in range(2, NS):
                    turn(0, k)
                with pe.Fori(1, E // 2 - 1) as i:
                    for k in range(NS):
                        turn(i, k)

                def turn_out(g):
                    pe.wait_ge(summed, reached(E // 2 - 1, 1, NG + g))
                    for n in range(2 * g, 2 * g + 2):
                        if n >= 4:
                            pe.wait_ge(out_kept, n - 3)
                        for c in range(2):
                            for kc in range(KC):
                                last = nc.tensor.transpose(gb[n % 4][0:CH, c * D + kc * P:c * D + (kc + 1) * P],
                                                           m.h[:, kc, (2 * n + c) * CH:(2 * n + c + 1) * CH], m.ident[:])
                        last.then_inc(out_turned, 1)

                for k in range(NS):
                    turn(E // 2 - 1, k)
                    if k >= NG + 3:
                        turn_out(k - NG - 3)
                for g in range(NS - NG - 3, NG):
                    turn_out(g)


class Held:

    def __init__(self, nc, ctx):
        def sb(name, shape, dt=F32):
            return ctx.enter_context(nc.sbuf_tensor(name, shape, dt))

        self.h = sb("h", [P, KC, NT])
        self.x_hi = sb("x_hi", [P, KC, NT], F32R)
        self.x_lo = sb("x_lo", [P, KC, NT], F32R)
        self.ident = sb("ident", [P, P])
        self.mean_w = sb("mean_w", [P, P])
        self.eps = sb("eps", [P, 1])
        self.one = sb("one", [P, 1])
        self.causal = sb("causal", [CH, CH])
        self.decay_sum = sb("decay_sum", [CH, HEADS, B * NCH])
        self.decay_rows_dram = nc.dram_tensor("decay_rows_dram", (HEADS, NT), F32, kind="Internal").ap()
        self.cw_dram = nc.dram_tensor("cw_dram", (E, NT), F32, kind="Internal").ap()


def build(nc, d):
    with ExitStack() as ctx:
        m = Held(nc, ctx)
        ctx.enter_context(nc.allow_non_contiguous_dma(reason="vectors of a few hundred elements"))
        stage_tokens(nc, m, d)
        stage_gla(nc, m, d)
        stage_hidden_experts(nc, m, d)
        stage_linear_attention(nc, m, d)
        stage_flat_experts(nc, m, d)


_ARGS = ['txt', 'L0_tok_cls_token', 'L0_tok_cls_pos_embedding', 'L0_tok_ln1_g', 'L0_tok_ln1_b', 'L0_tok_W',
         'L0_tok_bias', 'L0_tok_ln2_g', 'L0_tok_ln2_b', 'L0_attn_Wq', 'L0_attn_Wk', 'L0_attn_Wv', 'L0_attn_Wo',
         'L0_attn_Wg', 'L0_attn_bg', 'L0_attn_Wog', 'L0_ffn_gate_W', 'L0_ffn_W1', 'L0_ffn_b1', 'L0_ffn_W2', 'L0_ffn_b2',
         'L1_attn_Wq', 'L1_attn_bq', 'L1_attn_Wk', 'L1_attn_bk', 'L1_attn_Wv', 'L1_attn_bv', 'L1_attn_Wg', 'L1_attn_bg',
         'L1_attn_Wo', 'L1_attn_bo', 'L1_ffn_gate_w', 'L1_ffn_gate_b', 'L1_ffn_expert_w', 'L1_ffn_expert_b']


def position_table():
    omega = 1.0 / 10000.0 ** (np.arange(D // 4, dtype=np.float32) / np.float32(D // 4 - 1))
    omega = omega.astype(np.float32)
    y, x = np.meshgrid(np.arange(HP), np.arange(HP), indexing="ij")
    y = y.reshape(-1)[:, None].astype(np.float32) * omega[None]
    x = x.reshape(-1)[:, None].astype(np.float32) * omega[None]
    table = np.concatenate((np.sin(x), np.cos(x), np.sin(y), np.cos(y)), axis=1).astype(np.float32)
    return np.ascontiguousarray(table.T.reshape(KC, P, NPATCH).transpose(1, 0, 2))


def patch_rows(x):
    x = x.reshape(B, COLORS, HP, PATCH, HP, PATCH).transpose(0, 2, 4, 3, 5, 1)
    return np.ascontiguousarray(x.reshape(B * NPATCH, PATCH * PATCH * COLORS))


def make(nc, shapes):
    d = {name: nc.dram_tensor(f"in_{name}", shape, F32, kind="ExternalInput").ap() for name, shape in shapes.items()}
    d["out"] = nc.dram_tensor("out_0", (B, S, D), F32, kind="ExternalOutput").ap()
    build(nc, d)


def kernel(**inputs):
    import concourse.bacc as bacc
    from concourse.bass_utils import run_bass_kernel_spmd

    nc = bacc.Bacc("TRN2", target_bir_lowering=False, num_devices=1)
    arrays = {name: np.ascontiguousarray(inputs[name]) for name in _ARGS}
    arrays["pos"] = position_table()
    arrays["patches"] = patch_rows(np.asarray(inputs["x"]))
    make(nc, {n: a.shape for n, a in arrays.items()})
    r = run_bass_kernel_spmd(nc, [{f"in_{n}": a for n, a in arrays.items()}], core_ids=[0])
    return r.results[0]["out_0"]
```
